# Optimizing a Trainium2 kernel written in Bass

```python
import numpy as np
import jax
import jax.numpy as jnp

def _softmax(x, axis=-1):
    return jax.nn.softmax(x, axis=axis)

def _gelu(x):
    return jax.nn.gelu(x, approximate=True)

def _silu(x):
    return jax.nn.silu(x)

def _sigmoid(x):
    return jax.nn.sigmoid(x)

def _layernorm(x, axis=-1, eps=1e-05):
    m = jnp.mean(x, axis=axis, keepdims=True)
    v = jnp.var(x, axis=axis, keepdims=True)
    return (x - m) / jnp.sqrt(v + eps)

def _scatter_add(tgt, idx, src, axis=0):
    return tgt.at[idx].add(src)

def _segment_sum(src, seg, n):
    return jax.ops.segment_sum(src, seg, n)
kernel_name = 'mk_seq_preln_d1_jaxref_r4_a8d051'

def setup_inputs(seed: int=0):
    np.random.seed(seed)
    _w = jnp.asarray

    def _L0_attn_setup():
        import jax, jax.numpy as jnp
        import numpy as np
        B, S, D, DI = (2, 1024, 256, 1024)

        def _gelu(x):
            return jax.nn.gelu(x, approximate=False)

        def _ln(x, g, b, eps=1e-05):
            mu = jnp.mean(x, axis=-1, keepdims=True)
            var = jnp.mean((x - mu) ** 2, axis=-1, keepdims=True)
            return (x - mu) / jnp.sqrt(var + eps) * g + b

        def _mlp(x, w1, b1, w2, b2):
            return _gelu(x @ w1 + b1) @ w2 + b2
        key = jax.random.key(seed)
        ks = jax.random.split(key, 16)
        s = 0.02

        def W(k, shape):
            return jax.random.normal(k, shape, dtype=jnp.float32) * s
        return {'x': jax.random.normal(ks[0], (B, S, D), dtype=jnp.float32), 'ln_g': jnp.ones((D,), jnp.float32), 'ln_b': jnp.zeros((D,), jnp.float32), 'h1_w1': W(ks[1], (D, DI)), 'h1_b1': jnp.zeros((DI,), jnp.float32), 'h1_w2': W(ks[2], (DI, D)), 'h1_b2': jnp.zeros((D,), jnp.float32), 'h2_w1': W(ks[3], (D, DI)), 'h2_b1': jnp.zeros((DI,), jnp.float32), 'h2_w2': W(ks[4], (DI, D)), 'h2_b2': jnp.zeros((D,), jnp.float32), 'fm_w1': W(ks[5], (D, DI)), 'fm_b1': jnp.zeros((DI,), jnp.float32), 'fm_w2': W(ks[6], (DI, D)), 'fm_b2': jnp.zeros((D,), jnp.float32)}
    _L0_attn_in = _L0_attn_setup()

    def _L0_ffn_setup():
        import jax, jax.numpy as jnp
        import numpy as np
        E = 8
        K = 2
        key = jax.random.key(seed)
        ks = jax.random.split(key, 8)
        B, T, d = (4, 512, 256)
        h = 4 * d // E
        s = 0.02
        X = jax.random.normal(ks[0], (B, T, d), jnp.float32)
        routing_W = jax.random.normal(ks[1], (E, d), jnp.float32) * s
        expert_bias = jnp.zeros((E,), jnp.float32)
        sW1 = jax.random.normal(ks[2], (d, h), jnp.float32) * s
        sb1 = jnp.zeros((h,), jnp.float32)
        sW2 = jax.random.normal(ks[3], (h, d), jnp.float32) * s
        sb2 = jnp.zeros((d,), jnp.float32)
        rW1 = jax.random.normal(ks[4], (E, d, h), jnp.float32) * s
        rb1 = jnp.zeros((E, h), jnp.float32)
        rW2 = jax.random.normal(ks[5], (E, h, d), jnp.float32) * s
        rb2 = jnp.zeros((E, d), jnp.float32)
        return dict(X=X, routing_W=routing_W, expert_bias=expert_bias, sW1=sW1, sb1=sb1, sW2=sW2, sb2=sb2, rW1=rW1, rb1=rb1, rW2=rW2, rb2=rb2)
    _L0_ffn_in = _L0_ffn_setup()
    _d = {'L0_attn_x': _L0_attn_in['x'], 'L0_attn_ln_g': _L0_attn_in['ln_g'], 'L0_attn_ln_b': _L0_attn_in['ln_b'], 'L0_attn_h1_w1': _L0_attn_in['h1_w1'], 'L0_attn_h1_b1': _L0_attn_in['h1_b1'], 'L0_attn_h1_w2': _L0_attn_in['h1_w2'], 'L0_attn_h1_b2': _L0_attn_in['h1_b2'], 'L0_attn_h2_w1': _L0_attn_in['h2_w1'], 'L0_attn_h2_b1': _L0_attn_in['h2_b1'], 'L0_attn_h2_w2': _L0_attn_in['h2_w2'], 'L0_attn_h2_b2': _L0_attn_in['h2_b2'], 'L0_attn_fm_w1': _L0_attn_in['fm_w1'], 'L0_attn_fm_b1': _L0_attn_in['fm_b1'], 'L0_attn_fm_w2': _L0_attn_in['fm_w2'], 'L0_attn_fm_b2': _L0_attn_in['fm_b2'], 'L0_ffn_routing_W': _L0_ffn_in['routing_W'], 'L0_ffn_expert_bias': _L0_ffn_in['expert_bias'], 'L0_ffn_sW1': _L0_ffn_in['sW1'], 'L0_ffn_sb1': _L0_ffn_in['sb1'], 'L0_ffn_sW2': _L0_ffn_in['sW2'], 'L0_ffn_sb2': _L0_ffn_in['sb2'], 'L0_ffn_rW1': _L0_ffn_in['rW1'], 'L0_ffn_rb1': _L0_ffn_in['rb1'], 'L0_ffn_rW2': _L0_ffn_in['rW2'], 'L0_ffn_rb2': _L0_ffn_in['rb2']}
    _x0 = _d['L0_attn_x']
    _d['L0_attn_x'] = jax.random.normal(jax.random.fold_in(jax.random.key(seed), 1), (4, 2048, 256), dtype=_x0.dtype)
    del _x0
    return _d

def reference(L0_attn_x, L0_attn_ln_g, L0_attn_ln_b, L0_attn_h1_w1, L0_attn_h1_b1, L0_attn_h1_w2, L0_attn_h1_b2, L0_attn_h2_w1, L0_attn_h2_b1, L0_attn_h2_w2, L0_attn_h2_b2, L0_attn_fm_w1, L0_attn_fm_b1, L0_attn_fm_w2, L0_attn_fm_b2, L0_ffn_routing_W, L0_ffn_expert_bias, L0_ffn_sW1, L0_ffn_sb1, L0_ffn_sW2, L0_ffn_sb2, L0_ffn_rW1, L0_ffn_rb1, L0_ffn_rW2, L0_ffn_rb2):

    def _L0_attn_ref(x, ln_g, ln_b, h1_w1, h1_b1, h1_w2, h1_b2, h2_w1, h2_b1, h2_w2, h2_b2, fm_w1, fm_b1, fm_w2, fm_b2):
        import jax, jax.numpy as jnp
        import numpy as np
        B, S, D, DI = (2, 1024, 256, 1024)

        def _gelu(x):
            return jax.nn.gelu(x, approximate=False)

        def _ln(x, g, b, eps=1e-05):
            mu = jnp.mean(x, axis=-1, keepdims=True)
            var = jnp.mean((x - mu) ** 2, axis=-1, keepdims=True)
            return (x - mu) / jnp.sqrt(var + eps) * g + b

        def _mlp(x, w1, b1, w2, b2):
            return _gelu(x @ w1 + b1) @ w2 + b2
        n = _ln(x, ln_g, ln_b)
        W1 = _mlp(n, h1_w1, h1_b1, h1_w2, h1_b2)
        W2 = _mlp(n, h2_w1, h2_b1, h2_w2, h2_b2)
        W3 = jnp.einsum('bzn,bsn->bzs', W1, W2)
        W3 = jnp.tril(W3)
        t = jnp.einsum('bzs,bsm->bzm', W3, n)
        t = _ln(_gelu(t), ln_g, ln_b)
        x1 = x + t
        out = x + _mlp(_ln(x1, ln_g, ln_b), fm_w1, fm_b1, fm_w2, fm_b2)
        return out

    def _L0_ffn_ref(X, routing_W, expert_bias, sW1, sb1, sW2, sb2, rW1, rb1, rW2, rb2):
        import jax, jax.numpy as jnp
        import numpy as np
        E = 8
        K = 2
        B, T, d = X.shape
        shared = jax.nn.silu(X @ sW1 + sb1) @ sW2 + sb2
        logits = jnp.einsum('btd,ed->bte', X, routing_W) + expert_bias
        activation = jnp.sqrt(jax.nn.softplus(logits))
        top_vals, top_idx = jax.lax.top_k(activation, K)
        combine = jnp.sum(jax.nn.one_hot(top_idx, E, dtype=X.dtype) * top_vals[..., None], axis=-2)
        Xf = X.reshape(-1, d)
        cf = combine.reshape(-1, E)
        hdn = jax.nn.silu(jnp.einsum('nd,edh->enh', Xf, rW1) + rb1[:, None, :])
        y = jnp.einsum('enh,ehd->end', hdn, rW2) + rb2[:, None, :]
        routed = jnp.einsum('ne,end->nd', cf, y).reshape(B, T, d)
        return shared + routed
    x = L0_attn_x
    x = x + _L0_attn_ref(_layernorm(x, axis=-1), L0_attn_ln_g, L0_attn_ln_b, L0_attn_h1_w1, L0_attn_h1_b1, L0_attn_h1_w2, L0_attn_h1_b2, L0_attn_h2_w1, L0_attn_h2_b1, L0_attn_h2_w2, L0_attn_h2_b2, L0_attn_fm_w1, L0_attn_fm_b1, L0_attn_fm_w2, L0_attn_fm_b2)
    x = x + _L0_ffn_ref(_layernorm(x, axis=-1), L0_ffn_routing_W, L0_ffn_expert_bias, L0_ffn_sW1, L0_ffn_sb1, L0_ffn_sW2, L0_ffn_sb2, L0_ffn_rW1, L0_ffn_rb1, L0_ffn_rW2, L0_ffn_rb2)
    return x

_drawn_inputs = setup_inputs


def setup_inputs(seed=0):
    import zlib

    import numpy as np

    out = dict(_drawn_inputs(seed))
    spreads = {'L0_attn_ln_g': (1.0, 0.2),
     'L0_attn_ln_b': (0.0, 0.1),
     'L0_attn_h1_b1': (0.0, 0.503),
     'L0_attn_h1_b2': (0.0, 0.269),
     'L0_attn_h2_b1': (0.0, 0.459),
     'L0_attn_h2_b2': (0.0, 0.1),
     'L0_attn_fm_b1': (0.0, 0.392),
     'L0_attn_fm_b2': (0.0, 0.1),
     'L0_ffn_expert_bias': (0.0, 0.1),
     'L0_ffn_sb1': (0.0, 0.8),
     'L0_ffn_sb2': (0.0, 0.1),
     'L0_ffn_rb1': (0.0, 0.8),
     'L0_ffn_rb2': (0.0, 0.1)}
    factors = {'L0_ffn_sW1': 3.083, 'L0_ffn_sW2': 2.916}
    for name, (base, spread) in spreads.items():
        noise = np.random.default_rng([zlib.crc32(name.encode()), seed]).standard_normal(out[name].shape)
        drawn = base * np.exp(spread * noise) if base else spread * noise
        out[name] = jnp.asarray(drawn.astype(out[name].dtype))
    for name, factor in factors.items():
        out[name] = (out[name] * factor).astype(out[name].dtype)
    return out
```

```python
from contextlib import ExitStack

import concourse.bass as bass
from concourse import mybir

F32 = mybir.dt.float32
F32R = mybir.dt.float32r
U32 = mybir.dt.uint32
ALU = mybir.AluOpType
ACT = mybir.ActivationFunctionType

P = 128
TOKENS_PER_BLOCK = 512
TILES = TOKENS_PER_BLOCK // P
CHUNK_TILES = 2
CHUNKS = TILES // CHUNK_TILES
EPS = 1e-5


def bass_preln_layer(nc, x, ln_g, ln_b, h1_w1, h1_b1, h1_w2, h1_b2, h2_w1, h2_b1, h2_w2, h2_b2,
                     fm_w1, fm_b1, fm_w2, fm_b2, routing_W, expert_bias, sW1, sb1, sW2, sb2,
                     rW1, rb1, rW2, rb2, out):
    batches, seq, D = x.shape
    DI = h1_w1.shape[1]
    NBLK = batches * seq // TOKENS_PER_BLOCK
    BLOCKS_PER_BATCH = seq // TOKENS_PER_BLOCK
    KD = D // P
    NH = DI // P
    EXPERTS = routing_W.shape[0]
    UNITS = EXPERTS + 1
    assert D == 256 and NH == 8 and EXPERTS == 8 and rW1.shape[2] == P and BLOCKS_PER_BATCH == 4
    T4 = TOKENS_PER_BLOCK

    x_tok = x.rearrange("b s d -> (b s) d").rearrange("(n p) d -> p n d", p=P)
    out_tok = out.rearrange("b s d -> (b s) d").rearrange("(n p) d -> p n d", p=P)
    x2_dram = nc.dram_tensor("x2_between_phases", (P, NBLK * TILES, D), F32, kind="Internal").ap()

    KB = 1024
    base = ((nc.sbuf_base + 31) // 32) * 32

    class Region:
        def __init__(self, at):
            self.at = at

        def put(self, name, shape, dt=F32):
            t = nc.alloc_sbuf_tensor_at(name, shape, dt, offset=self.at)
            n = 4
            for s in shape[1:]:
                n *= s
            self.at += (n + 31) // 32 * 32
            assert self.at <= nc.sbuf_usable_end, (name, self.at)
            return t

    with ExitStack() as ctx:
        def sem(name):
            return ctx.enter_context(nc.semaphore(name))

        common = Region(base)
        ident = common.put("ident", [P, P])
        consts = common.put("consts", [P, 6, TILES])
        C_HALF, C_QUARTER, C_INVN, C_EPS, C_NEGHALF = (consts[:, j, :] for j in range(5))
        stats = common.put("stats", [P, TILES, 6])
        lnw = common.put("lnw", [P, 8, TILES])
        touch1 = common.put("touch1", [P, TILES])
        phase_base = common.at

        r1 = Region(phase_base)
        W = {}
        for mlp in ("h2", "h1", "fm"):
            for part in ("hi", "lo"):
                W[mlp, 1, part] = r1.put(f"{mlp}_w1_{part}", [P, KD, DI], F32R)
            for part in ("hi", "lo"):
                W[mlp, 2, part] = r1.put(f"{mlp}_w2_{part}", [P, NH, D], F32R)
        nT_at = r1.at
        nT = [r1.put(f"nT_{p_}", [P, KD, T4], F32R) for p_ in ("hi", "lo")]
        qreg = Region(nT_at)
        QT = [qreg.put(f"QT_{p_}", [P, KD, T4], F32R) for p_ in ("hi", "lo")]
        ntok = [r1.put(f"ntok_{p_}", [P, TILES, D], F32R) for p_ in ("hi", "lo")]
        KT = [r1.put(f"KT_{p_}", [P, KD, T4], F32R) for p_ in ("hi", "lo")]
        ktok_at = r1.at
        Ktok = [r1.put(f"Ktok_{p_}", [P, TILES, D], F32R) for p_ in ("hi", "lo")]
        n2T_at = r1.at
        n2T = [r1.put(f"n2T_{p_}", [P, KD, T4], F32R) for p_ in ("hi", "lo")]
        xin = r1.put("xin", [P, TILES, D])
        xa = r1.put("xa", [P, 2, TILES, D])
        resid = r1.put("resid", [P, 2, TILES, D])
        n32 = r1.put("n32", [P, TILES, D])
        work_at = r1.at
        work = r1.put("work", [P, TILES, D])
        KT32 = Region(work_at).put("KT32", [P, KD, T4])
        G = [r1.put(f"G_{p_}", [P, 3, T4], F32R) for p_ in ("hi", "lo")]
        G32 = r1.put("G32", [P, 2, T4])
        S32 = r1.put("S32", [P, 384])
        SP_ = [r1.put(f"S_{p_}", [P, CHUNKS, 384], F32R) for p_ in ("hi", "lo")]
        state = r1.put("state", [P, 2, KD * D])
        St = [[r1.put(f"state{c}_{p_}", [P, KD * D], F32R) for p_ in ("hi", "lo")] for c in range(CHUNKS)]
        tri = r1.put("tri", [P, P])
        gB = r1.put("gB", [P, D])
        bB = r1.put("bB", [P, D])
        fb2B = r1.put("fb2B", [P, D])
        bcol = r1.put("bcol", [P, 3, NH])
        b2col = r1.put("b2col", [P, 2, KD])
        stage_at = {}
        fm_at = phase_base + 2 * 4 * 8 * KB
        stage_at["h2", 1] = fm_at
        stage_at["h2", 2] = fm_at + 8 * KB
        stage_at["h1", 1] = fm_at + 16 * KB
        stage_at["h1", 2] = fm_at + 24 * KB
        stage_at["fm", 1] = n2T_at
        stage_at["fm", 2] = ktok_at
        stage = {}
        for (mlp, w), at in stage_at.items():
            shape = [P, KD, DI] if w == 1 else [P, NH, D]
            stage[mlp, w] = Region(at).put(f"{mlp}_w{w}_f32", shape)

        r2 = Region(phase_base)
        eW1 = [r2.put(f"eW1_{p_}", [P, KD, UNITS, P], F32R) for p_ in ("hi", "lo")]
        eW2 = [r2.put(f"eW2_{p_}", [P, UNITS, D], F32R) for p_ in ("hi", "lo")]
        e1_32 = r2.put("e1_32", [P, KD, UNITS, P])
        e2_32 = r2.put("e2_32", [P, UNITS, D])
        XT = [[r2.put(f"XT{q}_{p_}", [P, KD, T4], F32R) for p_ in ("hi", "lo")] for q in range(2)]
        x2 = [r2.put(f"x2_{q}", [P, TILES, D]) for q in range(2)]
        xn = r2.put("xn", [P, TILES, D])
        y = [r2.put(f"y_{q}", [P, TILES, D]) for q in range(2)]
        H = [r2.put(f"H_{p_}", [P, 3, T4], F32R) for p_ in ("hi", "lo")]
        s32 = r2.put("s32", [P, 2, T4])
        h32 = r2.put("h32", [P, 2, T4])
        rw32 = r2.put("rw32", [P, KD, EXPERTS])
        rw = r2.put("rw", [P, KD, 2 * EXPERTS], F32R)
        ebB = r2.put("ebB", [P, EXPERTS])
        eb1 = r2.put("eb1", [P, UNITS])
        sel32 = r2.put("sel32", [P, EXPERTS, P])
        sel = r2.put("sel", [P, EXPERTS, P], F32R)
        bias32 = r2.put("bias32", [P, D])
        biasR = [r2.put(f"biasR_{p_}", [P, D], F32R) for p_ in ("hi", "lo")]
        iota = r2.put("iota", [P, EXPERTS])
        rt = r2.put("rt", [P, 10, TILES, EXPERTS])
        top8 = r2.put("top8", [P, TILES, 8])
        topi = r2.put("topi", [P, TILES, 8], U32)
        topf = r2.put("topf", [P, TILES, 8])
        half8 = r2.put("half8", [P, TILES, EXPERTS])
        cfx = r2.put("cfx", [P, TILES, P])
        cfh = r2.put("cfh", [P, TILES, EXPERTS], F32R)
        cfT = [r2.put(f"cfT{q}", [P, T4], F32R) for q in range(2)]
        touch = r2.put("touch", [P, 8])

        bank = [ctx.enter_context(nc.psum_tensor(f"bank{j}", [P, 512], F32)) for j in range(8)]
        upB, A, B, M = bank[0:2], bank[2:4], bank[4:6], bank[6:8]

        def tok2(b):
            return b[:, :].rearrange("p (t d) -> p t d", t=2)

        names1 = """ld_x ld_const ld_h2w1 ld_h2w2 ld_h1w1 ld_h1w2 ld_fmw1 ld_fmw2 const_pool
            w_hi w_lo x_used a_stats a_rstd a_norm a_out nT_ps nT_hi nT_lo ntok_hi ntok_lo
            up_ready gelu_hi gelu_done split_ready down_done
            k_ready k_f32 k_hi k_lo ktok_ps ktok_hi ktok_lo q_ready q_hi q_lo
            delta_ready state_add state_hi state_lo qs_done s_ps s_masked s_hi s_lo s_start
            t_ready t_gelu e_stats e_rstd e_norm e_mid e_out n2T_ps n2T_hi n2T_lo
            f_ready resid_set x2_ready fb2_st_x2 pool_chain""".split()
        s = {n: sem(n) for n in names1}
        names2 = """m_ldw m_ldp m_pool m_whi m_wlo m_ldx_even m_ldx_odd m_stats m_rstd m_norm m_T_ps
            m_T_hi m_T_lo m_lg_ps m_r m_exp m_ln m_act m_cf m_cfx m_cfT_ps m_cfT m_cfb m_up m_silu
            m_mult m_hhi m_split m_down m_y m_yout m_out_even m_out_odd""".split()
        m = {n: sem(n) for n in names2}

        def mm(o, lhsT, rhs, start=False, stop=False):
            return nc.tensor.matmul(o, lhsT, rhs, start=start, stop=stop, skip_group_check=True)

        def mm3(o, w, v, ws, vs, start=False, stop=False):
            mm(o, w[1][ws], v[0][vs], start=start)
            mm(o, w[0][ws], v[1][vs])
            return mm(o, w[0][ws], v[0][vs], stop=stop)

        HU = 2 * NH
        FU = 3 * NH

        def unit_base(i):
            return 0 if isinstance(i, int) and i == 0 else i * FU - NH

        def off(i):
            return 0 if isinstance(i, int) and i == 0 else 1

        MLP = ("h2", "h1", "fm")
        W2 = {(mlp, w): (W[mlp, w, "hi"], W[mlp, w, "lo"]) for mlp in MLP for w in (1, 2)}

        def zero_or_state(i):
            if isinstance(i, int):
                return 0 if i % BLOCKS_PER_BATCH == 0 else 1
            return (((i % BLOCKS_PER_BATCH) + 3) >> 2).with_bounds(min_val=0, max_val=1)

        def one(i):
            return bass.ds(i, 1) if not isinstance(i, int) else slice(i, i + 1)

        def par(i):
            return one(i % 2)

        with nc.Block() as block:
            @block.sync
            def _(sp):
                sp.dma_start(xin[:, :, :], x_tok[:, 0:TILES, :]).then_inc(s["ld_x"], 16)
                sp.dma_start(fb2B[:, :], fm_b2.partition_broadcast(P)).then_inc(s["fb2_st_x2"], 16)
                w_dram = {("h2", 1): h2_w1, ("h2", 2): h2_w2, ("h1", 1): h1_w1, ("h1", 2): h1_w2,
                          ("fm", 1): fm_w1, ("fm", 2): fm_w2}
                for key in (("h2", 1), ("h2", 2), ("h1", 1), ("h1", 2), ("fm", 1), ("fm", 2)):
                    src = w_dram[key].rearrange("(k p) n -> p k n", p=P)
                    sp.dma_start(stage[key][:, :, :], src).then_inc(s[f"ld_{key[0]}w{key[1]}"], 16)

                def load_x(i):
                    sp.wait_ge(s["x_used"], i)
                    sp.wait_ge(s["x_used"], 1)
                    sp.dma_start(xin[:, :, :], x_tok[:, bass.ds(i * TILES, TILES), :]).then_inc(s["ld_x"], 16)

                def store_x2(i):
                    sp.wait_ge(s["x2_ready"], 2 * (i + 1) + 2)
                    sp.wait_ge(s["x2_ready"], 1)
                    sp.dma_start(x2_dram[:, bass.ds(i * TILES, TILES), :],
                                 resid[:, par(i), :, :].rearrange("p o t d -> p (o t) d")).then_inc(s["fb2_st_x2"], 16)

                load_x(1)
                with sp.Fori(1, NBLK - 1) as i:
                    load_x(i + 1)
                    store_x2(i - 1)
                store_x2(NBLK - 2)
                store_x2(NBLK - 1)
                sp.wait_ge(s["fb2_st_x2"], 16 * (NBLK + 1))

            @block.gpsimd
            def _(pool):
                g = nc.gpsimd

                g.memset(ident[:, :], 0.0).then_inc(s["pool_chain"], 1)
                g.memset(tri[:, :], 1.0).then_inc(s["pool_chain"], 1)
                g.memset(state[:, 0, :], 0.0).then_inc(s["const_pool"], 1)
                for col, val in ((C_HALF, 0.5), (C_QUARTER, 0.25), (C_INVN, 1.0 / D), (C_EPS, EPS), (C_NEGHALF, -0.5)):
                    g.memset(col, val).then_inc(s["pool_chain"], 1)
                pool.wait_ge(s["pool_chain"], 7)
                g.affine_select(out=ident[:, :], in_=ident[:, :], compare_op=ALU.not_equal, fill=1.0,
                                base=0, pattern=[[-1, P]], channel_multiplier=1).then_inc(s["const_pool"], 1)
                g.affine_select(out=tri[:, :], in_=tri[:, :], compare_op=ALU.is_ge, fill=0.0,
                                base=0, pattern=[[1, P]], channel_multiplier=-1).then_inc(s["const_pool"], 1)
                for dst, src in ((gB, ln_g), (bB, ln_b)):
                    pool.dma_start(dst[:, :], src.partition_broadcast(P)).then_inc(s["ld_const"], 16)
                for j, src in enumerate((h2_b1, h1_b1, fm_b1)):
                    pool.dma_start(bcol[:, j, :], src.rearrange("(k p) -> p k", p=P),
                                   allow_slow_non_contiguous=True).then_inc(s["ld_const"], 16)
                for j, src in enumerate((h2_b2, h1_b2)):
                    pool.dma_start(b2col[:, j, :], src.rearrange("(k p) -> p k", p=P),
                                   allow_slow_non_contiguous=True).then_inc(s["ld_const"], 16)

                def rstd(stat_sem, stat_count, done, done_before):
                    me, mo, v0, v1 = stats[:, :, 1], stats[:, :, 4], stats[:, :, 2], stats[:, :, 5]
                    w = [lnw[:, j, :] for j in range(8)]
                    pool.wait_ge(stat_sem, stat_count)
                    g.tensor_tensor(w[2], me, mo, ALU.add).then_inc(done, 1)
                    g.tensor_tensor(w[3], me, mo, ALU.subtract).then_inc(done, 1)
                    g.tensor_tensor(w[4], v0, v1, ALU.add).then_inc(done, 1)
                    k = 3
                    for o, a, b, op in ((w[0], w[2], C_HALF, ALU.mult), (w[5], w[3], w[3], ALU.mult),
                                        (w[6], w[5], C_QUARTER, ALU.mult), (w[7], w[4], C_INVN, ALU.mult),
                                        (w[5], w[6], w[7], ALU.add), (w[6], w[5], C_EPS, ALU.add),
                                        (w[1], w[6], C_NEGHALF, ALU.pow)):
                        pool.wait_ge(done, done_before + k)
                        g.tensor_tensor(o, a, b, op).then_inc(done, 1)
                        k += 1

                gB3 = gB[:, :].unsqueeze(1).to_broadcast([P, TILES, D])
                bB3 = bB[:, :].unsqueeze(1).to_broadcast([P, TILES, D])

                def norm_n(i):
                    rstd(s["a_stats"], 8 * i + 4, s["a_rstd"], 20 * i)
                    rstd(s["a_stats"], 8 * i + 8, s["a_rstd"], 20 * i + 10)
                    pool.wait_ge(s["a_norm"], 2 * TILES * (i + 1))
                    g.tensor_tensor(n32[:, :, :], n32[:, :, :], gB3, ALU.mult).then_inc(s["a_out"], 1)
                    pool.wait_ge(s["a_out"], 2 * i + 1)
                    g.tensor_tensor(n32[:, :, :], n32[:, :, :], bB3, ALU.add).then_inc(s["a_out"], 1)

                def norm_t(i):
                    rstd(s["e_stats"], 8 * i + 4, s["e_rstd"], 20 * i)
                    rstd(s["e_stats"], 8 * i + 8, s["e_rstd"], 20 * i + 10)
                    pool.wait_ge(s["e_norm"], 2 * TILES * (i + 1))
                    g.tensor_tensor(work[:, :, :], work[:, :, :], gB3, ALU.mult).then_inc(s["e_out"], 1)
                    pool.wait_ge(s["e_out"], 2 * i + 1)
                    g.tensor_tensor(work[:, :, :], work[:, :, :], bB3, ALU.add).then_inc(s["e_out"], 1)

                pool.wait_ge(s["ld_const"], 16 * 7)
                norm_n(0)
                norm_n(1)
                norm_t(0)
                with pool.Fori(1, NBLK - 1) as i:
                    norm_n(i + 1)
                    norm_t(i)
                norm_t(NBLK - 1)

            @block.scalar
            def _(act):
                a = nc.scalar

                def hi_weights(key):
                    act.wait_ge(s[f"ld_{key[0]}w{key[1]}"], 16)
                    if key == ("fm", 1):
                        act.wait_ge(s["w_lo"], 4)
                    a.copy(W[key[0], key[1], "hi"][:, :, :], stage[key][:, :, :]).then_inc(s["w_hi"], 1)

                def unit(i, u, j, ht, slot_off):
                    U = unit_base(i) + u
                    slot = (slot_off + u) % 3
                    known_first = isinstance(i, int) and i == 0
                    act.wait_ge(s["up_ready"], U + 1)
                    if not (known_first and u < 3):
                        act.wait_ge(s["down_done"], U - 2)
                    a.activation(G[0][:, slot, :], upB[u % 2][:, :], ACT.Gelu,
                                 bias=bcol[:, j, ht:ht + 1]).then_inc(s["gelu_hi"], 1)
                    if not (known_first and u < 2):
                        act.wait_ge(s["split_ready"], U - 1)
                    a.activation(G32[:, u % 2, :], upB[u % 2][:, :], ACT.Gelu,
                                 bias=bcol[:, j, ht:ht + 1]).then_inc(s["gelu_done"], 1)

                def hi_T(dst, ps, hi, before, free=None):
                    for k in range(KD):
                        act.wait_ge(s[ps], before + k + 1)
                        a.copy(dst[0][:, k, :], M[k][:, :]).then_inc(s[hi], 1)

                def nT_hi(i):
                    hi_T(nT, "nT_ps", "nT_hi", 2 * i)
                    a.copy(ntok[0][:, :, :], n32[:, :, :]).then_inc(s["ntok_hi"], 1)

                def state_hi(c, i):
                    if c == 0:
                        if not (isinstance(i, int) and i == 0):
                            act.wait_ge(s["state_add"], 2 * i)
                            act.wait_ge(s["qs_done"], 2 * i - 1)
                        src = state[:, one(zero_or_state(i)), :]
                    else:
                        act.wait_ge(s["state_add"], 2 * i + 1)
                        if not (isinstance(i, int) and i == 0):
                            act.wait_ge(s["qs_done"], 2 * i)
                        src = state[:, 1:2, :]
                    a.copy(St[c][0][:, :], src.rearrange("p o n -> p (o n)")).then_inc(s["state_hi"], 1)

                def front(i, last):
                    o = off(i)
                    for u in range(HU):
                        unit(i, u, u // NH, u % NH, o)
                        if u == 4 and not (isinstance(i, int) and i == 0):
                            hi_T(n2T, "n2T_ps", "n2T_hi", 2 * (i - 1))
                        if u == 9:
                            for f in range(KD):
                                if f == 0:
                                    act.wait_ge(s["k_ready"], i + 1)
                                else:
                                    act.wait_ge(s["down_done"], unit_base(i) + NH)
                                a.activation(KT32[:, f, :], A[f][:, :], ACT.Identity,
                                             bias=b2col[:, 0, f:f + 1]).then_inc(s["k_f32"], 1)
                                a.activation(KT[0][:, f, :], A[f][:, :], ACT.Identity,
                                             bias=b2col[:, 0, f:f + 1]).then_inc(s["k_hi"], 1)
                        if u == 12:
                            if isinstance(i, int) and i == 0:
                                act.wait_ge(s["w_lo"], 6)
                            for h in range(2):
                                act.wait_ge(s["ktok_ps"], 2 * i + h + 1)
                                a.copy(Ktok[0][:, 2 * h:2 * h + 2, :], tok2(M[h])).then_inc(s["ktok_hi"], 1)
                        if isinstance(i, int) and i == 0 and u in (8, 10):
                            hi_weights(("fm", 1 if u == 8 else 2))
                    state_hi(1, i)
                    for f in range(KD):
                        if f == 0:
                            act.wait_ge(s["q_ready"], i + 1)
                        else:
                            act.wait_ge(s["down_done"], unit_base(i) + HU)
                        a.activation(QT[0][:, f, :], B[f][:, :], ACT.Identity,
                                     bias=b2col[:, 1, f:f + 1]).then_inc(s["q_hi"], 1)
                    for c in range(CHUNKS):
                        act.wait_ge(s["s_masked"], 4 * i + 2 * c + 2)
                        a.copy(SP_[0][:, c, :], S32[:, :]).then_inc(s["s_hi"], 1)
                    if not last:
                        state_hi(0, i + 1)
                    for c in range(CHUNKS):
                        act.wait_ge(s["t_ready"], 2 * i + c + 1)
                        a.activation(work[:, 2 * c:2 * c + 2, :], tok2(A[c]), ACT.Gelu).then_inc(s["t_gelu"], 1)
                    if not last:
                        nT_hi(i + 1)

                def back(i, first_unit, o):
                    for v in range(NH):
                        unit(i, first_unit + v, 2, v, o)

                act.wait_ge(s["ld_const"], 16 * 7)
                act.wait_ge(s["const_pool"], 3)
                state_hi(0, 0)
                hi_weights(("h2", 1))
                nT_hi(0)
                hi_weights(("h2", 2))
                hi_weights(("h1", 1))
                hi_weights(("h1", 2))
                front(0, False)
                with act.Fori(1, NBLK - 1) as i:
                    front(i, False)
                    back(i, HU, 1)
                front(NBLK - 1, True)
                back(NBLK - 1, HU, 1)
                hi_T(n2T, "n2T_ps", "n2T_hi", 2 * (NBLK - 1))
                back(NBLK, 0, 1)

            @block.vector
            def _(dve):
                v = nc.vector

                def lo(dst, src, hi):
                    return v.tensor_tensor(dst, src, hi.bitcast(F32), ALU.subtract)

                def lo_weights(key, before):
                    dve.wait_ge(s["w_hi"], before + 1)
                    lo(W[key[0], key[1], "lo"][:, :, :], stage[key][:, :, :],
                       W[key[0], key[1], "hi"][:, :, :]).then_inc(s["w_lo"], 1)

                def lo_T(dst, ps, hi, lo_, before):
                    for k in range(KD):
                        dve.wait_ge(s[hi], before + k + 1)
                        lo(dst[1][:, k, :], M[k][:, :], dst[0][:, k, :]).then_inc(s[lo_], 1)

                def nT_lo(i):
                    lo_T(nT, "nT_ps", "nT_hi", "nT_lo", 2 * i)
                    dve.wait_ge(s["ntok_hi"], i + 1)
                    lo(ntok[1][:, :, :], n32[:, :, :], ntok[0][:, :, :]).then_inc(s["ntok_lo"], 1)

                def row_stats(buf, done):
                    for t in range(TILES):
                        v.bn_stats(stats[:, t, :], buf[:, t, :]).then_inc(done, 1)

                def normalise(dst, src, done):
                    for t in range(TILES):
                        v.tensor_scalar(dst[:, t, :], src[:, t, :], lnw[:, 0, t:t + 1], lnw[:, 1, t:t + 1],
                                        ALU.subtract, ALU.mult).then_inc(done, 1)

                def xa_of(i):
                    return xa[:, par(i), :, :].rearrange("p o t d -> p (o t) d")

                def resid_of(i):
                    return resid[:, par(i), :, :].rearrange("p o t d -> p (o t) d")

                def a_step(i, step):
                    if step == 0:
                        dve.wait_ge(s["ld_x"], 16 * (i + 1))
                        row_stats(xin, s["a_stats"])
                    elif step == 1:
                        dve.wait_ge(s["a_rstd"], 20 * i + 10)
                        normalise(xa_of(i), xin, s["a_norm"])
                    elif step == 2:
                        dve.wait_ge(s["a_norm"], 2 * TILES * i + TILES)
                        v.tensor_copy(touch1[:, :], lnw[:, 0, :])
                        row_stats(xa_of(i), s["a_stats"])
                    else:
                        dve.wait_ge(s["a_rstd"], 20 * i + 20)
                        normalise(n32, xa_of(i), s["a_norm"])

                def residual(i):
                    dve.wait_ge(s["fb2_st_x2"], 16 if isinstance(i, int) and i == 0 else 16 * i)
                    v.tensor_tensor(resid_of(i), xin[:, :, :], xa_of(i), ALU.add).then_inc(s["x_used"], 1)
                    dve.wait_ge(s["x_used"], i + 1)
                    v.tensor_tensor(resid_of(i), resid_of(i), fb2B[:, :].unsqueeze(1).to_broadcast([P, TILES, D]),
                                    ALU.add).then_inc(s["resid_set"], 1)

                def unit(i, u, slot_off):
                    U = unit_base(i) + u
                    slot = (slot_off + u) % 3
                    dve.wait_ge(s["gelu_done"], U + 1)
                    lo(G[1][:, slot, :], G32[:, u % 2, :], G[0][:, slot, :]).then_inc(s["split_ready"], 1)

                def e_step(i, step):
                    w3 = work[:, :, :]
                    if step == 0:
                        dve.wait_ge(s["t_gelu"], 2 * i + 2)
                        row_stats(work, s["e_stats"])
                    elif step == 1:
                        dve.wait_ge(s["e_rstd"], 20 * i + 10)
                        normalise(work, work, s["e_norm"])
                    elif step == 2:
                        dve.wait_ge(s["e_norm"], 2 * TILES * i + TILES)
                        v.tensor_tensor(w3, w3, gB[:, :].unsqueeze(1).to_broadcast([P, TILES, D]),
                                        ALU.mult).then_inc(s["e_mid"], 1)
                    elif step == 3:
                        dve.wait_ge(s["e_mid"], 3 * i + 1)
                        v.tensor_tensor(w3, w3, bB[:, :].unsqueeze(1).to_broadcast([P, TILES, D]),
                                        ALU.add).then_inc(s["e_mid"], 1)
                        dve.wait_ge(s["e_mid"], 3 * i + 2)
                        v.tensor_tensor(w3, w3, xa_of(i), ALU.add).then_inc(s["e_mid"], 1)
                    elif step == 4:
                        dve.wait_ge(s["e_mid"], 3 * i + 3)
                        row_stats(work, s["e_stats"])
                    else:
                        dve.wait_ge(s["e_rstd"], 20 * i + 20)
                        normalise(work, work, s["e_norm"])

                def state_lo(c, i):
                    dve.wait_ge(s["state_hi"], 2 * i + c + 1)
                    src = state[:, one(zero_or_state(i)), :] if c == 0 else state[:, 1:2, :]
                    lo(St[c][1][:, :], src.rearrange("p o n -> p (o n)"), St[c][0][:, :]).then_inc(s["state_lo"], 1)

                def add_delta(c, i):
                    dve.wait_ge(s["delta_ready"], 2 * i + c + 1)
                    src = state[:, one(zero_or_state(i)), :] if c == 0 else state[:, 1:2, :]
                    dve.wait_ge(s["state_lo"], 2 * i + c + 1)
                    v.tensor_tensor(state[:, 1, :], upB[c][:, :], src.rearrange("p o n -> p (o n)"),
                                    ALU.add).then_inc(s["state_add"], 1)

                def front(i, last):
                    first = isinstance(i, int) and i == 0
                    o = off(i)
                    for u in range(HU):
                        unit(i, u, o)
                        if u == 1:
                            residual(i)
                        if first and u in (8, 10):
                            lo_weights(("fm", 1 if u == 8 else 2), 4 if u == 8 else 5)
                        if u == 4 and not first:
                            lo_T(n2T, "n2T_ps", "n2T_hi", "n2T_lo", 2 * (i - 1))
                        if u == 9:
                            for f in range(KD):
                                dve.wait_ge(s["k_hi"], 2 * i + f + 1)
                                lo(KT[1][:, f, :], KT32[:, f, :], KT[0][:, f, :]).then_inc(s["k_lo"], 1)
                        if u == 12:
                            for h in range(2):
                                dve.wait_ge(s["ktok_hi"], 2 * i + h + 1)
                                lo(Ktok[1][:, 2 * h:2 * h + 2, :], tok2(M[h]),
                                   Ktok[0][:, 2 * h:2 * h + 2, :]).then_inc(s["ktok_lo"], 1)
                        if not last:
                            if u in (7, 10, 11, 14):
                                a_step(i + 1, (7, 10, 11, 14).index(u))
                    add_delta(0, i)
                    state_lo(1, i)
                    for f in range(KD):
                        dve.wait_ge(s["q_hi"], 2 * i + f + 1)
                        v.scalar_tensor_tensor(out=QT[1][:, f, :], in0=B[f][:, :], scalar=b2col[:, 1, f:f + 1],
                                               in1=QT[0][:, f, :].bitcast(F32), op0=ALU.add,
                                               op1=ALU.subtract).then_inc(s["q_lo"], 1)
                    add_delta(1, i)
                    for c in range(CHUNKS):
                        dve.wait_ge(s["s_ps"], 2 * i + c + 1)
                        if not (first and c == 0):
                            dve.wait_ge(s["s_lo"], 2 * i + c)
                        diag = S32[:, :].rearrange("p (a b) -> p a b", b=P)
                        src = M[c][:, 0:384].rearrange("p (a b) -> p a b", b=P)
                        v.tensor_tensor(diag[:, 0:3:2, :], src[:, 0:3:2, :],
                                        tri[:, :].unsqueeze(1).to_broadcast([P, 2, P]),
                                        ALU.mult).then_inc(s["s_masked"], 1)
                        v.tensor_copy(diag[:, 1, :], src[:, 1, :]).then_inc(s["s_masked"], 1)
                        dve.wait_ge(s["s_hi"], 2 * i + c + 1)
                        lo(SP_[1][:, c, :], S32[:, :], SP_[0][:, c, :]).then_inc(s["s_lo"], 1)
                    if not last:
                        state_lo(0, i + 1)
                        nT_lo(i + 1)

                def x2_out(i, units):
                    r = resid_of(i)
                    dve.wait_ge(s["resid_set"], i + 1)
                    for h in range(2):
                        if h == 0:
                            dve.wait_ge(s["f_ready"], i + 1)
                        else:
                            dve.wait_ge(s["down_done"], units)
                        v.tensor_tensor(r[:, 2 * h:2 * h + 2, :], tok2(B[h]), r[:, 2 * h:2 * h + 2, :],
                                        ALU.add).then_inc(s["x2_ready"], 1)

                def back(i, first_unit, o, e_block):
                    for k in range(NH):
                        unit(i, first_unit + k, o)
                        if e_block is not None and k < 6:
                            e_step(e_block, k)

                v.memset(touch1[:, :], 0.0).then_inc(s["x2_ready"], 2)
                for step in range(4):
                    a_step(0, step)
                dve.wait_ge(s["const_pool"], 3)
                state_lo(0, 0)
                lo_weights(("h2", 1), 0)
                nT_lo(0)
                lo_weights(("h2", 2), 1)
                lo_weights(("h1", 1), 2)
                lo_weights(("h1", 2), 3)
                front(0, False)
                for step in range(6):
                    e_step(0, step)
                with dve.Fori(1, NBLK - 1) as i:
                    front(i, False)
                    back(i, HU, 1, i)
                    x2_out(i - 1, unit_base(i + 1))
                last = NBLK - 1
                front(last, True)
                back(last, HU, 1, last)
                x2_out(last - 1, unit_base(NBLK))
                lo_T(n2T, "n2T_ps", "n2T_hi", "n2T_lo", 2 * last)
                back(NBLK, 0, 1, None)
                x2_out(last, unit_base(NBLK) + NH)

            @block.tensor
            def _(pe):
                t_ = nc.tensor

                def up(i, u, j, ht, src):
                    U = unit_base(i) + u
                    first = isinstance(i, int) and i == 0
                    if not (first and u < 2):
                        pe.wait_ge(s["gelu_done"], U - 1)
                    b = upB[u % 2]
                    w = W2[MLP[j], 1]
                    for k in range(KD):
                        last = mm3(b[:, :], w, src, (slice(None), k, slice(ht * P, ht * P + P)),
                                   (slice(None), k, slice(None)), start=(k == 0), stop=(k == KD - 1))
                    last.then_inc(s["up_ready"], 1)

                def down_rows(i, u, ht, slot_off):
                    pe.wait_ge(s["split_ready"], unit_base(i) + u + 1)
                    slot = (slot_off + u) % 3
                    for t in range(TILES):
                        last = mm3(tok2(B[t // 2])[:, t % 2, :], G, W2["fm", 2],
                                   (slice(None), slot, slice(t * P, t * P + P)), (slice(None), ht, slice(None)),
                                   start=(ht == 0 and t % 2 == 0), stop=(ht == NH - 1))
                        if ht == NH - 1 and t % 2 == 1 and t < TILES - 1:
                            last.then_inc(s["f_ready"], 1)
                    return last

                def transposes(src_tile, ps):
                    for k in range(KD):
                        for t in range(TILES):
                            last = t_.transpose(M[k][:, t * P:(t + 1) * P], src_tile[:, t, k * P:(k + 1) * P],
                                                ident[:, :])
                        last.then_inc(s[ps], 1)

                def T_nT(i):
                    pe.wait_ge(s["a_out"], 2 * i + 2)
                    if not (isinstance(i, int) and i == 0):
                        pe.wait_ge(s["s_masked"], 4 * i)
                    transposes(n32, "nT_ps")

                def T_n2T(i):
                    pe.wait_ge(s["e_out"], 2 * i + 2)
                    if isinstance(i, int) and i == NBLK - 1:
                        pe.wait_ge(s["s_masked"], 4 * NBLK)
                    else:
                        pe.wait_ge(s["nT_lo"], 2 * (i + 2))
                    transposes(work, "n2T_ps")

                def down_h(i, u, o):
                    j = u // NH
                    ht = u % NH
                    acc, ready = ((A, "k_ready"), (B, "q_ready"))[j]
                    if ht == 0 and not (isinstance(i, int) and i == 0):
                        if j == 0:
                            pe.wait_ge(s["t_gelu"], 2 * i)
                        else:
                            pe.wait_ge(s["x2_ready"], 2 * i)
                    pe.wait_ge(s["split_ready"], unit_base(i) + u + 1)
                    slot = (o + u) % 3
                    w = W2[MLP[j], 2]
                    for f in range(KD):
                        ws = (slice(None), ht, slice(f * P, f * P + P))
                        vs = (slice(None), slot, slice(None))
                        last = mm3(acc[f][:, :], w, G, ws, vs, start=(ht == 0), stop=(ht == NH - 1))
                        if ht == NH - 1 and f == 0:
                            last.then_inc(s[ready], 1)
                    last.then_inc(s["down_done"], 1)

                def front(i, last):
                    first = isinstance(i, int) and i == 0
                    o = off(i)
                    pe.wait_ge(s["nT_lo"], 2 * (i + 1))
                    if not first:
                        pe.wait_ge(s["state_add"], 2 * i)
                    for u in range(HU):
                        if first and u in (0, 2, 8, 10):
                            pe.wait_ge(s["w_lo"], {0: 1, 2: 2, 8: 3, 10: 4}[u])
                        up(i, u, u // NH, u % NH, nT)
                        if u >= 2:
                            down_h(i, u - 2, o)
                        if u == 4 and not first:
                            T_n2T(i - 1)
                        if u == 12:
                            pe.wait_ge(s["k_f32"], 2 * i + 2)
                            if first:
                                pe.wait_ge(s["nT_lo"], 2)
                            else:
                                pe.wait_ge(s["n2T_lo"], 2 * i)
                            for h in range(2):
                                for t in (2 * h, 2 * h + 1):
                                    for k in range(KD):
                                        lt = t_.transpose(tok2(M[h])[:, t % 2, k * P:(k + 1) * P],
                                                          KT32[:, k, t * P:(t + 1) * P], ident[:, :])
                                lt.then_inc(s["ktok_ps"], 1)
                    down_h(i, HU - 2, o)

                    def delta(c):
                        pe.wait_ge(s["gelu_done"], unit_base(i) + HU - 1 + c)
                        if c == 0:
                            pe.wait_ge(s["ktok_lo"], 2 * i + 2)
                            pe.wait_ge(s["ntok_lo"], i + 1)
                        for fh in range(KD):
                            for t in (2 * c, 2 * c + 1):
                                lt = mm3(upB[c][:, fh * D:(fh + 1) * D], Ktok, ntok,
                                         (slice(None), t, slice(fh * P, (fh + 1) * P)), (slice(None), t, slice(None)),
                                         start=(fh == 0 and t == 2 * c), stop=(t == 2 * c + 1))
                        lt.then_inc(s["delta_ready"], 1)

                    delta(0)
                    down_h(i, HU - 1, o)
                    delta(1)
                    pe.wait_ge(s["q_lo"], 2 * i + 2)
                    pe.wait_ge(s["k_lo"], 2 * i + 2)
                    for c in range(CHUNKS):
                        t0 = 2 * c
                        for n, (st_, z0, zn, c0) in enumerate(((t0, t0, 2, 0), (t0 + 1, t0 + 1, 1, 2 * P))):
                            for k in range(KD):
                                lt = mm3(M[c][:, c0:c0 + zn * P], KT, QT,
                                         (slice(None), k, slice(st_ * P, st_ * P + P)),
                                         (slice(None), k, slice(z0 * P, (z0 + zn) * P)),
                                         start=(n == 0 and k == 0), stop=(k == KD - 1))
                        lt.then_inc(s["s_ps"], 1)
                    for c in range(CHUNKS):
                        pe.wait_ge(s["state_lo"], 2 * i + c + 1)
                        for zz in range(2):
                            for k in range(KD):
                                lt = mm3(tok2(A[c])[:, zz, :], QT, St[c],
                                         (slice(None), k, slice((2 * c + zz) * P, (2 * c + zz + 1) * P)),
                                         (slice(None), slice(k * D, (k + 1) * D)), start=(zz == 0 and k == 0))
                        lt.then_inc(s["qs_done"], 1)
                        pe.wait_ge(s["s_lo"], 2 * i + c + 1)
                        for zz, col, key in ((0, 0, 0), (1, P, 0), (1, 2 * P, 1)):
                            lt = mm3(tok2(A[c])[:, zz, :], SP_, ntok, (slice(None), c, slice(col, col + P)),
                                     (slice(None), 2 * c + key, slice(None)), stop=(zz == key))
                        lt.then_inc(s["t_ready"], 1)
                    if not last:
                        T_nT(i + 1)

                def back(i, blk, first_unit, o):
                    if isinstance(i, int) and i == NBLK:
                        pe.wait_ge(s["x2_ready"], 2 * blk + 2)
                    else:
                        pe.wait_ge(s["state_add"], 2 * i + 2)
                        pe.wait_ge(s["q_lo"], 2 * i + 2)
                    pe.wait_ge(s["n2T_lo"], 2 * (blk + 1))
                    for k in range(NH + 2):
                        if k < NH:
                            up(i, first_unit + k, 2, k, n2T)
                        if k >= 2:
                            down_rows(i, first_unit + k - 2, k - 2, o).then_inc(s["down_done"], 1)

                pe.wait_ge(s["const_pool"], 3)
                T_nT(0)
                front(0, False)
                pe.wait_ge(s["w_lo"], 6)
                with pe.Fori(1, NBLK - 1) as i:
                    front(i, False)
                    back(i, i - 1, HU, 1)
                front(NBLK - 1, True)
                back(NBLK - 1, NBLK - 2, HU, 1)
                T_n2T(NBLK - 1)
                back(NBLK, NBLK - 1, 0, 1)

        CB, Y = bank[2:4], bank[4:6]
        ROUTE = 17

        def at_parity(q, even, odd):
            return m[odd] if q else m[even]

        with nc.Block() as block2:
            def pairs(eng, body):
                body(0, 0, True)
                with eng.Fori(0, NBLK // 2 - 1) as j:
                    body(2 * j + 1, 1, True)
                    body(2 * j + 2, 0, True)
                body(NBLK - 1, 1, False)

            def half_count(b, q):
                return (b - q) // 2 + 1 if isinstance(b, int) else ((b - q) >> 1) + 1

            @block2.sync
            def _(sp):
                def load(b, q):
                    if not isinstance(b, int) or b >= 2:
                        sp.wait_ge(m["m_yout"], 2 * (b - 1))
                        sp.wait_ge(m["m_pool"], 1)
                    sp.dma_start(x2[q][:, :, :], x2_dram[:, bass.ds(b * TILES, TILES), :])\
                      .then_inc(at_parity(q, "m_ldx_even", "m_ldx_odd"), 16)

                load(0, 0)
                for k in range(KD):
                    sp.dma_start(rw32[:, k, :], routing_W[:, k * P:(k + 1) * P].rearrange("e p -> p e"),
                                   allow_slow_non_contiguous=True)\
                      .then_inc(m["m_ldw"], 16)
                    sp.dma_start(e1_32[:, k, 0:EXPERTS, :], rW1[:, k * P:(k + 1) * P, :].rearrange("e p h -> p e h"))\
                      .then_inc(m["m_ldw"], 16)
                    sp.dma_start(e1_32[:, k, EXPERTS, :], sW1[k * P:(k + 1) * P, :]).then_inc(m["m_ldw"], 16)
                sp.dma_start(e2_32[:, 0:EXPERTS, :], rW2.rearrange("e h d -> h e d")).then_inc(m["m_ldw"], 16)
                sp.dma_start(e2_32[:, EXPERTS, :], sW2).then_inc(m["m_out_odd"], 16)
                def turn(b, q, has_next):
                    if has_next:
                        load(b + 1, 1 - q)
                    sp.wait_ge(m["m_yout"], 2 * (b + 1))
                    sp.wait_ge(m["m_pool"], 1)
                    sp.dma_start(out_tok[:, bass.ds(b * TILES, TILES), :], y[q][:, :, :])\
                      .then_inc(at_parity(q, "m_out_even", "m_out_odd"), 16)

                pairs(sp, turn)
                sp.wait_ge(m["m_out_even"], 16 * (NBLK // 2))
                sp.wait_ge(m["m_out_odd"], 16 * (NBLK // 2 + 1))

            @block2.gpsimd
            def _(pool):
                g = nc.gpsimd
                g.memset(bias32[:, :], 0.0).then_inc(m["m_pool"], 1)
                g.memset(sel32[:, :, :], 0.0).then_inc(m["m_pool"], 1)
                g.memset(cfx[:, :, :], 0.0).then_inc(m["m_pool"], 1)
                g.memset(half8[:, :, :], 0.5).then_inc(m["m_pool"], 1)
                for e in range(EXPERTS):
                    g.memset(iota[:, e:e + 1], float(e)).then_inc(m["m_pool"], 1)
                n = 4 + EXPERTS
                pool.wait_ge(m["m_pool"], n)
                pool.dma_start(bias32[0:EXPERTS, :], rb2).then_inc(m["m_ldp"], 16)
                pool.dma_start(bias32[EXPERTS:2 * EXPERTS, :], rb2).then_inc(m["m_ldp"], 16)
                pool.dma_start(bias32[2 * EXPERTS:2 * EXPERTS + 1, :], sb2.rearrange("(a d) -> a d", a=1)).then_inc(m["m_ldp"], 16)
                pool.dma_start(ebB[:, :], expert_bias.partition_broadcast(P)).then_inc(m["m_ldp"], 16)
                pool.dma_start(eb1[:, 0:EXPERTS], rb1.rearrange("e h -> h e"),
                                   allow_slow_non_contiguous=True).then_inc(m["m_ldp"], 16)
                pool.dma_start(eb1[:, EXPERTS:UNITS], sb1.rearrange("(h a) -> h a", a=1),
                                   allow_slow_non_contiguous=True).then_inc(m["m_ldp"], 16)
                g.memset(cfx[:, :, 2 * EXPERTS:2 * EXPERTS + 1], 1.0).then_inc(m["m_pool"], 1)
                for half in range(2):
                    g.affine_select(out=sel32[:, :, :], in_=sel32[:, :, :], compare_op=ALU.not_equal, fill=1.0,
                                    base=-EXPERTS * half, pattern=[[-1, EXPERTS], [0, P]],
                                    channel_multiplier=1).then_inc(m["m_pool"], 1)
                    pool.wait_ge(m["m_pool"], n + 2 + half)

                def rstd(b):
                    me, mo, v0, v1 = stats[:, :, 1], stats[:, :, 4], stats[:, :, 2], stats[:, :, 5]
                    w = [lnw[:, j, :] for j in range(8)]
                    pool.wait_ge(m["m_stats"], TILES * (b + 1))
                    g.tensor_tensor(w[2], me, mo, ALU.add).then_inc(m["m_rstd"], 1)
                    g.tensor_tensor(w[3], me, mo, ALU.subtract).then_inc(m["m_rstd"], 1)
                    g.tensor_tensor(w[4], v0, v1, ALU.add).then_inc(m["m_rstd"], 1)
                    k = 3
                    for o, a, b_, op in ((w[0], w[2], C_HALF, ALU.mult), (w[5], w[3], w[3], ALU.mult),
                                         (w[6], w[5], C_QUARTER, ALU.mult), (w[7], w[4], C_INVN, ALU.mult),
                                         (w[5], w[6], w[7], ALU.add), (w[6], w[5], C_EPS, ALU.add),
                                         (w[1], w[6], C_NEGHALF, ALU.pow)):
                        pool.wait_ge(m["m_rstd"], 10 * b + k)
                        g.tensor_tensor(o, a, b_, op).then_inc(m["m_rstd"], 1)
                        k += 1

                def act_pow(b):
                    pool.wait_ge(m["m_r"], ROUTE * b + 13)
                    g.tensor_tensor(rt[:, 8, :, :], rt[:, 6, :, :], half8[:, :, :], ALU.pow).then_inc(m["m_act"], 1)

                rstd(0)
                act_pow(0)

                def turn(b, q, has_next):
                    if has_next:
                        rstd(b + 1)
                        act_pow(b + 1)

                pairs(pool, turn)

            @block2.scalar
            def _(act):
                a = nc.scalar

                def XT_hi(b, q):
                    for k in range(KD):
                        act.wait_ge(m["m_T_ps"], 2 * b + k + 1)
                        a.copy(XT[q][0][:, k, :], M[k][:, :]).then_inc(m["m_T_hi"], 1)

                def softplus_tables(b):
                    act.wait_ge(m["m_r"], ROUTE * b + 4)
                    a.activation(rt[:, 3, :, :], rt[:, 2, :, :], ACT.Exp, scale=-1.0).then_inc(m["m_exp"], 1)
                    act.wait_ge(m["m_r"], ROUTE * b + 5)
                    a.activation(rt[:, 5, :, :], rt[:, 4, :, :], ACT.Ln).then_inc(m["m_ln"], 1)

                def cfT_out(b, q):
                    act.wait_ge(m["m_cfT_ps"], b + 1)
                    a.copy(cfT[q][:, :], M[1][:, :]).then_inc(m["m_cfT"], 1)

                act.wait_ge(m["m_ldp"], 16 * 6)
                act.wait_ge(m["m_pool"], 15)
                act.wait_ge(m["m_ldw"], 16 * 7)
                act.wait_ge(m["m_out_odd"], 16)
                a.copy(eW1[0][:, :, :, :], e1_32[:, :, :, :]).then_inc(m["m_whi"], 1)
                a.copy(eW2[0][:, :, :], e2_32[:, :, :]).then_inc(m["m_whi"], 1)
                a.copy(sel[:, :, :], sel32[:, :, :]).then_inc(m["m_whi"], 1)
                a.copy(rw[:, :, 0:EXPERTS], rw32[:, :, :]).then_inc(m["m_whi"], 1)
                a.copy(biasR[0][:, :], bias32[:, :]).then_inc(m["m_whi"], 1)
                XT_hi(0, 0)
                softplus_tables(0)
                cfT_out(0, 0)

                def turn(b, q, has_next):
                    first = isinstance(b, int) and b == 0
                    for u in range(UNITS):
                        U = UNITS * b + u
                        slot, two = u % 3, (q + u) % 2
                        act.wait_ge(m["m_up"], U + 1)
                        if not (first and u < 2):
                            act.wait_ge(m["m_split"], U - 1)
                        a.activation(s32[:, two, :], upB[two][:, :], ACT.Silu,
                                     bias=eb1[:, u:u + 1]).then_inc(m["m_silu"], 1)
                        if not (first and u < 3):
                            act.wait_ge(m["m_down"], U - 2)
                        if u < EXPERTS:
                            act.wait_ge(m["m_mult"], EXPERTS * b + u + 1)
                            a.copy(H[0][:, slot, :], h32[:, two, :]).then_inc(m["m_hhi"], 1)
                        else:
                            a.activation(H[0][:, slot, :], upB[two][:, :], ACT.Silu,
                                         bias=eb1[:, u:u + 1]).then_inc(m["m_hhi"], 1)
                        if has_next:
                            if u == 3:
                                XT_hi(b + 1, 1 - q)
                            if u == 5:
                                softplus_tables(b + 1)
                    if has_next:
                        cfT_out(b + 1, 1 - q)

                pairs(act, turn)

            @block2.vector
            def _(dve):
                v = nc.vector

                def lo(dst, src, hi):
                    return v.tensor_tensor(dst, src, hi.bitcast(F32), ALU.subtract)

                def row_stats(b, q):
                    dve.wait_ge(at_parity(q, "m_ldx_even", "m_ldx_odd"), 16 * half_count(b, q))
                    for t in range(TILES):
                        v.bn_stats(stats[:, t, :], x2[q][:, t, :]).then_inc(m["m_stats"], 1)

                def normalise(b, q):
                    dve.wait_ge(m["m_rstd"], 10 * (b + 1))
                    if not (isinstance(b, int) and b == 0):
                        dve.wait_ge(m["m_T_ps"], 2 * b)
                    for t in range(TILES):
                        v.tensor_scalar(xn[:, t, :], x2[q][:, t, :], lnw[:, 0, t:t + 1], lnw[:, 1, t:t + 1],
                                        ALU.subtract, ALU.mult).then_inc(m["m_norm"], 1)

                def XT_lo(b, q):
                    for k in range(KD):
                        dve.wait_ge(m["m_T_hi"], 2 * b + k + 1)
                        lo(XT[q][1][:, k, :], M[k][:, :], XT[q][0][:, k, :]).then_inc(m["m_T_lo"], 1)

                def step(b, k):
                    dve.wait_ge(m["m_r"], ROUTE * b + k)

                R = [rt[:, j, :, :] for j in range(10)]

                def softplus(b):
                    lg = M[0][:, 0:TILES * 2 * EXPERTS].rearrange("p (t e) -> p t e", t=TILES)
                    r = m["m_r"]
                    dve.wait_ge(m["m_lg_ps"], b + 1)
                    v.tensor_tensor(R[0], lg[:, :, EXPERTS:2 * EXPERTS],
                                    ebB[:, :].unsqueeze(1).to_broadcast([P, TILES, EXPERTS]), ALU.add).then_inc(r, 1)
                    step(b, 1)
                    v.tensor_tensor(R[1], lg[:, :, 0:EXPERTS], R[0], ALU.add).then_inc(r, 1)
                    step(b, 2)
                    v.tensor_scalar(R[0], R[1], -1.0, None, ALU.mult).then_inc(r, 1)
                    step(b, 3)
                    v.tensor_tensor(R[2], R[1], R[0], ALU.max).then_inc(r, 1)
                    dve.wait_ge(m["m_exp"], b + 1)
                    v.tensor_scalar(R[4], R[3], 1.0, None, ALU.add).then_inc(r, 1)
                    step(b, 5)
                    v.tensor_scalar(R[0], R[4], -1.0, None, ALU.add).then_inc(r, 1)
                    step(b, 6)
                    v.tensor_scalar(R[7], R[0], 1e-30, None, ALU.max).then_inc(r, 1)
                    step(b, 7)
                    v.reciprocal(R[9], R[7]).then_inc(r, 1)
                    v.scalar_tensor_tensor(out=R[0], in0=R[0], scalar=0.0, in1=R[3], op0=ALU.is_equal,
                                           op1=ALU.mult).then_inc(r, 1)
                    step(b, 9)
                    v.tensor_tensor(R[9], R[9], R[3], ALU.mult).then_inc(r, 1)
                    v.scalar_tensor_tensor(out=R[0], in0=R[1], scalar=0.0, in1=R[0], op0=ALU.max,
                                           op1=ALU.add).then_inc(r, 1)
                    step(b, 11)
                    dve.wait_ge(m["m_ln"], b + 1)
                    v.tensor_tensor(R[6], R[5], R[9], ALU.mult).then_inc(r, 1)
                    step(b, 12)
                    v.tensor_tensor(R[6], R[6], R[0], ALU.add).then_inc(r, 1)

                def combine(b):
                    r = m["m_r"]
                    dve.wait_ge(m["m_act"], b + 1)
                    v.tensor_copy(touch[:, 0:4], R[8][:, :, 0])
                    for t in range(TILES):
                        mx = v.max(top8[:, t, :], R[8][:, t, :])
                    mx.then_inc(r, 1)
                    step(b, 14)
                    v.tensor_copy(touch[:, 4:8], top8[:, :, 0])
                    for t in range(TILES):
                        mx = v.max_index(topi[:, t, :], top8[:, t, :], R[8][:, t, :])
                    mx.then_inc(r, 1)
                    step(b, 15)
                    v.tensor_copy(topf[:, :, 0:2], topi[:, :, 0:2]).then_inc(r, 1)
                    step(b, 16)
                    io = iota[:, :].unsqueeze(1).to_broadcast([P, TILES, EXPERTS])
                    for j in range(2):
                        last = v.tensor_tensor(R[2 + 2 * j], io, topf[:, :, j:j + 1].to_broadcast([P, TILES, EXPERTS]),
                                               ALU.is_equal)
                    last.then_inc(r, 1)
                    step(b, 17)
                    v.tensor_tensor(R[0], R[2], R[4], ALU.add).then_inc(m["m_cf"], 1)
                    dve.wait_ge(m["m_cf"], 3 * b + 1)
                    v.tensor_tensor(R[7], R[0], R[8], ALU.mult).then_inc(m["m_cf"], 1)
                    dve.wait_ge(m["m_cf"], 3 * b + 2)
                    if not (isinstance(b, int) and b == 0):
                        dve.wait_ge(m["m_cfT_ps"], b)
                    v.tensor_copy(cfh[:, :, :], R[7]).then_inc(m["m_cf"], 1)
                    dve.wait_ge(m["m_cf"], 3 * b + 3)
                    v.tensor_copy(cfx[:, :, 0:EXPERTS], cfh[:, :, :].bitcast(F32))
                    lo(cfx[:, :, EXPERTS:2 * EXPERTS], R[7], cfh[:, :, :]).then_inc(m["m_cfx"], 1)

                row_stats(0, 0)
                normalise(0, 0)
                dve.wait_ge(m["m_whi"], 5)
                lo(rw[:, :, EXPERTS:2 * EXPERTS], rw32[:, :, :], rw[:, :, 0:EXPERTS]).then_inc(m["m_wlo"], 1)
                lo(biasR[1][:, :], bias32[:, :], biasR[0][:, :]).then_inc(m["m_wlo"], 1)
                lo(eW1[1][:, :, :, :].rearrange("p k e h -> p (k e h)"), e1_32[:, :, :, :].rearrange("p k e h -> p (k e h)"),
                   eW1[0][:, :, :, :].rearrange("p k e h -> p (k e h)")).then_inc(m["m_wlo"], 1)
                lo(eW2[1][:, :, :], e2_32[:, :, :], eW2[0][:, :, :]).then_inc(m["m_wlo"], 1)
                XT_lo(0, 0)
                softplus(0)
                combine(0)

                def turn(b, q, has_next):
                    for u in range(UNITS):
                        U = UNITS * b + u
                        slot, two = u % 3, (q + u) % 2
                        if u < EXPERTS:
                            dve.wait_ge(m["m_silu"], U + 1)
                            dve.wait_ge(m["m_cfb"], EXPERTS * b + u + 1)
                            v.tensor_tensor(h32[:, two, :], CB[u % 2][:, :], s32[:, two, :],
                                            ALU.mult).then_inc(m["m_mult"], 1)
                        dve.wait_ge(m["m_hhi"], U + 1)
                        lo(H[1][:, slot, :], (h32 if u < EXPERTS else s32)[:, two, :],
                           H[0][:, slot, :]).then_inc(m["m_split"], 1)
                        if has_next:
                            if u == 1:
                                row_stats(b + 1, 1 - q)
                            if u == 2:
                                normalise(b + 1, 1 - q)
                            if u == 3:
                                XT_lo(b + 1, 1 - q)
                            if u == 5:
                                softplus(b + 1)
                            if u == 6:
                                combine(b + 1)
                    if not isinstance(b, int) or b >= 2:
                        dve.wait_ge(at_parity(q, "m_out_even", "m_out_odd"), 16 * (half_count(b, q) - 1 + q))
                    for h in range(2):
                        dve.wait_ge(m["m_y"], 2 * b + h + 1)
                        v.tensor_tensor(y[q][:, 2 * h:2 * h + 2, :], tok2(Y[h]), x2[q][:, 2 * h:2 * h + 2, :],
                                        ALU.add).then_inc(m["m_yout"], 1)

                pairs(dve, turn)

            @block2.tensor
            def _(pe):
                def T_X(b):
                    pe.wait_ge(m["m_norm"], TILES * (b + 1))
                    if not (isinstance(b, int) and b == 0):
                        pe.wait_ge(m["m_r"], ROUTE * (b - 1) + 2)
                        pe.wait_ge(m["m_cfT"], b)
                    for k in range(KD):
                        for t in range(TILES):
                            last = nc.tensor.transpose(M[k][:, t * P:(t + 1) * P], xn[:, t, k * P:(k + 1) * P],
                                                       ident[:, :])
                        last.then_inc(m["m_T_ps"], 1)

                def logits(b, q):
                    pe.wait_ge(m["m_T_lo"], 2 * (b + 1))
                    E2 = 2 * EXPERTS
                    for t in range(TILES):
                        for k in range(KD):
                            for part in (1, 0):
                                last = mm(M[0][:, t * E2:(t + 1) * E2], XT[q][part][:, k, t * P:(t + 1) * P],
                                          rw[:, k, :], start=(t == 0 and k == 0 and part == 1),
                                          stop=(k == KD - 1 and part == 0))
                    last.then_inc(m["m_lg_ps"], 1)

                def T_cf(b):
                    pe.wait_ge(m["m_cfx"], b + 1)
                    pe.wait_ge(m["m_T_lo"], 2 * (b + 1))
                    for t in range(TILES):
                        last = nc.tensor.transpose(M[1][:, t * P:(t + 1) * P], cfx[:, t, :], ident[:, :])
                    last.then_inc(m["m_cfT_ps"], 1)

                T_X(0)
                pe.wait_ge(m["m_wlo"], 4)
                logits(0, 0)
                T_cf(0)

                def turn(b, q, has_next):
                    first = isinstance(b, int) and b == 0

                    def up(u):
                        U = UNITS * b + u
                        two = (q + u) % 2
                        if not (first and u < 2):
                            pe.wait_ge(m["m_hhi"], U - 1)
                        for k in range(KD):
                            last = mm3(upB[two][:, :], eW1, XT[q], (slice(None), k, u, slice(None)),
                                       (slice(None), k, slice(None)), start=(k == 0), stop=(k == KD - 1))
                        last.then_inc(m["m_up"], 1)
                        if u < EXPERTS:
                            if not (first and u < 2):
                                pe.wait_ge(m["m_mult"], EXPERTS * b + u - 1)
                            mm(CB[u % 2][:, :], sel[:, u, :], cfT[q][:, :], start=True, stop=True)\
                                .then_inc(m["m_cfb"], 1)

                    def down(u):
                        pe.wait_ge(m["m_split"], UNITS * b + u + 1)
                        if u == 0 and not (isinstance(b, int) and b == 0):
                            pe.wait_ge(m["m_yout"], 2 * b)
                        for t in range(TILES):
                            last = mm3(tok2(Y[t // 2])[:, t % 2, :], H, eW2, (slice(None), u % 3, slice(t * P, t * P + P)),
                                       (slice(None), u, slice(None)), start=(u == 0 and t % 2 == 0))
                        last.then_inc(m["m_down"], 1)

                    pe.wait_ge(m["m_T_lo"], 2 * (b + 1))
                    pe.wait_ge(m["m_cfT"], b + 1)
                    for u in range(UNITS):
                        up(u)
                        if u >= 2:
                            down(u - 2)
                        if has_next:
                            if u == 3:
                                T_X(b + 1)
                            if u == 5:
                                logits(b + 1, 1 - q)
                    down(UNITS - 2)
                    down(UNITS - 1)
                    for t in range(TILES):
                        for part in (1, 0):
                            last = mm(tok2(Y[t // 2])[:, t % 2, :], cfT[q][:, t * P:(t + 1) * P],
                                      biasR[part][:, :], stop=(part == 0))
                        if t % 2 == 1:
                            last.then_inc(m["m_y"], 1)
                    if has_next:
                        T_cf(b + 1)

                pairs(pe, turn)


_INS = ["L0_attn_x", "L0_attn_ln_g", "L0_attn_ln_b", "L0_attn_h1_w1", "L0_attn_h1_b1", "L0_attn_h1_w2",
        "L0_attn_h1_b2", "L0_attn_h2_w1", "L0_attn_h2_b1", "L0_attn_h2_w2", "L0_attn_h2_b2", "L0_attn_fm_w1",
        "L0_attn_fm_b1", "L0_attn_fm_w2", "L0_attn_fm_b2", "L0_ffn_routing_W", "L0_ffn_expert_bias",
        "L0_ffn_sW1", "L0_ffn_sb1", "L0_ffn_sW2", "L0_ffn_sb2", "L0_ffn_rW1", "L0_ffn_rb1", "L0_ffn_rW2",
        "L0_ffn_rb2"]
_OUTS = [((4, 2048, 256), "float32")]


def kernel(**inputs):
    import numpy as _np
    import concourse.bacc as _bacc
    from concourse import mybir as _mybir
    from concourse.bass_utils import run_bass_kernel_spmd as _run

    nc = _bacc.Bacc("TRN2", target_bir_lowering=False, num_devices=1)
    arrays, args = {}, []
    for name in _INS:
        a = _np.ascontiguousarray(inputs[name])
        arrays[f"in_{name}_dram"] = a
        args.append(nc.dram_tensor(f"in_{name}_dram", a.shape, _mybir.dt.from_np(a.dtype), kind="ExternalInput").ap())
    for i, (shape, dtype) in enumerate(_OUTS):
        dt = _mybir.dt.from_np(_np.dtype(dtype))
        args.append(nc.dram_tensor(f"out_{i}_dram", shape, dt, kind="ExternalOutput").ap())
    bass_preln_layer(nc, *args)
    r = _run(nc, [arrays], core_ids=[0])
    return r.results[0]["out_0_dram"]
```

```python
from contextlib import ExitStack

import concourse.bass as bass
from concourse import mybir

F32 = mybir.dt.float32
F32R = mybir.dt.float32r
U32 = mybir.dt.uint32
ALU = mybir.AluOpType
ACT = mybir.ActivationFunctionType

P = 128
TOKENS_PER_BLOCK = 512
TILES = TOKENS_PER_BLOCK // P
CHUNK_TILES = 2
CHUNKS = TILES // CHUNK_TILES
EPS = 1e-5


def bass_preln_layer(nc, x, ln_g, ln_b, h1_w1, h1_b1, h1_w2, h1_b2, h2_w1, h2_b1, h2_w2, h2_b2,
                     fm_w1, fm_b1, fm_w2, fm_b2, routing_W, expert_bias, sW1, sb1, sW2, sb2,
                     rW1, rb1, rW2, rb2, out):
    batches, seq, D = x.shape
    DI = h1_w1.shape[1]
    NBLK = batches * seq // TOKENS_PER_BLOCK
    BLOCKS_PER_BATCH = seq // TOKENS_PER_BLOCK
    KD = D // P
    NH = DI // P
    EXPERTS = routing_W.shape[0]
    UNITS = EXPERTS + 1
    assert D == 256 and NH == 8 and EXPERTS == 8 and rW1.shape[2] == P and BLOCKS_PER_BATCH == 4
    T4 = TOKENS_PER_BLOCK

    x_tok = x.rearrange("b s d -> (b s) d").rearrange("(n p) d -> p n d", p=P)
    out_tok = out.rearrange("b s d -> (b s) d").rearrange("(n p) d -> p n d", p=P)
    x2_dram = nc.dram_tensor("x2_between_phases", (P, NBLK * TILES, D), F32, kind="Internal").ap()

    KB = 1024
    base = ((nc.sbuf_base + 31) // 32) * 32

    class Region:
        def __init__(self, at):
            self.at = at

        def put(self, name, shape, dt=F32):
            t = nc.alloc_sbuf_tensor_at(name, shape, dt, offset=self.at)
            n = 4
            for s in shape[1:]:
                n *= s
            self.at += (n + 31) // 32 * 32
            assert self.at <= nc.sbuf_usable_end, (name, self.at)
            return t

    with ExitStack() as ctx:
        def sem(name):
            return ctx.enter_context(nc.semaphore(name))

        common = Region(base)
        ident = common.put("ident", [P, P])
        consts = common.put("consts", [P, 6, TILES])
        C_HALF, C_QUARTER, C_INVN, C_EPS, C_NEGHALF = (consts[:, j, :] for j in range(5))
        stats = common.put("stats", [P, TILES, 6])
        lnw = common.put("lnw", [P, 8, TILES])
        touch1 = common.put("touch1", [P, TILES])
        ROW = dict(h2_b1=0, h1_b1=NH, fm_b1=2 * NH, h2_b2=3 * NH, h1_b2=3 * NH + KD, rb1=3 * NH + 2 * KD)
        ROW["sb1"] = ROW["rb1"] + EXPERTS
        ROW["routing"] = ROW["sb1"] + 1
        NROWS = ROW["routing"] + KD * EXPERTS
        cols = common.put("cols", [P, NROWS])

        def col(name, k=0):
            return cols[:, ROW[name] + k:ROW[name] + k + 1]

        phase_base = common.at

        r1 = Region(phase_base)
        W = {}
        for mlp in ("h2", "h1", "fm"):
            for part in ("hi", "lo"):
                W[mlp, 1, part] = r1.put(f"{mlp}_w1_{part}", [P, KD, DI], F32R)
            for part in ("hi", "lo"):
                W[mlp, 2, part] = r1.put(f"{mlp}_w2_{part}", [P, NH, D], F32R)
        nT_at = r1.at
        nT = [r1.put(f"nT_{p_}", [P, KD, T4], F32R) for p_ in ("hi", "lo")]
        qreg = Region(nT_at)
        QT = [qreg.put(f"QT_{p_}", [P, KD, T4], F32R) for p_ in ("hi", "lo")]
        ntok = [r1.put(f"ntok_{p_}", [P, TILES, D], F32R) for p_ in ("hi", "lo")]
        KT = [r1.put(f"KT_{p_}", [P, KD, T4], F32R) for p_ in ("hi", "lo")]
        ktok_at = r1.at
        Ktok = [r1.put(f"Ktok_{p_}", [P, TILES, D], F32R) for p_ in ("hi", "lo")]
        n2T_at = r1.at
        n2T = [r1.put(f"n2T_{p_}", [P, KD, T4], F32R) for p_ in ("hi", "lo")]
        xin_at = r1.at
        xin = r1.put("xin", [P, TILES, D])
        xa = r1.put("xa", [P, 2, TILES, D])
        resid = r1.put("resid", [P, 2, TILES, D])
        n32 = r1.put("n32", [P, TILES, D])
        work_at = r1.at
        work = r1.put("work", [P, TILES, D])
        KT32 = Region(work_at).put("KT32", [P, KD, T4])
        G = [r1.put(f"G_{p_}", [P, 3, T4], F32R) for p_ in ("hi", "lo")]
        G32 = r1.put("G32", [P, 2, T4])
        S32 = r1.put("S32", [P, CHUNKS, 384])
        sp_at = r1.at
        SP_ = [r1.put(f"S_{p_}", [P, CHUNKS, 384], F32R) for p_ in ("hi", "lo")]
        state = r1.put("state", [P, 2, KD * D])
        St = [[r1.put(f"state{c}_{p_}", [P, KD * D], F32R) for p_ in ("hi", "lo")] for c in range(CHUNKS)]
        sp_end = r1.at
        tri = r1.put("tri", [P, P])
        gB = r1.put("gB", [P, D])
        bB = r1.put("bB", [P, D])
        fb2B = r1.put("fb2B", [P, D])
        brows = r1.put("brows", [P, P])
        stage_at = {}
        fm_at = phase_base + 2 * 4 * 8 * KB
        stage_at["h2", 1] = fm_at
        stage_at["h2", 2] = fm_at + 8 * KB
        stage_at["h1", 1] = fm_at + 16 * KB
        stage_at["h1", 2] = fm_at + 24 * KB
        stage_at["fm", 1] = n2T_at
        stage_at["fm", 2] = ktok_at
        stage = {}
        for (mlp, w), at in stage_at.items():
            shape = [P, KD, DI] if w == 1 else [P, NH, D]
            stage[mlp, w] = Region(at).put(f"{mlp}_w{w}_f32", shape)

        r2 = Region(phase_base)
        eW1 = [r2.put(f"eW1_{p_}", [P, KD, UNITS, P], F32R) for p_ in ("hi", "lo")]
        eW2 = [r2.put(f"eW2_{p_}", [P, UNITS, D], F32R) for p_ in ("hi", "lo")]
        e1_32 = r2.put("e1_32", [P, KD, UNITS, P])
        e2_32 = r2.put("e2_32", [P, UNITS, D])
        sel = r2.put("sel", [P, EXPERTS, P], F32R)
        bias32 = r2.put("bias32", [P, D])
        biasR = r2.put("biasR", [P, D], F32R)
        rw = r2.put("rw", [P, KD, 2 * EXPERTS], F32R)
        ebB = r2.put("ebB", [P, EXPERTS])
        iota = r2.put("iota", [P, EXPERTS])
        half8 = r2.put("half8", [P, TILES, EXPERTS])
        assert r2.at <= fm_at
        r3 = Region(fm_at)
        H = [r3.put(f"H_{p_}", [P, 3, T4], F32R) for p_ in ("hi", "lo")]
        s32 = r3.put("s32", [P, 2, T4])
        h32 = Region(xin_at).put("h32", [P, 2, T4])
        y = [r3.put(f"y_{q}", [P, TILES, D]) for q in range(2)]
        cfT1 = r3.put("cfT1", [P, T4], F32R)
        assert r3.at <= nT_at
        r4 = Region(nT_at)
        x2 = r4.put("x2", [P, 4, TILES, D])
        XT0 = [r4.put(f"XT0_{p_}", [P, KD, T4], F32R) for p_ in ("hi", "lo")]
        xn = r4.put("xn", [P, TILES, D])
        cfx = r4.put("cfx", [P, TILES, P])
        assert r4.at <= n2T_at
        r5 = Region(n2T_at)
        XT1 = [r5.put(f"XT1_{p_}", [P, KD, T4], F32R) for p_ in ("hi", "lo")]
        r6 = Region(sp_at)
        cfT0 = r6.put("cfT0", [P, T4], F32R)
        rt = r6.put("rt", [P, 11, TILES, EXPERTS])
        top8 = r6.put("top8", [P, TILES, 8])
        topi = r6.put("topi", [P, TILES, 8], U32)
        topf = r6.put("topf", [P, TILES, 8])
        cfh = r6.put("cfh", [P, TILES, EXPERTS], F32R)
        touch = r6.put("touch", [P, 8])
        stats2 = r6.put("stats2", [P, TILES, 6])
        lnw2 = r6.put("lnw2", [P, 8, TILES])
        assert r6.at <= sp_end
        XT = [XT0, XT1]
        cfT = [cfT0, cfT1]

        bank = [ctx.enter_context(nc.psum_tensor(f"bank{j}", [P, 512], F32)) for j in range(8)]
        upB, A, B, M = bank[0:2], bank[2:4], bank[4:6], bank[6:8]
        up3, CB, Y, M1 = bank[0:3], bank[3:5], bank[5:7], bank[7]

        def tok2(b):
            return b[:, :].rearrange("p (t d) -> p t d", t=2)

        names1 = """aggregated eps_added ld_x ld_rows cols_ps cols_out ld_const ld_h2w1 ld_h2w2 ld_h1w1 ld_h1w2 ld_fmw1 ld_fmw2 const_pool
            w_hi w_lo x_used a_stats a_rstd a_norm a_out nT_ps nT_hi nT_lo ntok_hi ntok_lo
            up_ready gelu_hi gelu_done split_ready down_done
            k_ready k_f32 k_hi k_lo ktok_ps ktok_hi ktok_lo q_ready q_hi q_lo
            delta_ready state_add state_hi state_lo qs_done s_ps s_masked s_hi s_lo s_start
            t_ready t_gelu e_stats e_rstd e_norm e_mid e_out n2T_ps n2T_hi n2T_lo
            f_ready resid_set x2_ready fb2_st_x2 pool_chain""".split()
        s = {n: sem(n) for n in names1}
        names2 = """m_ldw m_ldp m_pool m_whi m_ldx2 m_copy m_wlo m_ldx_even m_ldx_odd m_stats m_rstd m_norm m_T_ps
            m_T_hi m_T_lo m_lg_ps m_r m_exp m_ln m_act m_cf m_cfx m_cfT_ps m_cfT m_cfb m_up m_silu
            m_mult m_hhi m_split m_down m_y m_yout m_out_even m_out_odd""".split()
        m = {n: sem(n) for n in names2}

        def mm(o, lhsT, rhs, start=False, stop=False):
            return nc.tensor.matmul(o, lhsT, rhs, start=start, stop=stop, skip_group_check=True)

        def mm3(o, w, v, ws, vs, start=False, stop=False):
            mm(o, w[1][ws], v[0][vs], start=start)
            mm(o, w[0][ws], v[1][vs])
            return mm(o, w[0][ws], v[0][vs], stop=stop)

        HU = 2 * NH
        FU = 3 * NH

        def unit_base(i):
            return 0 if isinstance(i, int) and i == 0 else i * FU - NH

        def off(i):
            return 0 if isinstance(i, int) and i == 0 else 1

        MLP = ("h2", "h1", "fm")
        B1 = ("h2_b1", "h1_b1", "fm_b1")
        LAG = 3
        routing_cols = cols[:, ROW["routing"]:NROWS].rearrange("p (k e) -> p k e", k=KD)
        W2 = {(mlp, w): (W[mlp, w, "hi"], W[mlp, w, "lo"]) for mlp in MLP for w in (1, 2)}

        def zero_or_state(i):
            if isinstance(i, int):
                return 0 if i % BLOCKS_PER_BATCH == 0 else 1
            return (((i % BLOCKS_PER_BATCH) + 3) >> 2).with_bounds(min_val=0, max_val=1)

        def one(i):
            return bass.ds(i, 1) if not isinstance(i, int) else slice(i, i + 1)

        def par(i):
            return one(i % 2)

        BIAS_LO = 32
        ROUTE = 18
        LAST = UNITS - LAG

        def at_parity(q, even, odd):
            return m[odd] if q else m[even]

        def routing_bank(b, j):
            return A[j] if is_first(b) else M1

        def x2_of(b):
            slot = b % 4
            return x2[:, one(slot if isinstance(b, int) else slot.with_bounds(min_val=0, max_val=3)), :, :]\
                .rearrange("p o t d -> p (o t) d")

        def pairs(eng, body):
            body(0, 0, 2)
            with eng.Fori(0, NBLK // 2 - 2) as j:
                body(2 * j + 1, 1, 2)
                body(2 * j + 2, 0, 2)
            for b in range(NBLK - 3, NBLK):
                body(b, b % 2, min(2, NBLK - 1 - b))

        def is_first(b):
            return isinstance(b, int) and b == 0

        def half_count(b, q):
            return (b - q) // 2 + 1 if isinstance(b, int) else ((b - q) >> 1) + 1

        with nc.Block() as block:
            @block.sync
            def _(sp):
                def load(b, q):
                    sp.dma_start(x2_of(b), x2_dram[:, bass.ds(b * TILES, TILES), :])\
                      .then_inc(at_parity(q, "m_ldx_even", "m_ldx_odd"), 16)

                def store(b, q):
                    sp.wait_ge(m["m_yout"], 2 * (b + 1))
                    sp.wait_ge(m["m_whi"], 1)
                    sp.dma_start(out_tok[:, bass.ds(b * TILES, TILES), :], y[q][:, :, :])\
                      .then_inc(at_parity(q, "m_out_even", "m_out_odd"), 16)

                def store_then_load(b, q):
                    store(b, q)
                    load(b + 3, 1 - q)

                sp.dma_start(xin[:, :, :], x_tok[:, 0:TILES, :]).then_inc(s["ld_x"], 16)
                for name, src in (("h2_b1", h2_b1), ("h1_b1", h1_b1), ("fm_b1", fm_b1), ("h2_b2", h2_b2),
                                  ("h1_b2", h1_b2), ("sb1", sb1)):
                    rows = src.rearrange("(k p) -> k p", p=P)
                    sp.dma_start(brows[ROW[name]:ROW[name] + rows.shape[0], :], rows).then_inc(s["ld_rows"], 16)
                sp.dma_start(brows[ROW["rb1"]:ROW["rb1"] + EXPERTS, :], rb1).then_inc(s["ld_rows"], 16)
                for k in range(KD):
                    at = ROW["routing"] + k * EXPERTS
                    sp.dma_start(brows[at:at + EXPERTS, :], routing_W[:, k * P:(k + 1) * P]).then_inc(s["ld_rows"], 16)
                sp.dma_start(fb2B[:, :], fm_b2.partition_broadcast(P)).then_inc(s["fb2_st_x2"], 16)
                w_dram = {("h2", 1): h2_w1, ("h2", 2): h2_w2, ("h1", 1): h1_w1, ("h1", 2): h1_w2,
                          ("fm", 1): fm_w1, ("fm", 2): fm_w2}
                for key in (("h2", 1), ("h2", 2), ("h1", 1), ("h1", 2), ("fm", 1), ("fm", 2)):
                    src = w_dram[key].rearrange("(k p) n -> p k n", p=P)
                    sp.dma_start(stage[key][:, :, :], src).then_inc(s[f"ld_{key[0]}w{key[1]}"], 16)

                def load_x(i):
                    sp.wait_ge(s["x_used"], i)
                    sp.wait_ge(s["x_used"], 1)
                    sp.dma_start(xin[:, :, :], x_tok[:, bass.ds(i * TILES, TILES), :]).then_inc(s["ld_x"], 16)

                def store_x2(i):
                    sp.wait_ge(s["x2_ready"], 2 * (i + 1) + 2)
                    sp.wait_ge(s["x2_ready"], 1)
                    sp.dma_start(x2_dram[:, bass.ds(i * TILES, TILES), :],
                                 resid[:, par(i), :, :].rearrange("p o t d -> p (o t) d")).then_inc(s["fb2_st_x2"], 16)

                load_x(1)
                with sp.Fori(1, NBLK - 1) as i:
                    load_x(i + 1)
                    store_x2(i - 1)
                sp.wait_ge(s["down_done"], unit_base(NBLK - 1) + HU)
                for k in range(KD):
                    sp.dma_start(e1_32[:, k, 0:EXPERTS, :], rW1[:, k * P:(k + 1) * P, :].rearrange("e p h -> p e h"))\
                      .then_inc(m["m_ldw"], 16)
                    sp.dma_start(e1_32[:, k, EXPERTS, :], sW1[k * P:(k + 1) * P, :]).then_inc(m["m_ldw"], 16)
                sp.dma_start(e2_32[:, 0:EXPERTS, :], rW2.rearrange("e h d -> h e d")).then_inc(m["m_ldw"], 16)
                sp.dma_start(e2_32[:, EXPERTS, :], sW2).then_inc(m["m_out_odd"], 16)
                sp.dma_start(ebB[:, :], expert_bias.partition_broadcast(P)).then_inc(m["m_out_even"], 16)
                sp.wait_ge(m["m_pool"], 1)
                for r in (0, BIAS_LO):
                    sp.dma_start(bias32[r:r + EXPERTS, :], rb2).then_inc(m["m_ldw"], 16)
                    sp.dma_start(bias32[r + EXPERTS:r + 2 * EXPERTS, :], rb2).then_inc(m["m_ldw"], 16)
                    sp.dma_start(bias32[r + 2 * EXPERTS:r + 2 * EXPERTS + 1, :], sb2.rearrange("(a d) -> a d", a=1))\
                      .then_inc(m["m_ldw"], 16)
                sp.wait_ge(s["fb2_st_x2"], 16 * (NBLK - 1))
                sp.wait_ge(s["t_ready"], 2 * NBLK)
                load(0, 0)
                load(1, 1)
                store_x2(NBLK - 2)
                sp.wait_ge(m["m_stats"], TILES)
                load(2, 0)
                store_x2(NBLK - 1)
                sp.wait_ge(s["fb2_st_x2"], 16 * (NBLK + 1))
                store_then_load(0, 0)
                with sp.Fori(0, (NBLK - 4) // 2) as j:
                    store_then_load(2 * j + 1, 1)
                    store_then_load(2 * j + 2, 0)
                for b in range(NBLK - 3, NBLK):
                    store(b, b % 2)
                sp.wait_ge(m["m_out_even"], 16 * (NBLK // 2 + 1))
                sp.wait_ge(m["m_out_odd"], 16 * (NBLK // 2 + 1))

            @block.gpsimd
            def _(pool):
                g = nc.gpsimd

                g.memset(ident[:, :], 0.0).then_inc(s["pool_chain"], 1)
                g.memset(tri[:, :], 1.0).then_inc(s["pool_chain"], 1)
                g.memset(state[:, 0, :], 0.0).then_inc(s["const_pool"], 1)
                for col, val in ((C_HALF, 0.5), (C_QUARTER, 0.25), (C_INVN, 1.0 / D), (C_EPS, EPS), (C_NEGHALF, -0.5)):
                    g.memset(col, val).then_inc(s["pool_chain"], 1)
                pool.wait_ge(s["pool_chain"], 7)
                g.affine_select(out=ident[:, :], in_=ident[:, :], compare_op=ALU.not_equal, fill=1.0,
                                base=0, pattern=[[-1, P]], channel_multiplier=1).then_inc(s["const_pool"], 1)
                g.affine_select(out=tri[:, :], in_=tri[:, :], compare_op=ALU.is_ge, fill=0.0,
                                base=0, pattern=[[1, P]], channel_multiplier=-1).then_inc(s["const_pool"], 1)
                for dst, src in ((gB, ln_g), (bB, ln_b)):
                    pool.dma_start(dst[:, :], src.partition_broadcast(P)).then_inc(s["ld_const"], 16)

                def rstd(st, w, stat_sem, stat_count, done, done_before):
                    me, mo, v0, v1 = st[:, :, 1], st[:, :, 4], st[:, :, 2], st[:, :, 5]
                    w = [w[:, j, :] for j in range(8)]
                    pool.wait_ge(stat_sem, stat_count)
                    g.tensor_tensor(w[2], me, mo, ALU.add).then_inc(done, 1)
                    g.tensor_tensor(w[3], me, mo, ALU.subtract).then_inc(done, 1)
                    g.tensor_tensor(w[4], v0, v1, ALU.add).then_inc(done, 1)
                    k = 3
                    for o, a, b, op in ((w[0], w[2], C_HALF, ALU.mult), (w[5], w[3], w[3], ALU.mult),
                                        (w[6], w[5], C_QUARTER, ALU.mult), (w[7], w[4], C_INVN, ALU.mult),
                                        (w[5], w[6], w[7], ALU.add), (w[6], w[5], C_EPS, ALU.add),
                                        (w[1], w[6], C_NEGHALF, ALU.pow)):
                        pool.wait_ge(done, done_before + k)
                        g.tensor_tensor(o, a, b, op).then_inc(done, 1)
                        k += 1

                def rstd_of(w, aggregates, done):
                    pool.wait_ge(s["aggregated"], TILES * aggregates)
                    g.tensor_tensor(w[:, 7, :], w[:, 6, :], C_EPS, ALU.add).then_inc(s["eps_added"], 1)
                    pool.wait_ge(s["eps_added"], aggregates)
                    g.tensor_tensor(w[:, 1, :], w[:, 7, :], C_NEGHALF, ALU.pow).then_inc(done, 10)

                def x2_rstd(b):
                    rstd(stats2, lnw2, m["m_stats"], TILES * (b + 1), m["m_rstd"], 10 * b)

                def act_pow(b):
                    pool.wait_ge(m["m_r"], ROUTE * b + 13)
                    g.tensor_tensor(rt[:, 8, :, :], rt[:, 6, :, :], half8[:, :, :], ALU.pow).then_inc(m["m_act"], 1)

                gB3 = gB[:, :].unsqueeze(1).to_broadcast([P, TILES, D])
                bB3 = bB[:, :].unsqueeze(1).to_broadcast([P, TILES, D])

                def norm_n(i):
                    if isinstance(i, int) and i == 0:
                        rstd_of(lnw, 1, s["a_rstd"])
                        rstd_of(lnw, 2, s["a_rstd"])
                        return
                    rstd(stats, lnw, s["a_stats"], 8 * i + 4, s["a_rstd"], 20 * i)
                    rstd(stats, lnw, s["a_stats"], 8 * i + 8, s["a_rstd"], 20 * i + 10)
                    pool.wait_ge(s["a_norm"], 2 * TILES * (i + 1))
                    g.tensor_tensor(n32[:, :, :], n32[:, :, :], gB3, ALU.mult).then_inc(s["a_out"], 1)
                    pool.wait_ge(s["a_out"], 2 * i + 1)
                    g.tensor_tensor(n32[:, :, :], n32[:, :, :], bB3, ALU.add).then_inc(s["a_out"], 1)

                def norm_t(i):
                    if isinstance(i, int) and i == NBLK - 1:
                        rstd_of(lnw, 3, s["e_rstd"])
                        rstd_of(lnw, 4, s["e_rstd"])
                        return
                    rstd(stats, lnw, s["e_stats"], 8 * i + 4, s["e_rstd"], 20 * i)
                    rstd(stats, lnw, s["e_stats"], 8 * i + 8, s["e_rstd"], 20 * i + 10)
                    pool.wait_ge(s["e_norm"], 2 * TILES * (i + 1))
                    g.tensor_tensor(work[:, :, :], work[:, :, :], gB3, ALU.mult).then_inc(s["e_out"], 1)
                    pool.wait_ge(s["e_out"], 2 * i + 1)
                    g.tensor_tensor(work[:, :, :], work[:, :, :], bB3, ALU.add).then_inc(s["e_out"], 1)

                norm_n(0)
                pool.wait_ge(s["ld_const"], 16 * 2)
                norm_n(1)
                norm_t(0)
                with pool.Fori(1, NBLK - 1) as i:
                    norm_n(i + 1)
                    norm_t(i)
                pool.wait_ge(s["down_done"], unit_base(NBLK - 1) + HU)
                g.memset(bias32[:, :], 0.0).then_inc(m["m_pool"], 1)
                g.memset(sel[:, :, :].bitcast(F32), 0.0).then_inc(m["m_pool"], 1)
                g.memset(half8[:, :, :], 0.5).then_inc(m["m_pool"], 1)
                for e in range(EXPERTS):
                    g.memset(iota[:, e:e + 1], float(e)).then_inc(m["m_pool"], 1)
                for half in range(2):
                    pool.wait_ge(m["m_pool"], 3 + EXPERTS + half)
                    g.affine_select(out=sel[:, :, :], in_=sel[:, :, :].bitcast(F32), compare_op=ALU.not_equal,
                                    fill=1.0, base=-EXPERTS * half, pattern=[[-1, EXPERTS], [0, P]],
                                    channel_multiplier=1).then_inc(m["m_pool"], 1)
                pool.wait_ge(s["delta_ready"], 2 * NBLK)
                g.memset(cfx[:, :, :], 0.0).then_inc(m["m_pool"], 1)
                pool.wait_ge(m["m_pool"], 14)
                for r in (0, BIAS_LO):
                    g.memset(cfx[:, :, r + 2 * EXPERTS:r + 2 * EXPERTS + 1], 1.0).then_inc(m["m_pool"], 1)
                norm_t(NBLK - 1)
                x2_rstd(0)
                x2_rstd(1)
                act_pow(0)

                def turn(b, q, ahead):
                    if ahead >= 1:
                        act_pow(b + 1)
                    if ahead >= 2:
                        x2_rstd(b + 2)

                pairs(pool, turn)

            @block.scalar
            def _(act):
                a = nc.scalar

                def hi_weights(key):
                    act.wait_ge(s[f"ld_{key[0]}w{key[1]}"], 16)
                    if key == ("fm", 1):
                        act.wait_ge(s["w_lo"], 4)
                    a.copy(W[key[0], key[1], "hi"][:, :, :], stage[key][:, :, :]).then_inc(s["w_hi"], 1)

                def unit(i, u, j, ht, slot_off, between=None):
                    U = unit_base(i) + u
                    slot = (slot_off + u) % 3
                    known_first = isinstance(i, int) and i == 0
                    act.wait_ge(s["up_ready"], U + 1)
                    if not (known_first and u < 3):
                        act.wait_ge(s["down_done"], U - 2)
                    a.activation(G[0][:, slot, :], upB[u % 2][:, :], ACT.Gelu,
                                 bias=col(B1[j], ht)).then_inc(s["gelu_hi"], 1)
                    if not (known_first and u < 2):
                        act.wait_ge(s["split_ready"], U - 1)
                    if between is not None:
                        between()
                    a.activation(G32[:, u % 2, :], upB[u % 2][:, :], ACT.Gelu,
                                 bias=col(B1[j], ht)).then_inc(s["gelu_done"], 1)

                def hi_T(dst, banks, ps, hi, before):
                    for k in range(KD):
                        act.wait_ge(s[ps], before + k + 1)
                        a.copy(dst[0][:, k, :], banks[k][:, :]).then_inc(s[hi], 1)

                def nT_hi(i):
                    hi_T(nT, A, "nT_ps", "nT_hi", 2 * i)
                    a.copy(ntok[0][:, :, :], n32[:, :, :]).then_inc(s["ntok_hi"], 1)

                def state_hi(c, i):
                    if c == 0:
                        if not (isinstance(i, int) and i == 0):
                            act.wait_ge(s["state_add"], 2 * i)
                            act.wait_ge(s["qs_done"], 2 * i - 1)
                        src = state[:, one(zero_or_state(i)), :]
                    else:
                        act.wait_ge(s["state_add"], 2 * i + 1)
                        if not (isinstance(i, int) and i == 0):
                            act.wait_ge(s["qs_done"], 2 * i)
                        src = state[:, 1:2, :]
                    a.copy(St[c][0][:, :], src.rearrange("p o n -> p (o n)")).then_inc(s["state_hi"], 1)

                def next_units(i):
                    for u in range(LAG):
                        unit(i, u, 0, u, off(i))

                def h_part(i):
                    first = isinstance(i, int) and i == 0
                    for u in range(LAG, HU):
                        unit(i, u, u // NH, u % NH, off(i))
                        if u == 9 and not first:
                            hi_T(n2T, M, "n2T_ps", "n2T_hi", 2 * (i - 1))
                        if first and u in (8, 9):
                            hi_weights(("fm", u - 7))
                        if u == 10:
                            for f in range(KD):
                                if f == 0:
                                    act.wait_ge(s["k_ready"], i + 1)
                                else:
                                    act.wait_ge(s["down_done"], unit_base(i) + NH)
                                a.activation(KT32[:, f, :], A[f][:, :], ACT.Identity,
                                             bias=col("h2_b2", f)).then_inc(s["k_f32"], 1)
                                a.activation(KT[0][:, f, :], A[f][:, :], ACT.Identity,
                                             bias=col("h2_b2", f)).then_inc(s["k_hi"], 1)
                        if u == 13:
                            if first:
                                act.wait_ge(s["w_lo"], 6)
                            for h in range(2):
                                act.wait_ge(s["ktok_ps"], 2 * i + h + 1)
                                a.copy(Ktok[0][:, 2 * h:2 * h + 2, :], tok2(M[h])).then_inc(s["ktok_hi"], 1)

                def fm_units(i, lo_, hi_, base):
                    for v_ in range(lo_, hi_):
                        q_first = (lambda: QT_hi(i, 0)) if base == HU and v_ == LAG - 1 else None
                        unit(i, base + v_, 2, v_, 1, q_first)

                def QT_hi(i, f):
                    if f == 0:
                        act.wait_ge(s["q_ready"], i + 1)
                    else:
                        act.wait_ge(s["down_done"], unit_base(i) + HU)
                    a.activation(QT[0][:, f, :], B[f][:, :], ACT.Identity,
                                 bias=col("h1_b2", f)).then_inc(s["q_hi"], 1)

                def attention(i, last):
                    if isinstance(i, int) and i == 0:
                        QT_hi(i, 0)
                    QT_hi(i, 1)
                    state_hi(1, i)
                    for c in range(CHUNKS):
                        act.wait_ge(s["s_masked"], 4 * i + 2 * c + 2)
                        a.copy(SP_[0][:, c, :], S32[:, c, :]).then_inc(s["s_hi"], 1)
                    if not last:
                        state_hi(0, i + 1)
                    for c in range(CHUNKS):
                        act.wait_ge(s["t_ready"], 2 * i + c + 1)
                        a.activation(work[:, 2 * c:2 * c + 2, :], tok2(M[c]), ACT.Gelu).then_inc(s["t_gelu"], 1)
                    if not last:
                        nT_hi(i + 1)

                def XT_hi(b, q, k):
                    act.wait_ge(m["m_T_ps"], 2 * b + k + 1)
                    a.copy(XT[q][0][:, k, :], routing_bank(b, k)[:, :]).then_inc(m["m_T_hi"], 1)

                def softplus_tables(b):
                    a.preload_act_table_set("natural_log_exp_and_others")
                    act.wait_ge(m["m_r"], ROUTE * b + 4)
                    a.activation(rt[:, 3, :, :], rt[:, 2, :, :], ACT.Exp, scale=-1.0).then_inc(m["m_exp"], 1)
                    act.wait_ge(m["m_r"], ROUTE * b + 5)
                    a.activation(rt[:, 5, :, :], rt[:, 4, :, :], ACT.Ln).then_inc(m["m_ln"], 1)

                def cfT_out(b, q):
                    act.wait_ge(m["m_cfT_ps"], b + 1)
                    a.copy(cfT[q][:, :], routing_bank(b, 1)[:, :]).then_inc(m["m_cfT"], 1)

                act.wait_ge(s["cols_ps"], 1)
                a.copy(cols[:, :], B[0][:, 0:NROWS]).then_inc(s["cols_out"], 1)
                act.wait_ge(s["const_pool"], 3)
                act.wait_ge(s["cols_out"], 1)
                state_hi(0, 0)
                hi_weights(("h2", 1))
                hi_weights(("h2", 2))
                a.preload_act_table_set("gelu_and_others")
                nT_hi(0)
                next_units(0)
                hi_weights(("h1", 1))
                hi_weights(("h1", 2))
                h_part(0)
                attention(0, False)
                next_units(1)
                with act.Fori(1, NBLK - 1) as i:
                    h_part(i)
                    fm_units(i, 0, LAG, HU)
                    attention(i, False)
                    fm_units(i, LAG, NH, HU)
                    next_units(i + 1)
                last = NBLK - 1
                h_part(last)
                fm_units(last, 0, LAG, HU)
                attention(last, True)
                fm_units(last, LAG, NH, HU)
                a.copy(rw[:, :, 0:EXPERTS], routing_cols).then_inc(m["m_whi"], 1)
                act.wait_ge(m["m_ldw"], 16 * 11)
                act.wait_ge(m["m_out_odd"], 16)
                act.wait_ge(m["m_out_even"], 16)
                a.copy(eW1[0][:, :, :, :], e1_32[:, :, :, :]).then_inc(m["m_whi"], 1)
                a.copy(eW2[0][:, :, :], e2_32[:, :, :]).then_inc(m["m_whi"], 1)
                a.copy(biasR[:, :], bias32[:, :]).then_inc(m["m_whi"], 1)
                hi_T(n2T, M, "n2T_ps", "n2T_hi", 2 * last)
                fm_units(NBLK, 0, 2, 0)
                for k in range(KD):
                    XT_hi(0, 0, k)
                fm_units(NBLK, 2, 3, 0)
                softplus_tables(0)
                fm_units(NBLK, 3, NH, 0)
                XT_hi(1, 1, 0)

                def turn(b, q, ahead):
                    first = is_first(b)
                    late = int(first)
                    cfT_out(b, q)
                    for u in range(UNITS):
                        U = UNITS * b + u
                        slot, two = u % 3, (q + u) % 2
                        bias = col("rb1", u) if u < EXPERTS else col("sb1")
                        act.wait_ge(m["m_up"], U + 1)
                        if not (first and u < 2):
                            act.wait_ge(m["m_split"], U - 1)
                        a.activation(s32[:, two, :], up3[slot][:, :], ACT.Silu, bias=bias).then_inc(m["m_silu"], 1)
                        if not (first and u < 3):
                            act.wait_ge(m["m_down"], U - 2)
                        if u < EXPERTS:
                            act.wait_ge(m["m_mult"], EXPERTS * b + u + 1)
                            a.copy(H[0][:, slot, :], h32[:, two, :]).then_inc(m["m_hhi"], 1)
                        else:
                            a.activation(H[0][:, slot, :], up3[slot][:, :], ACT.Silu, bias=bias)\
                             .then_inc(m["m_hhi"], 1)
                        if ahead >= 1:
                            if u in (0, 1) and not (first and u == 1):
                                XT_hi(b + 1, 1 - q, u + late)
                            if u - late == 2:
                                softplus_tables(b + 1)

                pairs(act, turn)

            @block.vector
            def _(dve):
                v = nc.vector

                def lo(dst, src, hi):
                    return v.tensor_tensor(dst, src, hi.bitcast(F32), ALU.subtract)

                def lo_weights(key, before):
                    dve.wait_ge(s["w_hi"], before + 1)
                    lo(W[key[0], key[1], "lo"][:, :, :], stage[key][:, :, :],
                       W[key[0], key[1], "hi"][:, :, :]).then_inc(s["w_lo"], 1)

                def lo_T(dst, banks, hi, lo_, before):
                    for k in range(KD):
                        dve.wait_ge(s[hi], before + k + 1)
                        lo(dst[1][:, k, :], banks[k][:, :], dst[0][:, k, :]).then_inc(s[lo_], 1)

                def nT_lo(i):
                    lo_T(nT, A, "nT_hi", "nT_lo", 2 * i)
                    dve.wait_ge(s["ntok_hi"], i + 1)
                    lo(ntok[1][:, :, :], n32[:, :, :], ntok[0][:, :, :]).then_inc(s["ntok_lo"], 1)

                def row_stats(buf, done):
                    for t in range(TILES):
                        v.bn_stats(stats[:, t, :], buf[:, t, :]).then_inc(done, 1)

                def normalise(dst, src, done):
                    for t in range(TILES):
                        v.tensor_scalar(dst[:, t, :], src[:, t, :], lnw[:, 0, t:t + 1], lnw[:, 1, t:t + 1],
                                        ALU.subtract, ALU.mult).then_inc(done, 1)

                def scale_shift(buf, at_sem, at_count, norm_sem, norm_count, done, done_before):
                    dve.wait_ge(at_sem, at_count)
                    dve.wait_ge(norm_sem, norm_count)
                    v.tensor_tensor(buf[:, :, :], buf[:, :, :], gB[:, :].unsqueeze(1).to_broadcast([P, TILES, D]),
                                    ALU.mult).then_inc(done, 1)
                    dve.wait_ge(done, done_before + 1)
                    v.tensor_tensor(buf[:, :, :], buf[:, :, :], bB[:, :].unsqueeze(1).to_broadcast([P, TILES, D]),
                                    ALU.add).then_inc(done, 1)

                def xa_of(i):
                    return xa[:, par(i), :, :].rearrange("p o t d -> p (o t) d")

                def resid_of(i):
                    return resid[:, par(i), :, :].rearrange("p o t d -> p (o t) d")

                def aggregate(stat_sem, count):
                    dve.wait_ge(stat_sem, count)
                    for t in range(TILES):
                        v.bn_aggr(lnw[:, 0:7:6, t], stats[:, t, :]).then_inc(s["aggregated"], 1)

                def a_step(i, step):
                    if step == 0:
                        dve.wait_ge(s["ld_x"], 16 * (i + 1))
                        row_stats(xin, s["a_stats"])
                    elif step == 1:
                        dve.wait_ge(s["a_rstd"], 20 * i + 10)
                        normalise(xa_of(i), xin, s["a_norm"])
                    elif step == 2:
                        dve.wait_ge(s["a_norm"], 2 * TILES * i + TILES)
                        v.tensor_copy(touch1[:, :], lnw[:, 0, :])
                        row_stats(xa_of(i), s["a_stats"])
                    else:
                        dve.wait_ge(s["a_rstd"], 20 * i + 20)
                        normalise(n32, xa_of(i), s["a_norm"])

                def residual(i):
                    dve.wait_ge(s["fb2_st_x2"], 16 if isinstance(i, int) and i == 0 else 16 * i)
                    v.tensor_tensor(resid_of(i), xin[:, :, :], xa_of(i), ALU.add).then_inc(s["x_used"], 1)
                    dve.wait_ge(s["x_used"], i + 1)
                    v.tensor_tensor(resid_of(i), resid_of(i), fb2B[:, :].unsqueeze(1).to_broadcast([P, TILES, D]),
                                    ALU.add).then_inc(s["resid_set"], 1)

                def unit(i, u, slot_off):
                    U = unit_base(i) + u
                    slot = (slot_off + u) % 3
                    dve.wait_ge(s["gelu_done"], U + 1)
                    lo(G[1][:, slot, :], G32[:, u % 2, :], G[0][:, slot, :]).then_inc(s["split_ready"], 1)

                def e_step(i, step):
                    w3 = work[:, :, :]
                    if step == 0:
                        dve.wait_ge(s["t_gelu"], 2 * i + 2)
                        row_stats(work, s["e_stats"])
                    elif step == 1:
                        dve.wait_ge(s["e_rstd"], 20 * i + 10)
                        normalise(work, work, s["e_norm"])
                    elif step == 2:
                        dve.wait_ge(s["e_norm"], 2 * TILES * i + TILES)
                        v.tensor_tensor(w3, w3, gB[:, :].unsqueeze(1).to_broadcast([P, TILES, D]),
                                        ALU.mult).then_inc(s["e_mid"], 1)
                    elif step == 3:
                        dve.wait_ge(s["e_mid"], 3 * i + 1)
                        v.tensor_tensor(w3, w3, bB[:, :].unsqueeze(1).to_broadcast([P, TILES, D]),
                                        ALU.add).then_inc(s["e_mid"], 1)
                        dve.wait_ge(s["e_mid"], 3 * i + 2)
                        v.tensor_tensor(w3, w3, xa_of(i), ALU.add).then_inc(s["e_mid"], 1)
                    elif step == 4:
                        dve.wait_ge(s["e_mid"], 3 * i + 3)
                        row_stats(work, s["e_stats"])
                    else:
                        dve.wait_ge(s["e_rstd"], 20 * i + 20)
                        normalise(work, work, s["e_norm"])

                def state_lo(c, i):
                    dve.wait_ge(s["state_hi"], 2 * i + c + 1)
                    src = state[:, one(zero_or_state(i)), :] if c == 0 else state[:, 1:2, :]
                    lo(St[c][1][:, :], src.rearrange("p o n -> p (o n)"), St[c][0][:, :]).then_inc(s["state_lo"], 1)

                def add_delta(c, i):
                    dve.wait_ge(s["delta_ready"], 2 * i + c + 1)
                    src = state[:, one(zero_or_state(i)), :] if c == 0 else state[:, 1:2, :]
                    dve.wait_ge(s["state_lo"], 2 * i + c + 1)
                    v.tensor_tensor(state[:, 1, :], M[c][:, :], src.rearrange("p o n -> p (o n)"),
                                    ALU.add).then_inc(s["state_add"], 1)

                def next_units(i):
                    for u in range(LAG):
                        unit(i, u, off(i))

                def h_part(i, last):
                    first = isinstance(i, int) and i == 0
                    for u in range(LAG, HU):
                        unit(i, u, off(i))
                        if u == 9 and not first:
                            lo_T(n2T, M, "n2T_hi", "n2T_lo", 2 * (i - 1))
                        if not first and u in (3, 5):
                            e_step(i - 1, 4 if u == 3 else 5)
                        if u == 6:
                            residual(i)
                        if first and u in (8, 9):
                            lo_weights(("fm", u - 7), u - 4)
                        if u == 10:
                            for f in range(KD):
                                dve.wait_ge(s["k_hi"], 2 * i + f + 1)
                                lo(KT[1][:, f, :], KT32[:, f, :], KT[0][:, f, :]).then_inc(s["k_lo"], 1)
                        if u == 13:
                            for h in range(2):
                                dve.wait_ge(s["ktok_hi"], 2 * i + h + 1)
                                lo(Ktok[1][:, 2 * h:2 * h + 2, :], tok2(M[h]),
                                   Ktok[0][:, 2 * h:2 * h + 2, :]).then_inc(s["ktok_lo"], 1)
                        if not last and u in (9, 11, 12, 14):
                            a_step(i + 1, (9, 11, 12, 14).index(u))

                def QT_lo(i, f):
                    dve.wait_ge(s["q_hi"], 2 * i + f + 1)
                    v.scalar_tensor_tensor(out=QT[1][:, f, :], in0=B[f][:, :], scalar=col("h1_b2", f),
                                           in1=QT[0][:, f, :].bitcast(F32), op0=ALU.add,
                                           op1=ALU.subtract).then_inc(s["q_lo"], 1)

                def attention(i, last):
                    if isinstance(i, int) and i == 0:
                        QT_lo(i, 0)
                    QT_lo(i, 1)
                    add_delta(0, i)
                    state_lo(1, i)
                    add_delta(1, i)
                    for c in range(CHUNKS):
                        dve.wait_ge(s["s_ps"], 2 * i + c + 1)
                        dst = S32[:, c, :].rearrange("p (a b) -> p a b", b=P)
                        src = A[c][:, 0:384].rearrange("p (a b) -> p a b", b=P)
                        v.tensor_tensor(dst[:, 0:3:2, :], src[:, 0:3:2, :],
                                        tri[:, :].unsqueeze(1).to_broadcast([P, 2, P]),
                                        ALU.mult).then_inc(s["s_masked"], 1)
                        v.tensor_copy(dst[:, 1, :], src[:, 1, :]).then_inc(s["s_masked"], 1)
                    for c in range(CHUNKS):
                        dve.wait_ge(s["s_hi"], 2 * i + c + 1)
                        lo(SP_[1][:, c, :], S32[:, c, :], SP_[0][:, c, :]).then_inc(s["s_lo"], 1)
                    if not last:
                        state_lo(0, i + 1)
                        nT_lo(i + 1)

                def x2_out(i, units):
                    r = resid_of(i)
                    dve.wait_ge(s["resid_set"], i + 1)
                    for h in range(2):
                        if h == 0:
                            dve.wait_ge(s["f_ready"], i + 1)
                        else:
                            dve.wait_ge(s["down_done"], units)
                        v.tensor_tensor(r[:, 2 * h:2 * h + 2, :], tok2(B[h]), r[:, 2 * h:2 * h + 2, :],
                                        ALU.add).then_inc(s["x2_ready"], 1)

                def fm_units(i, lo_, hi_, base, e_block=None):
                    for v_ in range(lo_, hi_):
                        if base == HU and v_ == LAG - 1:
                            QT_lo(i, 0)
                        unit(i, base + v_, 1)
                        if e_block is not None and v_ > LAG:
                            e_step(e_block, v_ - LAG - 1)

                def x2_stats(b, q):
                    dve.wait_ge(at_parity(q, "m_ldx_even", "m_ldx_odd"), 16 * half_count(b, q))
                    v.tensor_copy(touch[:, 0:4], ident[:, 0:4])
                    for t in range(TILES):
                        v.bn_stats(stats2[:, t, :], x2_of(b)[:, t, :]).then_inc(m["m_stats"], 1)

                def x2_normalise(b):
                    dve.wait_ge(m["m_rstd"], 10 * (b + 1))
                    if not is_first(b):
                        dve.wait_ge(m["m_T_ps"], 2 * b)
                    for t in range(TILES):
                        v.tensor_scalar(xn[:, t, :], x2_of(b)[:, t, :], lnw2[:, 0, t:t + 1], lnw2[:, 1, t:t + 1],
                                        ALU.subtract, ALU.mult).then_inc(m["m_norm"], 1)

                def XT_lo(b, q, k):
                    dve.wait_ge(m["m_T_hi"], 2 * b + k + 1)
                    lo(XT[q][1][:, k, :], routing_bank(b, k)[:, :], XT[q][0][:, k, :]).then_inc(m["m_T_lo"], 1)

                def r_step(b, k):
                    dve.wait_ge(m["m_r"], ROUTE * b + k)

                R = [rt[:, j, :, :] for j in range(11)]

                def softplus_start(b):
                    lg = routing_bank(b, 0)[:, 0:TILES * 2 * EXPERTS].rearrange("p (t e) -> p t e", t=TILES)
                    r = m["m_r"]
                    dve.wait_ge(m["m_lg_ps"], b + 1)
                    v.tensor_tensor(R[0], lg[:, :, EXPERTS:2 * EXPERTS],
                                    ebB[:, :].unsqueeze(1).to_broadcast([P, TILES, EXPERTS]), ALU.add).then_inc(r, 1)
                    r_step(b, 1)
                    v.tensor_tensor(R[1], lg[:, :, 0:EXPERTS], R[0], ALU.add).then_inc(r, 1)
                    r_step(b, 2)
                    v.tensor_scalar(R[0], R[1], -1.0, None, ALU.mult).then_inc(r, 1)
                    r_step(b, 3)
                    v.tensor_tensor(R[2], R[1], R[0], ALU.max).then_inc(r, 1)
                    dve.wait_ge(m["m_exp"], b + 1)
                    v.tensor_scalar(R[4], R[3], 1.0, None, ALU.add).then_inc(r, 1)

                def softplus_end(b):
                    r = m["m_r"]
                    r_step(b, 5)
                    v.tensor_scalar(R[0], R[4], -1.0, None, ALU.add).then_inc(r, 1)
                    r_step(b, 6)
                    v.tensor_scalar(R[7], R[0], 1e-30, None, ALU.max).then_inc(r, 1)
                    r_step(b, 7)
                    v.reciprocal(R[9], R[7]).then_inc(r, 1)
                    v.scalar_tensor_tensor(out=R[0], in0=R[0], scalar=0.0, in1=R[3], op0=ALU.is_equal,
                                           op1=ALU.mult).then_inc(r, 1)
                    r_step(b, 9)
                    v.tensor_tensor(R[9], R[9], R[3], ALU.mult).then_inc(r, 1)
                    v.scalar_tensor_tensor(out=R[0], in0=R[1], scalar=0.0, in1=R[0], op0=ALU.max,
                                           op1=ALU.add).then_inc(r, 1)
                    r_step(b, 11)
                    dve.wait_ge(m["m_ln"], b + 1)
                    v.tensor_tensor(R[6], R[5], R[9], ALU.mult).then_inc(r, 1)
                    r_step(b, 12)
                    v.tensor_tensor(R[6], R[6], R[0], ALU.add).then_inc(r, 1)

                def select(b):
                    r = m["m_r"]
                    v.tensor_copy(touch[:, 0:4], R[1][:, :, 0])
                    for t in range(TILES):
                        mx = v.max(top8[:, t, :], R[1][:, t, :])
                    mx.then_inc(r, 1)
                    r_step(b, 14)
                    v.tensor_copy(touch[:, 4:8], top8[:, :, 0])
                    for t in range(TILES):
                        mx = v.max_index(topi[:, t, :], top8[:, t, :], R[1][:, t, :])
                    mx.then_inc(r, 1)
                    r_step(b, 15)
                    v.tensor_copy(topf[:, :, 0:2], topi[:, :, 0:2]).then_inc(r, 1)
                    r_step(b, 16)
                    io = iota[:, :].unsqueeze(1).to_broadcast([P, TILES, EXPERTS])
                    v.tensor_tensor(R[10], io, topf[:, :, 0:1].to_broadcast([P, TILES, EXPERTS]), ALU.is_equal)
                    v.tensor_tensor(R[2], io, topf[:, :, 1:2].to_broadcast([P, TILES, EXPERTS]),
                                    ALU.is_equal).then_inc(r, 1)
                    r_step(b, 17)
                    v.tensor_tensor(R[10], R[10], R[2], ALU.add).then_inc(r, 1)

                def combine(b):
                    dve.wait_ge(m["m_act"], b + 1)
                    r_step(b, ROUTE)
                    v.tensor_tensor(R[7], R[10], R[8], ALU.mult).then_inc(m["m_cf"], 1)
                    dve.wait_ge(m["m_cf"], 2 * b + 1)
                    if not is_first(b):
                        dve.wait_ge(m["m_cfT_ps"], b)
                    v.tensor_copy(cfh[:, :, :], R[7]).then_inc(m["m_cf"], 1)
                    dve.wait_ge(m["m_cf"], 2 * b + 2)
                    for r in (0, BIAS_LO):
                        v.tensor_copy(cfx[:, :, r:r + EXPERTS], cfh[:, :, :].bitcast(F32))
                        last = lo(cfx[:, :, r + EXPERTS:r + 2 * EXPERTS], R[7], cfh[:, :, :])
                    last.then_inc(m["m_cfx"], 1)

                def output(b, q):
                    if not is_first(b):
                        dve.wait_ge(at_parity(q, "m_out_even", "m_out_odd"), 16 * half_count(b, q))
                    for h in range(2):
                        dve.wait_ge(m["m_y"], 2 * b + h + 1)
                        v.tensor_tensor(y[q][:, 2 * h:2 * h + 2, :], tok2(Y[h]), x2_of(b)[:, 2 * h:2 * h + 2, :],
                                        ALU.add).then_inc(m["m_yout"], 1)

                v.memset(touch1[:, :], 0.0).then_inc(s["x2_ready"], 2)
                a_step(0, 0)
                aggregate(s["a_stats"], TILES)
                a_step(0, 1)
                a_step(0, 2)
                aggregate(s["a_stats"], 2 * TILES)
                dve.wait_ge(s["const_pool"], 3)
                state_lo(0, 0)
                a_step(0, 3)
                scale_shift(n32, s["ld_const"], 16 * 2, s["a_norm"], 2 * TILES, s["a_out"], 0)
                lo_weights(("h2", 1), 0)
                nT_lo(0)
                lo_weights(("h2", 2), 1)
                dve.wait_ge(s["cols_out"], 1)
                for u in range(LAG):
                    unit(0, u, off(0))
                lo_weights(("h1", 1), 2)
                lo_weights(("h1", 2), 3)
                h_part(0, False)
                attention(0, False)
                for u in range(LAG):
                    unit(1, u, off(1))
                    for step in ((0,), (1, 2), (3,))[u]:
                        e_step(0, step)
                with dve.Fori(1, NBLK - 1) as i:
                    h_part(i, False)
                    fm_units(i, 0, LAG, HU)
                    attention(i, False)
                    fm_units(i, LAG, NH, HU, i)
                    next_units(i + 1)
                    x2_out(i - 1, unit_base(i + 1))
                last = NBLK - 1
                h_part(last, True)
                fm_units(last, 0, LAG, HU)
                attention(last, True)
                for v_ in range(LAG, NH):
                    unit(last, HU + v_, 1)
                    for step in ((0,), (1,), (2, 3), (4,), (5,))[v_ - LAG]:
                        e_step(last, step)
                        if step == 0:
                            aggregate(s["e_stats"], 8 * last + TILES)
                        if step == 4:
                            aggregate(s["e_stats"], 8 * last + 2 * TILES)
                    if v_ == LAG + 3:
                        x2_stats(0, 0)
                scale_shift(work, s["ld_const"], 16 * 2, s["e_norm"], 2 * TILES * NBLK, s["e_out"], 2 * last)
                lo_T(n2T, M, "n2T_hi", "n2T_lo", 2 * last)
                dve.wait_ge(m["m_whi"], 1)
                lo(rw[:, :, EXPERTS:2 * EXPERTS], routing_cols, rw[:, :, 0:EXPERTS]).then_inc(m["m_wlo"], 1)
                x2_normalise(0)
                x2_out(last - 1, unit_base(NBLK))
                dve.wait_ge(m["m_whi"], 4)
                lo(eW1[1][:, :, :, :].rearrange("p k e h -> p (k e h)"), e1_32[:, :, :, :].rearrange("p k e h -> p (k e h)"),
                   eW1[0][:, :, :, :].rearrange("p k e h -> p (k e h)")).then_inc(m["m_wlo"], 1)
                fm_units(NBLK, 0, 2, 0)
                for k in range(KD):
                    XT_lo(0, 0, k)
                fm_units(NBLK, 2, 3, 0)
                softplus_start(0)
                x2_stats(1, 1)
                fm_units(NBLK, 3, 4, 0)
                softplus_end(0)
                select(0)
                fm_units(NBLK, 4, 5, 0)
                lo(eW2[1][:, :, :], e2_32[:, :, :], eW2[0][:, :, :]).then_inc(m["m_wlo"], 1)
                low = slice(BIAS_LO, 2 * BIAS_LO)
                lo(biasR[low, :], bias32[low, :], biasR[low, :]).then_inc(m["m_wlo"], 1)
                fm_units(NBLK, 5, 6, 0)
                x2_normalise(1)
                fm_units(NBLK, 6, 7, 0)
                dve.wait_ge(m["m_pool"], 16)
                combine(0)
                fm_units(NBLK, 7, NH, 0)
                XT_lo(1, 1, 0)

                def turn(b, q, ahead):
                    late = int(is_first(b))
                    if is_first(b):
                        x2_out(NBLK - 1, unit_base(NBLK) + NH)
                    for u in range(UNITS):
                        U = UNITS * b + u
                        slot, two = u % 3, (q + u) % 2
                        if u < EXPERTS:
                            dve.wait_ge(m["m_silu"], U + 1)
                            dve.wait_ge(m["m_cfb"], EXPERTS * b + u + 1)
                            v.tensor_tensor(h32[:, two, :], CB[u % 2][:, :], s32[:, two, :],
                                            ALU.mult).then_inc(m["m_mult"], 1)
                        if not is_first(b) and u == LAG - 1:
                            output(b - 1, 1 - q)
                        if ahead >= 1 and u == 6:
                            combine(b + 1)
                        dve.wait_ge(m["m_hhi"], U + 1)
                        lo(H[1][:, slot, :], (h32 if u < EXPERTS else s32)[:, two, :],
                           H[0][:, slot, :]).then_inc(m["m_split"], 1)
                        if ahead >= 1:
                            if u in (0, 1) and not (is_first(b) and u == 1):
                                XT_lo(b + 1, 1 - q, u + late)
                            if u - late == 2:
                                softplus_start(b + 1)
                            if u - late == 3:
                                softplus_end(b + 1)
                            if u - late == 4:
                                select(b + 1)
                        if ahead >= 2:
                            if u == 5:
                                x2_stats(b + 2, q)
                            if u == 7:
                                x2_normalise(b + 2)

                pairs(dve, turn)
                output(NBLK - 1, 1)

            @block.tensor
            def _(pe):
                t_ = nc.tensor

                def up(i, u, j, ht, src):
                    U = unit_base(i) + u
                    first = isinstance(i, int) and i == 0
                    if not (first and u < 2):
                        pe.wait_ge(s["gelu_done"], U - 1)
                    b = upB[u % 2]
                    w = W2[MLP[j], 1]
                    for k in range(KD):
                        last = mm3(b[:, :], w, src, (slice(None), k, slice(ht * P, ht * P + P)),
                                   (slice(None), k, slice(None)), start=(k == 0), stop=(k == KD - 1))
                    last.then_inc(s["up_ready"], 1)

                def down_rows(i, u, ht, slot_off):
                    pe.wait_ge(s["split_ready"], unit_base(i) + u + 1)
                    slot = (slot_off + u) % 3
                    for t in range(TILES):
                        last = mm3(tok2(B[t // 2])[:, t % 2, :], G, W2["fm", 2],
                                   (slice(None), slot, slice(t * P, t * P + P)), (slice(None), ht, slice(None)),
                                   start=(ht == 0 and t % 2 == 0), stop=(ht == NH - 1))
                        if ht == NH - 1 and t % 2 == 1 and t < TILES - 1:
                            last.then_inc(s["f_ready"], 1)
                    return last

                def transposes(src_tile, banks, ps):
                    for k in range(KD):
                        for t in range(TILES):
                            last = t_.transpose(banks[k][:, t * P:(t + 1) * P], src_tile[:, t, k * P:(k + 1) * P],
                                                ident[:, :])
                        last.then_inc(s[ps], 1)

                def T_nT(i):
                    pe.wait_ge(s["a_out"], 2 * i + 2)
                    if not (isinstance(i, int) and i == 0):
                        pe.wait_ge(s["s_masked"], 4 * i)
                    transposes(n32, A, "nT_ps")

                def T_n2T(i):
                    pe.wait_ge(s["e_out"], 2 * i + 2)
                    transposes(work, M, "n2T_ps")

                def down_h(i, u, o):
                    j = u // NH
                    ht = u % NH
                    acc, ready = ((A, "k_ready"), (B, "q_ready"))[j]
                    if ht == 0 and not (isinstance(i, int) and i == 0):
                        if j == 0:
                            pe.wait_ge(s["t_gelu"], 2 * i)
                        else:
                            pe.wait_ge(s["x2_ready"], 2 * i)
                    pe.wait_ge(s["split_ready"], unit_base(i) + u + 1)
                    slot = (o + u) % 3
                    w = W2[MLP[j], 2]
                    for f in range(KD):
                        ws = (slice(None), ht, slice(f * P, f * P + P))
                        vs = (slice(None), slot, slice(None))
                        last = mm3(acc[f][:, :], w, G, ws, vs, start=(ht == 0), stop=(ht == NH - 1))
                        if ht == NH - 1 and f == 0:
                            last.then_inc(s[ready], 1)
                    last.then_inc(s["down_done"], 1)

                def down(i, u):
                    if u < HU:
                        down_h(i, u, off(i))
                        return
                    if u == HU:
                        pe.wait_ge(s["q_lo"], 2 * i + 2)
                    down_rows(i, u, u - HU, 1).then_inc(s["down_done"], 1)

                def next_units(i, has_fm):
                    pe.wait_ge(s["nT_lo"], 2 * (i + 1))
                    for u in range(LAG):
                        up(i, u, 0, u, nT)
                        if has_fm:
                            down(i - 1, FU - LAG + u)

                def h_part(i):
                    first = isinstance(i, int) and i == 0
                    for u in range(LAG, HU):
                        if first and u in (3, 8, 11):
                            pe.wait_ge(s["w_lo"], {3: 2, 8: 3, 11: 4}[u])
                        up(i, u, u // NH, u % NH, nT)
                        down(i, u - LAG)
                        if u == 9 and not first:
                            T_n2T(i - 1)
                        if u == 13:
                            pe.wait_ge(s["k_f32"], 2 * i + 2)
                            if not first:
                                pe.wait_ge(s["n2T_lo"], 2 * i)
                            for h in range(2):
                                for t in (2 * h, 2 * h + 1):
                                    for k in range(KD):
                                        lt = t_.transpose(tok2(M[h])[:, t % 2, k * P:(k + 1) * P],
                                                          KT32[:, k, t * P:(t + 1) * P], ident[:, :])
                                lt.then_inc(s["ktok_ps"], 1)

                def attention(i, last):
                    pe.wait_ge(s["ktok_lo"], 2 * i + 2)
                    pe.wait_ge(s["ntok_lo"], i + 1)
                    for c in range(CHUNKS):
                        for fh in range(KD):
                            for t in (2 * c, 2 * c + 1):
                                lt = mm3(M[c][:, fh * D:(fh + 1) * D], Ktok, ntok,
                                         (slice(None), t, slice(fh * P, (fh + 1) * P)), (slice(None), t, slice(None)),
                                         start=(fh == 0 and t == 2 * c), stop=(t == 2 * c + 1))
                        lt.then_inc(s["delta_ready"], 1)
                    pe.wait_ge(s["k_lo"], 2 * i + 2)
                    for k in range(KD):
                        pe.wait_ge(s["q_lo"], 2 * i + k + 1)
                        for c in range(CHUNKS):
                            for n, (key, zn, c0) in enumerate(((2 * c, 2, 0), (2 * c + 1, 1, 2 * P))):
                                lt = mm3(A[c][:, c0:c0 + zn * P], KT, QT,
                                         (slice(None), k, slice(key * P, key * P + P)),
                                         (slice(None), k, slice(key * P, (key + zn) * P)),
                                         start=(n == 0 and k == 0), stop=(k == KD - 1))
                            if k == KD - 1:
                                lt.then_inc(s["s_ps"], 1)
                    for c in range(CHUNKS):
                        pe.wait_ge(s["state_lo"], 2 * i + c + 1)
                        pe.wait_ge(s["state_add"], 2 * i + c + 1)
                        for zz in range(2):
                            for k in range(KD):
                                lt = mm3(tok2(M[c])[:, zz, :], QT, St[c],
                                         (slice(None), k, slice((2 * c + zz) * P, (2 * c + zz + 1) * P)),
                                         (slice(None), slice(k * D, (k + 1) * D)), start=(zz == 0 and k == 0))
                        lt.then_inc(s["qs_done"], 1)
                    for c in range(CHUNKS):
                        pe.wait_ge(s["s_lo"], 2 * i + c + 1)
                        for zz, at_, key in ((0, 0, 0), (1, P, 0), (1, 2 * P, 1)):
                            lt = mm3(tok2(M[c])[:, zz, :], SP_, ntok, (slice(None), c, slice(at_, at_ + P)),
                                     (slice(None), 2 * c + key, slice(None)), stop=(zz == key))
                        lt.then_inc(s["t_ready"], 1)
                    if not last:
                        T_nT(i + 1)

                def fm_units(i, lo_, hi_):
                    if lo_ == 0:
                        pe.wait_ge(s["n2T_lo"], 2 * i)
                    for v_ in range(lo_, hi_):
                        up(i, HU + v_, 2, v_, n2T)
                        down(i, HU + v_ - LAG)

                def T_X(b, k):
                    if k == 0:
                        pe.wait_ge(m["m_norm"], TILES * (b + 1))
                        if is_first(b):
                            pe.wait_ge(s["s_masked"], 4 * NBLK)
                        elif not (isinstance(b, int) and b == 1):
                            pe.wait_ge(m["m_cfT"], b)
                    elif not is_first(b):
                        pe.wait_ge(m["m_T_lo"], 2 * b + 1)
                    for t in range(TILES):
                        last = nc.tensor.transpose(routing_bank(b, k)[:, t * P:(t + 1) * P], xn[:, t, k * P:(k + 1) * P],
                                                   ident[:, :])
                    last.then_inc(m["m_T_ps"], 1)

                def logits(b, q):
                    pe.wait_ge(m["m_T_lo"], 2 * (b + 1))
                    E2 = 2 * EXPERTS
                    for t in range(TILES):
                        for k in range(KD):
                            for part in (1, 0):
                                last = mm(routing_bank(b, 0)[:, t * E2:(t + 1) * E2], XT[q][part][:, k, t * P:(t + 1) * P],
                                          rw[:, k, :], start=(t == 0 and k == 0 and part == 1),
                                          stop=(k == KD - 1 and part == 0))
                    last.then_inc(m["m_lg_ps"], 1)

                def T_cf(b):
                    pe.wait_ge(m["m_cfx"], b + 1)
                    for t in range(TILES):
                        last = nc.tensor.transpose(routing_bank(b, 1)[:, t * P:(t + 1) * P], cfx[:, t, :], ident[:, :])
                    last.then_inc(m["m_cfT_ps"], 1)

                def expert_up(b, q, u):
                    U = UNITS * b + u
                    if not (is_first(b) and u < 3):
                        pe.wait_ge(m["m_hhi"], U - 2)
                    elif u < 2:
                        pe.wait_ge(s["gelu_done"], unit_base(NBLK) + NH - 1 + u)
                    for k in range(KD):
                        last = mm3(up3[u % 3][:, :], eW1, XT[q], (slice(None), k, u, slice(None)),
                                   (slice(None), k, slice(None)), start=(k == 0), stop=(k == KD - 1))
                    last.then_inc(m["m_up"], 1)

                def spread(b, q, u):
                    if u == 0:
                        pe.wait_ge(m["m_cfT"], b + 1)
                    if not (is_first(b) and u < 2):
                        pe.wait_ge(m["m_mult"], EXPERTS * b + u - 1)
                    elif u == 1:
                        pe.wait_ge(s["x2_ready"], 2 * NBLK + 1)
                    mm(CB[u % 2][:, :], sel[:, u, :], cfT[q][:, :], start=True, stop=True).then_inc(m["m_cfb"], 1)

                def expert_down(b, u):
                    pe.wait_ge(m["m_split"], UNITS * b + u + 1)
                    for t in range(TILES):
                        if u == 0 and t % 2 == 0 and not is_first(b):
                            pe.wait_ge(m["m_yout"], 2 * b - 1 + t // 2)
                        elif u == 0 and t == 0:
                            pe.wait_ge(m["m_wlo"], 4)
                            pe.wait_ge(s["x2_ready"], 2 * NBLK + 2)
                        last = mm3(tok2(Y[t // 2])[:, t % 2, :], H, eW2, (slice(None), u % 3, slice(t * P, t * P + P)),
                                   (slice(None), u, slice(None)), start=(u == 0 and t % 2 == 0))
                    last.then_inc(m["m_down"], 1)

                def biases(b, q):
                    rows = slice(0, 2 * BIAS_LO)
                    for t in range(TILES):
                        last = mm(tok2(Y[t // 2])[:, t % 2, :], cfT[q][rows, t * P:(t + 1) * P], biasR[rows, :],
                                  stop=True)
                        if t % 2 == 1:
                            last.then_inc(m["m_y"], 1)

                pe.wait_ge(s["const_pool"], 3)
                pe.wait_ge(s["ld_rows"], 16 * 9)
                t_.transpose(B[0][:, 0:NROWS], brows[0:NROWS, :], ident[0:NROWS, 0:NROWS]).then_inc(s["cols_ps"], 1)
                T_nT(0)
                pe.wait_ge(s["w_lo"], 1)
                next_units(0, False)
                h_part(0)
                for u in range(HU - LAG, HU):
                    down(0, u)
                attention(0, False)
                pe.wait_ge(s["w_lo"], 6)
                next_units(1, False)
                with pe.Fori(1, NBLK - 1) as i:
                    h_part(i)
                    fm_units(i, 0, LAG)
                    attention(i, False)
                    fm_units(i, LAG, NH)
                    next_units(i + 1, True)
                last = NBLK - 1
                h_part(last)
                fm_units(last, 0, LAG)
                attention(last, True)
                fm_units(last, LAG, NH)
                for u in range(FU - LAG, FU):
                    down(last, u)
                T_n2T(last)
                pe.wait_ge(s["n2T_lo"], 2 * NBLK)
                for v_ in range(NH + LAG):
                    if v_ < NH:
                        up(NBLK, v_, 2, v_, n2T)
                    else:
                        if v_ == NH:
                            pe.wait_ge(m["m_wlo"], 2)
                        expert_up(0, 0, v_ - NH)
                    if v_ == LAG:
                        pe.wait_ge(m["m_wlo"], 1)
                        logits(0, 0)
                    if v_ >= LAG:
                        if v_ == LAG:
                            pe.wait_ge(s["x2_ready"], 2 * NBLK)
                        down_rows(NBLK, v_ - LAG, v_ - LAG, 1).then_inc(s["down_done"], 1)
                    if v_ == 1:
                        T_X(0, 0)
                        T_X(0, 1)
                    if v_ == NH + 1:
                        T_cf(0)
                        T_X(1, 0)
                spread(0, 0, 0)

                def turn(b, q, ahead):
                    first = is_first(b)
                    late = int(first)
                    for u in range(UNITS):
                        lead_in = first and u < LAG
                        if not lead_in:
                            expert_up(b, q, u)
                        if u == 0 and not first:
                            expert_down(b - 1, LAST)
                            spread(b, q, 0)
                        elif u > 0:
                            if u < EXPERTS:
                                spread(b, q, u)
                            if u >= LAG:
                                expert_down(b, u - LAG)
                            elif not first:
                                expert_down(b - 1, LAST + u)
                                if u == LAG - 1:
                                    biases(b - 1, 1 - q)
                        if ahead >= 1:
                            if u in ((1,) if first else (0, 1)):
                                T_X(b + 1, u)
                            if u - late == 2:
                                logits(b + 1, 1 - q)
                            if u == UNITS - 1:
                                T_cf(b + 1)

                pairs(pe, turn)
                for u in range(LAST, UNITS):
                    expert_down(NBLK - 1, u)
                biases(NBLK - 1, 1)


_INS = ["L0_attn_x", "L0_attn_ln_g", "L0_attn_ln_b", "L0_attn_h1_w1", "L0_attn_h1_b1", "L0_attn_h1_w2",
        "L0_attn_h1_b2", "L0_attn_h2_w1", "L0_attn_h2_b1", "L0_attn_h2_w2", "L0_attn_h2_b2", "L0_attn_fm_w1",
        "L0_attn_fm_b1", "L0_attn_fm_w2", "L0_attn_fm_b2", "L0_ffn_routing_W", "L0_ffn_expert_bias",
        "L0_ffn_sW1", "L0_ffn_sb1", "L0_ffn_sW2", "L0_ffn_sb2", "L0_ffn_rW1", "L0_ffn_rb1", "L0_ffn_rW2",
        "L0_ffn_rb2"]
_OUTS = [((4, 2048, 256), "float32")]


def kernel(**inputs):
    import numpy as _np
    import concourse.bacc as _bacc
    from concourse import mybir as _mybir
    from concourse.bass_utils import run_bass_kernel_spmd as _run

    nc = _bacc.Bacc("TRN2", target_bir_lowering=False, num_devices=1)
    arrays, args = {}, []
    for name in _INS:
        a = _np.ascontiguousarray(inputs[name])
        arrays[f"in_{name}_dram"] = a
        args.append(nc.dram_tensor(f"in_{name}_dram", a.shape, _mybir.dt.from_np(a.dtype), kind="ExternalInput").ap())
    for i, (shape, dtype) in enumerate(_OUTS):
        dt = _mybir.dt.from_np(_np.dtype(dtype))
        args.append(nc.dram_tensor(f"out_{i}_dram", shape, dt, kind="ExternalOutput").ap())
    bass_preln_layer(nc, *args)
    r = _run(nc, [arrays], core_ids=[0])
    return r.results[0]["out_0_dram"]
```

```python
from contextlib import ExitStack

import concourse.bass as bass
from concourse import mybir

F32 = mybir.dt.float32
F32R = mybir.dt.float32r
U32 = mybir.dt.uint32
ALU = mybir.AluOpType
ACT = mybir.ActivationFunctionType

P = 128
TOKENS_PER_BLOCK = 512
TILES = TOKENS_PER_BLOCK // P
CHUNK_TILES = 2
CHUNKS = TILES // CHUNK_TILES
EPS = 1e-5


def bass_preln_layer(nc, x, ln_g, ln_b, h1_w1, h1_b1, h1_w2, h1_b2, h2_w1, h2_b1, h2_w2, h2_b2,
                     fm_w1, fm_b1, fm_w2, fm_b2, routing_W, expert_bias, sW1, sb1, sW2, sb2,
                     rW1, rb1, rW2, rb2, out):
    batches, seq, D = x.shape
    DI = h1_w1.shape[1]
    NBLK = batches * seq // TOKENS_PER_BLOCK
    BLOCKS_PER_BATCH = seq // TOKENS_PER_BLOCK
    KD = D // P
    NH = DI // P
    EXPERTS = routing_W.shape[0]
    UNITS = EXPERTS + 1
    assert D == 256 and NH == 8 and EXPERTS == 8 and rW1.shape[2] == P and BLOCKS_PER_BATCH == 4
    T4 = TOKENS_PER_BLOCK

    x_tok = x.rearrange("b s d -> (b s) d").rearrange("(n p) d -> p n d", p=P)
    out_tok = out.rearrange("b s d -> (b s) d").rearrange("(n p) d -> p n d", p=P)
    x2_dram = nc.dram_tensor("x2_between_phases", (P, NBLK * TILES, D), F32, kind="Internal").ap()

    KB = 1024
    base = ((nc.sbuf_base + 31) // 32) * 32

    class Region:
        def __init__(self, at):
            self.at = at

        def put(self, name, shape, dt=F32):
            t = nc.alloc_sbuf_tensor_at(name, shape, dt, offset=self.at)
            n = 4
            for s in shape[1:]:
                n *= s
            self.at += (n + 31) // 32 * 32
            assert self.at <= nc.sbuf_usable_end, (name, self.at)
            return t

    with ExitStack() as ctx:
        def sem(name):
            return ctx.enter_context(nc.semaphore(name))

        common = Region(base)
        ident = common.put("ident", [P, P])
        consts = common.put("consts", [P, 6, TILES])
        C_HALF, C_QUARTER, C_INVN, C_EPS, C_NEGHALF = (consts[:, j, :] for j in range(5))
        stats = common.put("stats", [P, TILES, 6])
        lnw = common.put("lnw", [P, 8, TILES])
        touch1 = common.put("touch1", [P, TILES])
        ROW = dict(h2_b1=0, h1_b1=NH, fm_b1=2 * NH, h2_b2=3 * NH, h1_b2=3 * NH + KD, rb1=3 * NH + 2 * KD)
        ROW["sb1"] = ROW["rb1"] + EXPERTS
        ROW["routing"] = ROW["sb1"] + 1
        NROWS = ROW["routing"] + KD * EXPERTS
        cols = common.put("cols", [P, NROWS])

        def col(name, k=0):
            return cols[:, ROW[name] + k:ROW[name] + k + 1]

        phase_base = common.at

        r1 = Region(phase_base)
        W = {}
        for mlp in ("h2", "h1", "fm"):
            for part in ("hi", "lo"):
                W[mlp, 1, part] = r1.put(f"{mlp}_w1_{part}", [P, KD, DI], F32R)
            for part in ("hi", "lo"):
                W[mlp, 2, part] = r1.put(f"{mlp}_w2_{part}", [P, NH, D], F32R)
        nT_at = r1.at
        nT = [r1.put(f"nT_{p_}", [P, KD, T4], F32R) for p_ in ("hi", "lo")]
        qreg = Region(nT_at)
        QT = [qreg.put(f"QT_{p_}", [P, KD, T4], F32R) for p_ in ("hi", "lo")]
        ntok = [r1.put(f"ntok_{p_}", [P, TILES, D], F32R) for p_ in ("hi", "lo")]
        KT = [r1.put(f"KT_{p_}", [P, KD, T4], F32R) for p_ in ("hi", "lo")]
        ktok_at = r1.at
        Ktok = [r1.put(f"Ktok_{p_}", [P, TILES, D], F32R) for p_ in ("hi", "lo")]
        n2T_at = r1.at
        n2T = [r1.put(f"n2T_{p_}", [P, KD, T4], F32R) for p_ in ("hi", "lo")]
        xin_at = r1.at
        xin = r1.put("xin", [P, TILES, D])
        xa = r1.put("xa", [P, 2, TILES, D])
        resid = r1.put("resid", [P, 2, TILES, D])
        n32 = r1.put("n32", [P, TILES, D])
        work_at = r1.at
        work = r1.put("work", [P, TILES, D])
        KT32 = Region(work_at).put("KT32", [P, KD, T4])
        G = [r1.put(f"G_{p_}", [P, 3, T4], F32R) for p_ in ("hi", "lo")]
        G32 = r1.put("G32", [P, 2, T4])
        S32 = r1.put("S32", [P, CHUNKS, 384])
        sp_at = r1.at
        SP_ = [r1.put(f"S_{p_}", [P, CHUNKS, 384], F32R) for p_ in ("hi", "lo")]
        state = r1.put("state", [P, 2, KD * D])
        St = [[r1.put(f"state{c}_{p_}", [P, KD * D], F32R) for p_ in ("hi", "lo")] for c in range(CHUNKS)]
        sp_end = r1.at
        tri = r1.put("tri", [P, P])
        gB = r1.put("gB", [P, D])
        bB = r1.put("bB", [P, D])
        fb2B = r1.put("fb2B", [P, D])
        brows = r1.put("brows", [P, P])
        stage_at = {}
        fm_at = phase_base + 2 * 4 * 8 * KB
        stage_at["h2", 1] = fm_at
        stage_at["h2", 2] = fm_at + 8 * KB
        stage_at["h1", 1] = fm_at + 16 * KB
        stage_at["h1", 2] = fm_at + 24 * KB
        stage_at["fm", 1] = n2T_at
        stage_at["fm", 2] = ktok_at
        stage = {}
        for (mlp, w), at in stage_at.items():
            shape = [P, KD, DI] if w == 1 else [P, NH, D]
            stage[mlp, w] = Region(at).put(f"{mlp}_w{w}_f32", shape)

        r2 = Region(phase_base)
        eW1 = [r2.put(f"eW1_{p_}", [P, KD, UNITS, P], F32R) for p_ in ("hi", "lo")]
        eW2 = [r2.put(f"eW2_{p_}", [P, UNITS, D], F32R) for p_ in ("hi", "lo")]
        e1_32 = r2.put("e1_32", [P, KD, UNITS, P])
        e2_32 = r2.put("e2_32", [P, UNITS, D])
        sel = r2.put("sel", [P, EXPERTS, P], F32R)
        bias32 = r2.put("bias32", [P, D])
        biasR = r2.put("biasR", [P, D], F32R)
        rw = r2.put("rw", [P, KD, 2 * EXPERTS], F32R)
        ebB = r2.put("ebB", [P, EXPERTS])
        iota = r2.put("iota", [P, EXPERTS])
        half8 = r2.put("half8", [P, TILES, EXPERTS])
        assert r2.at <= fm_at
        r3 = Region(fm_at)
        H = [r3.put(f"H_{p_}", [P, 3, T4], F32R) for p_ in ("hi", "lo")]
        s32 = r3.put("s32", [P, 2, T4])
        h32 = Region(xin_at).put("h32", [P, 2, T4])
        y = [r3.put(f"y_{q}", [P, TILES, D]) for q in range(2)]
        cfT1 = r3.put("cfT1", [P, T4], F32R)
        assert r3.at <= nT_at
        r4 = Region(nT_at)
        x2 = r4.put("x2", [P, 4, TILES, D])
        XT0 = [r4.put(f"XT0_{p_}", [P, KD, T4], F32R) for p_ in ("hi", "lo")]
        xn = r4.put("xn", [P, TILES, D])
        cfx = r4.put("cfx", [P, TILES, P])
        assert r4.at <= n2T_at
        r5 = Region(n2T_at)
        XT1 = [r5.put(f"XT1_{p_}", [P, KD, T4], F32R) for p_ in ("hi", "lo")]
        r6 = Region(sp_at)
        cfT0 = r6.put("cfT0", [P, T4], F32R)
        rt = r6.put("rt", [P, 11, TILES, EXPERTS])
        top8 = r6.put("top8", [P, TILES, 8])
        topi = r6.put("topi", [P, TILES, 8], U32)
        topf = r6.put("topf", [P, TILES, 8])
        cfh = r6.put("cfh", [P, TILES, EXPERTS], F32R)
        touch = r6.put("touch", [P, 8])
        stats2 = r6.put("stats2", [P, TILES, 6])
        lnw2 = r6.put("lnw2", [P, 8, TILES])
        assert r6.at <= sp_end
        XT = [XT0, XT1]
        cfT = [cfT0, cfT1]

        bank = [ctx.enter_context(nc.psum_tensor(f"bank{j}", [P, 512], F32)) for j in range(8)]
        upB, A, B, M = bank[0:2], bank[2:4], bank[4:6], bank[6:8]
        up3, CB, Y, M1 = bank[0:3], bank[3:5], bank[5:7], bank[7]

        def tok2(b):
            return b[:, :].rearrange("p (t d) -> p t d", t=2)

        names = """
            x_loaded rows_loaded norm_weights_loaded const_pool pool_chain cols_ps cols_out
            ld_h2w1 ld_h2w2 ld_h1w1 ld_h1w2 ld_fmw1 ld_fmw2 w_hi w_lo
            a_stats a_rstd a_norm a_out aggregated eps_added x_used resid_set
            nT_ps nT_hi nT_lo ntok_hi ntok_lo up_ready gelu_done split_ready down_done
            k_ready k_f32 k_hi k_lo ktok_ps ktok_hi ktok_lo q_ready q_hi q_lo
            delta_ready state_add state_hi state_lo qs_done s_ps s_masked s_hi s_lo t_ready t_gelu
            e_stats e_rstd e_norm e_mid e_out n2T_ps n2T_hi n2T_lo f_ready x2_ready fb2_st_x2""".split()
        s = {n: sem(n) for n in names}
        mixture_names = """
            weights_loaded consts_set weights_hi weights_lo x2_even_loaded x2_odd_loaded
            x2_stats x2_rstd x2_normed XT_ps XT_hi XT_lo logits_ps route_steps exp_done ln_done
            activation_done combine_steps cf_placed cfT_ps cfT_out spread_ps
            up_ps silu_done scaled hidden_hi hidden_lo down_done sum_ps y_formed
            y_even_stored y_odd_stored""".split()
        m = {n: sem("m_" + n) for n in mixture_names}

        def mm(o, lhsT, rhs, start=False, stop=False):
            return nc.tensor.matmul(o, lhsT, rhs, start=start, stop=stop, skip_group_check=True)

        def mm3(o, w, v, ws, vs, start=False, stop=False):
            mm(o, w[1][ws], v[0][vs], start=start)
            mm(o, w[0][ws], v[1][vs])
            return mm(o, w[0][ws], v[0][vs], stop=stop)

        HU = 2 * NH
        FU = 3 * NH

        def unit_base(i):
            return 0 if isinstance(i, int) and i == 0 else i * FU - NH

        def off(i):
            return 0 if isinstance(i, int) and i == 0 else 1

        MLP = ("h2", "h1", "fm")
        B1 = ("h2_b1", "h1_b1", "fm_b1")
        LAG = 3
        routing_cols = cols[:, ROW["routing"]:NROWS].rearrange("p (k e) -> p k e", k=KD)
        W2 = {(mlp, w): (W[mlp, w, "hi"], W[mlp, w, "lo"]) for mlp in MLP for w in (1, 2)}

        def zero_or_state(i):
            if isinstance(i, int):
                return 0 if i % BLOCKS_PER_BATCH == 0 else 1
            return (((i % BLOCKS_PER_BATCH) + 3) >> 2).with_bounds(min_val=0, max_val=1)

        def one(i):
            return bass.ds(i, 1) if not isinstance(i, int) else slice(i, i + 1)

        def par(i):
            return one(i % 2)

        BIAS_LO = 32
        ROUTE = 18
        LAST = UNITS - LAG

        def at_parity(q, even, odd):
            return m[odd] if q else m[even]

        def routing_bank(b, j):
            return A[j] if is_first(b) else M1

        def x2_of(b):
            slot = b % 4
            return x2[:, one(slot if isinstance(b, int) else slot.with_bounds(min_val=0, max_val=3)), :, :]\
                .rearrange("p o t d -> p (o t) d")

        def pairs(eng, body):
            body(0, 0, 2)
            with eng.Fori(0, NBLK // 2 - 2) as j:
                body(2 * j + 1, 1, 2)
                body(2 * j + 2, 0, 2)
            for b in range(NBLK - 3, NBLK):
                body(b, b % 2, min(2, NBLK - 1 - b))

        def is_first(b):
            return isinstance(b, int) and b == 0

        def half_count(b, q):
            return (b - q) // 2 + 1 if isinstance(b, int) else ((b - q) >> 1) + 1

        with nc.Block() as block:
            @block.sync
            def _(sp):
                def load(b, q):
                    sp.dma_start(x2_of(b), x2_dram[:, bass.ds(b * TILES, TILES), :])\
                      .then_inc(at_parity(q, "x2_even_loaded", "x2_odd_loaded"), 16)

                def store(b, q):
                    sp.wait_ge(m["y_formed"], 2 * (b + 1))
                    sp.wait_ge(m["weights_hi"], 1)
                    sp.dma_start(out_tok[:, bass.ds(b * TILES, TILES), :], y[q][:, :, :])\
                      .then_inc(at_parity(q, "y_even_stored", "y_odd_stored"), 16)

                def store_then_load(b, q):
                    store(b, q)
                    load(b + 3, 1 - q)

                sp.dma_start(xin[:, :, :], x_tok[:, 0:TILES, :]).then_inc(s["x_loaded"], 16)
                for name, src in (("h2_b1", h2_b1), ("h1_b1", h1_b1), ("fm_b1", fm_b1), ("h2_b2", h2_b2),
                                  ("h1_b2", h1_b2), ("sb1", sb1)):
                    rows = src.rearrange("(k p) -> k p", p=P)
                    sp.dma_start(brows[ROW[name]:ROW[name] + rows.shape[0], :], rows).then_inc(s["rows_loaded"], 16)
                sp.dma_start(brows[ROW["rb1"]:ROW["rb1"] + EXPERTS, :], rb1).then_inc(s["rows_loaded"], 16)
                for k in range(KD):
                    at = ROW["routing"] + k * EXPERTS
                    sp.dma_start(brows[at:at + EXPERTS, :], routing_W[:, k * P:(k + 1) * P]).then_inc(s["rows_loaded"], 16)
                sp.dma_start(fb2B[:, :], fm_b2.partition_broadcast(P)).then_inc(s["fb2_st_x2"], 16)
                w_dram = {("h2", 1): h2_w1, ("h2", 2): h2_w2, ("h1", 1): h1_w1, ("h1", 2): h1_w2,
                          ("fm", 1): fm_w1, ("fm", 2): fm_w2}
                for key in (("h2", 1), ("h2", 2), ("h1", 1), ("h1", 2), ("fm", 1), ("fm", 2)):
                    src = w_dram[key].rearrange("(k p) n -> p k n", p=P)
                    sp.dma_start(stage[key][:, :, :], src).then_inc(s[f"ld_{key[0]}w{key[1]}"], 16)

                def load_x(i):
                    sp.wait_ge(s["x_used"], i)
                    sp.wait_ge(s["x_used"], 1)
                    sp.dma_start(xin[:, :, :], x_tok[:, bass.ds(i * TILES, TILES), :]).then_inc(s["x_loaded"], 16)

                def store_x2(i):
                    sp.wait_ge(s["x2_ready"], 2 * (i + 1) + 2)
                    sp.wait_ge(s["x2_ready"], 1)
                    sp.dma_start(x2_dram[:, bass.ds(i * TILES, TILES), :],
                                 resid[:, par(i), :, :].rearrange("p o t d -> p (o t) d")).then_inc(s["fb2_st_x2"], 16)

                load_x(1)
                with sp.Fori(1, NBLK - 1) as i:
                    load_x(i + 1)
                    store_x2(i - 1)
                sp.wait_ge(s["down_done"], unit_base(NBLK - 1) + HU)
                for k in range(KD):
                    sp.dma_start(e1_32[:, k, 0:EXPERTS, :], rW1[:, k * P:(k + 1) * P, :].rearrange("e p h -> p e h"))\
                      .then_inc(m["weights_loaded"], 16)
                    sp.dma_start(e1_32[:, k, EXPERTS, :], sW1[k * P:(k + 1) * P, :]).then_inc(m["weights_loaded"], 16)
                sp.dma_start(e2_32[:, 0:EXPERTS, :], rW2.rearrange("e h d -> h e d")).then_inc(m["weights_loaded"], 16)
                sp.dma_start(e2_32[:, EXPERTS, :], sW2).then_inc(m["y_odd_stored"], 16)
                sp.dma_start(ebB[:, :], expert_bias.partition_broadcast(P)).then_inc(m["y_even_stored"], 16)
                sp.wait_ge(m["consts_set"], 1)
                for r in (0, BIAS_LO):
                    sp.dma_start(bias32[r:r + EXPERTS, :], rb2).then_inc(m["weights_loaded"], 16)
                    sp.dma_start(bias32[r + EXPERTS:r + 2 * EXPERTS, :], rb2).then_inc(m["weights_loaded"], 16)
                    sp.dma_start(bias32[r + 2 * EXPERTS:r + 2 * EXPERTS + 1, :], sb2.rearrange("(a d) -> a d", a=1))\
                      .then_inc(m["weights_loaded"], 16)
                sp.wait_ge(s["fb2_st_x2"], 16 * (NBLK - 1))
                sp.wait_ge(s["t_ready"], 2 * NBLK)
                load(0, 0)
                load(1, 1)
                store_x2(NBLK - 2)
                sp.wait_ge(m["x2_stats"], TILES)
                load(2, 0)
                store_x2(NBLK - 1)
                sp.wait_ge(s["fb2_st_x2"], 16 * (NBLK + 1))
                store_then_load(0, 0)
                with sp.Fori(0, (NBLK - 4) // 2) as j:
                    store_then_load(2 * j + 1, 1)
                    store_then_load(2 * j + 2, 0)
                for b in range(NBLK - 3, NBLK):
                    store(b, b % 2)
                sp.wait_ge(m["y_even_stored"], 16 * (NBLK // 2 + 1))
                sp.wait_ge(m["y_odd_stored"], 16 * (NBLK // 2 + 1))

            @block.gpsimd
            def _(pool):
                g = nc.gpsimd

                g.memset(ident[:, :], 0.0).then_inc(s["pool_chain"], 1)
                g.memset(tri[:, :], 1.0).then_inc(s["pool_chain"], 1)
                g.memset(state[:, 0, :], 0.0).then_inc(s["const_pool"], 1)
                for dst, val in ((C_HALF, 0.5), (C_QUARTER, 0.25), (C_INVN, 1.0 / D), (C_EPS, EPS), (C_NEGHALF, -0.5)):
                    g.memset(dst, val).then_inc(s["pool_chain"], 1)
                pool.wait_ge(s["pool_chain"], 7)
                g.affine_select(out=ident[:, :], in_=ident[:, :], compare_op=ALU.not_equal, fill=1.0,
                                base=0, pattern=[[-1, P]], channel_multiplier=1).then_inc(s["const_pool"], 1)
                g.affine_select(out=tri[:, :], in_=tri[:, :], compare_op=ALU.is_ge, fill=0.0,
                                base=0, pattern=[[1, P]], channel_multiplier=-1).then_inc(s["const_pool"], 1)
                for dst, src in ((gB, ln_g), (bB, ln_b)):
                    pool.dma_start(dst[:, :], src.partition_broadcast(P)).then_inc(s["norm_weights_loaded"], 16)

                def rstd(st, w, stat_sem, stat_count, done, done_before):
                    me, mo, v0, v1 = st[:, :, 1], st[:, :, 4], st[:, :, 2], st[:, :, 5]
                    w = [w[:, j, :] for j in range(8)]
                    pool.wait_ge(stat_sem, stat_count)
                    g.tensor_tensor(w[2], me, mo, ALU.add).then_inc(done, 1)
                    g.tensor_tensor(w[3], me, mo, ALU.subtract).then_inc(done, 1)
                    g.tensor_tensor(w[4], v0, v1, ALU.add).then_inc(done, 1)
                    k = 3
                    for o, a, b, op in ((w[0], w[2], C_HALF, ALU.mult), (w[5], w[3], w[3], ALU.mult),
                                        (w[6], w[5], C_QUARTER, ALU.mult), (w[7], w[4], C_INVN, ALU.mult),
                                        (w[5], w[6], w[7], ALU.add), (w[6], w[5], C_EPS, ALU.add),
                                        (w[1], w[6], C_NEGHALF, ALU.pow)):
                        pool.wait_ge(done, done_before + k)
                        g.tensor_tensor(o, a, b, op).then_inc(done, 1)
                        k += 1

                def rstd_of(w, aggregates, done):
                    pool.wait_ge(s["aggregated"], TILES * aggregates)
                    g.tensor_tensor(w[:, 7, :], w[:, 6, :], C_EPS, ALU.add).then_inc(s["eps_added"], 1)
                    pool.wait_ge(s["eps_added"], aggregates)
                    g.tensor_tensor(w[:, 1, :], w[:, 7, :], C_NEGHALF, ALU.pow).then_inc(done, 10)

                def x2_rstd(b):
                    rstd(stats2, lnw2, m["x2_stats"], TILES * (b + 1), m["x2_rstd"], 10 * b)

                def act_pow(b):
                    pool.wait_ge(m["route_steps"], ROUTE * b + 13)
                    g.tensor_tensor(rt[:, 8, :, :], rt[:, 6, :, :], half8[:, :, :], ALU.pow)\
                     .then_inc(m["activation_done"], 1)

                gB3 = gB[:, :].unsqueeze(1).to_broadcast([P, TILES, D])
                bB3 = bB[:, :].unsqueeze(1).to_broadcast([P, TILES, D])

                def norm_n(i):
                    if isinstance(i, int) and i == 0:
                        rstd_of(lnw, 1, s["a_rstd"])
                        rstd_of(lnw, 2, s["a_rstd"])
                        return
                    rstd(stats, lnw, s["a_stats"], 8 * i + 4, s["a_rstd"], 20 * i)
                    rstd(stats, lnw, s["a_stats"], 8 * i + 8, s["a_rstd"], 20 * i + 10)
                    pool.wait_ge(s["a_norm"], 2 * TILES * (i + 1))
                    g.tensor_tensor(n32[:, :, :], n32[:, :, :], gB3, ALU.mult).then_inc(s["a_out"], 1)
                    pool.wait_ge(s["a_out"], 2 * i + 1)
                    g.tensor_tensor(n32[:, :, :], n32[:, :, :], bB3, ALU.add).then_inc(s["a_out"], 1)

                def norm_t(i):
                    if isinstance(i, int) and i == NBLK - 1:
                        rstd_of(lnw, 3, s["e_rstd"])
                        rstd_of(lnw, 4, s["e_rstd"])
                        return
                    rstd(stats, lnw, s["e_stats"], 8 * i + 4, s["e_rstd"], 20 * i)
                    rstd(stats, lnw, s["e_stats"], 8 * i + 8, s["e_rstd"], 20 * i + 10)
                    pool.wait_ge(s["e_norm"], 2 * TILES * (i + 1))
                    g.tensor_tensor(work[:, :, :], work[:, :, :], gB3, ALU.mult).then_inc(s["e_out"], 1)
                    pool.wait_ge(s["e_out"], 2 * i + 1)
                    g.tensor_tensor(work[:, :, :], work[:, :, :], bB3, ALU.add).then_inc(s["e_out"], 1)

                norm_n(0)
                pool.wait_ge(s["norm_weights_loaded"], 16 * 2)
                norm_n(1)
                norm_t(0)
                with pool.Fori(1, NBLK - 1) as i:
                    norm_n(i + 1)
                    norm_t(i)
                pool.wait_ge(s["down_done"], unit_base(NBLK - 1) + HU)
                g.memset(bias32[:, :], 0.0).then_inc(m["consts_set"], 1)
                g.memset(sel[:, :, :].bitcast(F32), 0.0).then_inc(m["consts_set"], 1)
                g.memset(half8[:, :, :], 0.5).then_inc(m["consts_set"], 1)
                for e in range(EXPERTS):
                    g.memset(iota[:, e:e + 1], float(e)).then_inc(m["consts_set"], 1)
                for half in range(2):
                    pool.wait_ge(m["consts_set"], 3 + EXPERTS + half)
                    g.affine_select(out=sel[:, :, :], in_=sel[:, :, :].bitcast(F32), compare_op=ALU.not_equal,
                                    fill=1.0, base=-EXPERTS * half, pattern=[[-1, EXPERTS], [0, P]],
                                    channel_multiplier=1).then_inc(m["consts_set"], 1)
                pool.wait_ge(s["delta_ready"], 2 * NBLK)
                g.memset(cfx[:, :, :], 0.0).then_inc(m["consts_set"], 1)
                pool.wait_ge(m["consts_set"], 14)
                for r in (0, BIAS_LO):
                    g.memset(cfx[:, :, r + 2 * EXPERTS:r + 2 * EXPERTS + 1], 1.0).then_inc(m["consts_set"], 1)
                norm_t(NBLK - 1)
                x2_rstd(0)
                x2_rstd(1)
                act_pow(0)

                def turn(b, q, ahead):
                    if ahead >= 1:
                        act_pow(b + 1)
                    if ahead >= 2:
                        x2_rstd(b + 2)

                pairs(pool, turn)

            @block.scalar
            def _(act):
                a = nc.scalar

                def hi_weights(key):
                    act.wait_ge(s[f"ld_{key[0]}w{key[1]}"], 16)
                    if key == ("fm", 1):
                        act.wait_ge(s["w_lo"], 4)
                    a.copy(W[key[0], key[1], "hi"][:, :, :], stage[key][:, :, :]).then_inc(s["w_hi"], 1)

                def unit(i, u, j, ht, slot_off, q_first=False):
                    U = unit_base(i) + u
                    slot = (slot_off + u) % 3
                    known_first = isinstance(i, int) and i == 0
                    act.wait_ge(s["up_ready"], U + 1)
                    if not (known_first and u < 3):
                        act.wait_ge(s["down_done"], U - 2)
                    a.activation(G[0][:, slot, :], upB[u % 2][:, :], ACT.Gelu, bias=col(B1[j], ht))
                    if not (known_first and u < 2):
                        act.wait_ge(s["split_ready"], U - 1)
                    if q_first:
                        QT_hi(i, 0)
                    a.activation(G32[:, u % 2, :], upB[u % 2][:, :], ACT.Gelu,
                                 bias=col(B1[j], ht)).then_inc(s["gelu_done"], 1)

                def hi_T(dst, banks, ps, hi, before):
                    for k in range(KD):
                        act.wait_ge(s[ps], before + k + 1)
                        a.copy(dst[0][:, k, :], banks[k][:, :]).then_inc(s[hi], 1)

                def nT_hi(i):
                    hi_T(nT, A, "nT_ps", "nT_hi", 2 * i)
                    a.copy(ntok[0][:, :, :], n32[:, :, :]).then_inc(s["ntok_hi"], 1)

                def state_hi(c, i):
                    if c == 0:
                        if not (isinstance(i, int) and i == 0):
                            act.wait_ge(s["state_add"], 2 * i)
                            act.wait_ge(s["qs_done"], 2 * i - 1)
                        src = state[:, one(zero_or_state(i)), :]
                    else:
                        act.wait_ge(s["state_add"], 2 * i + 1)
                        if not (isinstance(i, int) and i == 0):
                            act.wait_ge(s["qs_done"], 2 * i)
                        src = state[:, 1:2, :]
                    a.copy(St[c][0][:, :], src.rearrange("p o n -> p (o n)")).then_inc(s["state_hi"], 1)

                def next_units(i):
                    for u in range(LAG):
                        unit(i, u, 0, u, off(i))

                def h_part(i):
                    first = isinstance(i, int) and i == 0
                    for u in range(LAG, HU):
                        unit(i, u, u // NH, u % NH, off(i))
                        if u == 9 and not first:
                            hi_T(n2T, M, "n2T_ps", "n2T_hi", 2 * (i - 1))
                        if first and u in (8, 9):
                            hi_weights(("fm", u - 7))
                        if u == 10:
                            for f in range(KD):
                                if f == 0:
                                    act.wait_ge(s["k_ready"], i + 1)
                                else:
                                    act.wait_ge(s["down_done"], unit_base(i) + NH)
                                a.activation(KT32[:, f, :], A[f][:, :], ACT.Identity,
                                             bias=col("h2_b2", f)).then_inc(s["k_f32"], 1)
                                a.activation(KT[0][:, f, :], A[f][:, :], ACT.Identity,
                                             bias=col("h2_b2", f)).then_inc(s["k_hi"], 1)
                        if u == 13:
                            if first:
                                act.wait_ge(s["w_lo"], 6)
                            for h in range(2):
                                act.wait_ge(s["ktok_ps"], 2 * i + h + 1)
                                a.copy(Ktok[0][:, 2 * h:2 * h + 2, :], tok2(M[h])).then_inc(s["ktok_hi"], 1)

                def fm_units(i, lo_, hi_, base):
                    for v_ in range(lo_, hi_):
                        unit(i, base + v_, 2, v_, 1, q_first=(base == HU and v_ == LAG - 1))

                def QT_hi(i, f):
                    if f == 0:
                        act.wait_ge(s["q_ready"], i + 1)
                    else:
                        act.wait_ge(s["down_done"], unit_base(i) + HU)
                    a.activation(QT[0][:, f, :], B[f][:, :], ACT.Identity,
                                 bias=col("h1_b2", f)).then_inc(s["q_hi"], 1)

                def attention(i, last):
                    if isinstance(i, int) and i == 0:
                        QT_hi(i, 0)
                    QT_hi(i, 1)
                    state_hi(1, i)
                    for c in range(CHUNKS):
                        act.wait_ge(s["s_masked"], 4 * i + 2 * c + 2)
                        a.copy(SP_[0][:, c, :], S32[:, c, :]).then_inc(s["s_hi"], 1)
                    if not last:
                        state_hi(0, i + 1)
                    for c in range(CHUNKS):
                        act.wait_ge(s["t_ready"], 2 * i + c + 1)
                        a.activation(work[:, 2 * c:2 * c + 2, :], tok2(M[c]), ACT.Gelu).then_inc(s["t_gelu"], 1)
                    if not last:
                        nT_hi(i + 1)

                def XT_hi(b, q, k):
                    act.wait_ge(m["XT_ps"], 2 * b + k + 1)
                    a.copy(XT[q][0][:, k, :], routing_bank(b, k)[:, :]).then_inc(m["XT_hi"], 1)

                def softplus_tables(b):
                    a.preload_act_table_set("natural_log_exp_and_others")
                    act.wait_ge(m["route_steps"], ROUTE * b + 4)
                    a.activation(rt[:, 3, :, :], rt[:, 2, :, :], ACT.Exp, scale=-1.0).then_inc(m["exp_done"], 1)
                    act.wait_ge(m["route_steps"], ROUTE * b + 5)
                    a.activation(rt[:, 5, :, :], rt[:, 4, :, :], ACT.Ln).then_inc(m["ln_done"], 1)

                def cfT_out(b, q):
                    act.wait_ge(m["cfT_ps"], b + 1)
                    a.copy(cfT[q][:, :], routing_bank(b, 1)[:, :]).then_inc(m["cfT_out"], 1)

                act.wait_ge(s["cols_ps"], 1)
                a.copy(cols[:, :], B[0][:, 0:NROWS]).then_inc(s["cols_out"], 1)
                act.wait_ge(s["const_pool"], 3)
                act.wait_ge(s["cols_out"], 1)
                state_hi(0, 0)
                hi_weights(("h2", 1))
                hi_weights(("h2", 2))
                a.preload_act_table_set("gelu_and_others")
                nT_hi(0)
                next_units(0)
                hi_weights(("h1", 1))
                hi_weights(("h1", 2))
                h_part(0)
                attention(0, False)
                next_units(1)
                with act.Fori(1, NBLK - 1) as i:
                    h_part(i)
                    fm_units(i, 0, LAG, HU)
                    attention(i, False)
                    fm_units(i, LAG, NH, HU)
                    next_units(i + 1)
                last = NBLK - 1
                h_part(last)
                fm_units(last, 0, LAG, HU)
                attention(last, True)
                fm_units(last, LAG, NH, HU)
                a.copy(rw[:, :, 0:EXPERTS], routing_cols).then_inc(m["weights_hi"], 1)
                act.wait_ge(m["weights_loaded"], 16 * 11)
                act.wait_ge(m["y_odd_stored"], 16)
                act.wait_ge(m["y_even_stored"], 16)
                a.copy(eW1[0][:, :, :, :], e1_32[:, :, :, :]).then_inc(m["weights_hi"], 1)
                a.copy(eW2[0][:, :, :], e2_32[:, :, :]).then_inc(m["weights_hi"], 1)
                a.copy(biasR[:, :], bias32[:, :]).then_inc(m["weights_hi"], 1)
                hi_T(n2T, M, "n2T_ps", "n2T_hi", 2 * last)
                fm_units(NBLK, 0, 2, 0)
                for k in range(KD):
                    XT_hi(0, 0, k)
                fm_units(NBLK, 2, 3, 0)
                softplus_tables(0)
                fm_units(NBLK, 3, NH, 0)
                XT_hi(1, 1, 0)
                cfT_out(0, 0)

                def turn(b, q, ahead):
                    first = is_first(b)
                    late = int(first)
                    for u in range(UNITS):
                        U = UNITS * b + u
                        slot, two = u % 3, (q + u) % 2
                        bias = col("rb1", u) if u < EXPERTS else col("sb1")
                        act.wait_ge(m["up_ps"], U + 1)
                        if not (first and u < 2):
                            act.wait_ge(m["hidden_lo"], U - 1)
                        a.activation(s32[:, two, :], up3[slot][:, :], ACT.Silu, bias=bias).then_inc(m["silu_done"], 1)
                        if not (first and u < 3):
                            act.wait_ge(m["down_done"], U - 2)
                        if u < EXPERTS:
                            act.wait_ge(m["scaled"], EXPERTS * b + u + 1)
                            a.copy(H[0][:, slot, :], h32[:, two, :]).then_inc(m["hidden_hi"], 1)
                        else:
                            if ahead >= 1:
                                cfT_out(b + 1, 1 - q)
                            a.activation(H[0][:, slot, :], up3[slot][:, :], ACT.Silu, bias=bias)\
                             .then_inc(m["hidden_hi"], 1)
                        if ahead >= 1:
                            if u in (0, 1) and not (first and u == 1):
                                XT_hi(b + 1, 1 - q, u + late)
                            if u - late == 2:
                                softplus_tables(b + 1)

                pairs(act, turn)

            @block.vector
            def _(dve):
                v = nc.vector

                def lo(dst, src, hi):
                    return v.tensor_tensor(dst, src, hi.bitcast(F32), ALU.subtract)

                def lo_weights(key, before):
                    dve.wait_ge(s["w_hi"], before + 1)
                    lo(W[key[0], key[1], "lo"][:, :, :], stage[key][:, :, :],
                       W[key[0], key[1], "hi"][:, :, :]).then_inc(s["w_lo"], 1)

                def lo_T(dst, banks, hi, lo_, before):
                    for k in range(KD):
                        dve.wait_ge(s[hi], before + k + 1)
                        lo(dst[1][:, k, :], banks[k][:, :], dst[0][:, k, :]).then_inc(s[lo_], 1)

                def nT_lo(i):
                    lo_T(nT, A, "nT_hi", "nT_lo", 2 * i)
                    dve.wait_ge(s["ntok_hi"], i + 1)
                    lo(ntok[1][:, :, :], n32[:, :, :], ntok[0][:, :, :]).then_inc(s["ntok_lo"], 1)

                def row_stats(buf, done):
                    for t in range(TILES):
                        v.bn_stats(stats[:, t, :], buf[:, t, :]).then_inc(done, 1)

                def normalise(dst, src, done):
                    for t in range(TILES):
                        v.tensor_scalar(dst[:, t, :], src[:, t, :], lnw[:, 0, t:t + 1], lnw[:, 1, t:t + 1],
                                        ALU.subtract, ALU.mult).then_inc(done, 1)

                def scale_shift(buf, at_sem, at_count, norm_sem, norm_count, done, done_before):
                    dve.wait_ge(at_sem, at_count)
                    dve.wait_ge(norm_sem, norm_count)
                    v.tensor_tensor(buf[:, :, :], buf[:, :, :], gB[:, :].unsqueeze(1).to_broadcast([P, TILES, D]),
                                    ALU.mult).then_inc(done, 1)
                    dve.wait_ge(done, done_before + 1)
                    v.tensor_tensor(buf[:, :, :], buf[:, :, :], bB[:, :].unsqueeze(1).to_broadcast([P, TILES, D]),
                                    ALU.add).then_inc(done, 1)

                def xa_of(i):
                    return xa[:, par(i), :, :].rearrange("p o t d -> p (o t) d")

                def resid_of(i):
                    return resid[:, par(i), :, :].rearrange("p o t d -> p (o t) d")

                def aggregate(stat_sem, count):
                    dve.wait_ge(stat_sem, count)
                    for t in range(TILES):
                        v.bn_aggr(lnw[:, 0:7:6, t], stats[:, t, :]).then_inc(s["aggregated"], 1)

                def a_step(i, step):
                    if step == 0:
                        dve.wait_ge(s["x_loaded"], 16 * (i + 1))
                        row_stats(xin, s["a_stats"])
                    elif step == 1:
                        dve.wait_ge(s["a_rstd"], 20 * i + 10)
                        normalise(xa_of(i), xin, s["a_norm"])
                    elif step == 2:
                        dve.wait_ge(s["a_norm"], 2 * TILES * i + TILES)
                        v.tensor_copy(touch1[:, :], lnw[:, 0, :])
                        row_stats(xa_of(i), s["a_stats"])
                    else:
                        dve.wait_ge(s["a_rstd"], 20 * i + 20)
                        normalise(n32, xa_of(i), s["a_norm"])

                def residual(i):
                    dve.wait_ge(s["fb2_st_x2"], 16 if isinstance(i, int) and i == 0 else 16 * i)
                    v.tensor_tensor(resid_of(i), xin[:, :, :], xa_of(i), ALU.add).then_inc(s["x_used"], 1)
                    dve.wait_ge(s["x_used"], i + 1)
                    v.tensor_tensor(resid_of(i), resid_of(i), fb2B[:, :].unsqueeze(1).to_broadcast([P, TILES, D]),
                                    ALU.add).then_inc(s["resid_set"], 1)

                def unit(i, u, slot_off):
                    U = unit_base(i) + u
                    slot = (slot_off + u) % 3
                    dve.wait_ge(s["gelu_done"], U + 1)
                    lo(G[1][:, slot, :], G32[:, u % 2, :], G[0][:, slot, :]).then_inc(s["split_ready"], 1)

                def e_step(i, step):
                    w3 = work[:, :, :]
                    if step == 0:
                        dve.wait_ge(s["t_gelu"], 2 * i + 2)
                        row_stats(work, s["e_stats"])
                    elif step == 1:
                        dve.wait_ge(s["e_rstd"], 20 * i + 10)
                        normalise(work, work, s["e_norm"])
                    elif step == 2:
                        dve.wait_ge(s["e_norm"], 2 * TILES * i + TILES)
                        v.tensor_tensor(w3, w3, gB[:, :].unsqueeze(1).to_broadcast([P, TILES, D]),
                                        ALU.mult).then_inc(s["e_mid"], 1)
                    elif step == 3:
                        dve.wait_ge(s["e_mid"], 3 * i + 1)
                        v.tensor_tensor(w3, w3, bB[:, :].unsqueeze(1).to_broadcast([P, TILES, D]),
                                        ALU.add).then_inc(s["e_mid"], 1)
                        dve.wait_ge(s["e_mid"], 3 * i + 2)
                        v.tensor_tensor(w3, w3, xa_of(i), ALU.add).then_inc(s["e_mid"], 1)
                    elif step == 4:
                        dve.wait_ge(s["e_mid"], 3 * i + 3)
                        row_stats(work, s["e_stats"])
                    else:
                        dve.wait_ge(s["e_rstd"], 20 * i + 20)
                        normalise(work, work, s["e_norm"])

                def state_lo(c, i):
                    dve.wait_ge(s["state_hi"], 2 * i + c + 1)
                    src = state[:, one(zero_or_state(i)), :] if c == 0 else state[:, 1:2, :]
                    lo(St[c][1][:, :], src.rearrange("p o n -> p (o n)"), St[c][0][:, :]).then_inc(s["state_lo"], 1)

                def add_delta(c, i):
                    dve.wait_ge(s["delta_ready"], 2 * i + c + 1)
                    src = state[:, one(zero_or_state(i)), :] if c == 0 else state[:, 1:2, :]
                    dve.wait_ge(s["state_lo"], 2 * i + c + 1)
                    v.tensor_tensor(state[:, 1, :], M[c][:, :], src.rearrange("p o n -> p (o n)"),
                                    ALU.add).then_inc(s["state_add"], 1)

                def next_units(i):
                    for u in range(LAG):
                        unit(i, u, off(i))

                def h_part(i, last):
                    first = isinstance(i, int) and i == 0
                    for u in range(LAG, HU):
                        unit(i, u, off(i))
                        if u == 9 and not first:
                            lo_T(n2T, M, "n2T_hi", "n2T_lo", 2 * (i - 1))
                        if not first and u in (3, 5):
                            e_step(i - 1, 4 if u == 3 else 5)
                        if u == 6:
                            residual(i)
                        if first and u in (8, 9):
                            lo_weights(("fm", u - 7), u - 4)
                        if u == 10:
                            for f in range(KD):
                                dve.wait_ge(s["k_hi"], 2 * i + f + 1)
                                lo(KT[1][:, f, :], KT32[:, f, :], KT[0][:, f, :]).then_inc(s["k_lo"], 1)
                        if u == 13:
                            for h in range(2):
                                dve.wait_ge(s["ktok_hi"], 2 * i + h + 1)
                                lo(Ktok[1][:, 2 * h:2 * h + 2, :], tok2(M[h]),
                                   Ktok[0][:, 2 * h:2 * h + 2, :]).then_inc(s["ktok_lo"], 1)
                        if not last and u in (9, 11, 12, 14):
                            a_step(i + 1, (9, 11, 12, 14).index(u))

                def mask(c, i):
                    dve.wait_ge(s["s_ps"], 2 * i + c + 1)
                    dst = S32[:, c, :].rearrange("p (a b) -> p a b", b=P)
                    src = A[c][:, 0:384].rearrange("p (a b) -> p a b", b=P)
                    v.tensor_tensor(dst[:, 0:3:2, :], src[:, 0:3:2, :], tri[:, :].unsqueeze(1).to_broadcast([P, 2, P]),
                                    ALU.mult).then_inc(s["s_masked"], 1)
                    v.tensor_copy(dst[:, 1, :], src[:, 1, :]).then_inc(s["s_masked"], 1)

                def QT_lo(i, f):
                    dve.wait_ge(s["q_hi"], 2 * i + f + 1)
                    v.scalar_tensor_tensor(out=QT[1][:, f, :], in0=B[f][:, :], scalar=col("h1_b2", f),
                                           in1=QT[0][:, f, :].bitcast(F32), op0=ALU.add,
                                           op1=ALU.subtract).then_inc(s["q_lo"], 1)

                def attention(i, last):
                    if isinstance(i, int) and i == 0:
                        QT_lo(i, 0)
                    QT_lo(i, 1)
                    add_delta(0, i)
                    state_lo(1, i)
                    mask(0, i)
                    add_delta(1, i)
                    mask(1, i)
                    for c in range(CHUNKS):
                        dve.wait_ge(s["s_hi"], 2 * i + c + 1)
                        lo(SP_[1][:, c, :], S32[:, c, :], SP_[0][:, c, :]).then_inc(s["s_lo"], 1)
                    if not last:
                        state_lo(0, i + 1)
                        nT_lo(i + 1)

                def x2_out(i, units):
                    r = resid_of(i)
                    dve.wait_ge(s["resid_set"], i + 1)
                    for h in range(2):
                        if h == 0:
                            dve.wait_ge(s["f_ready"], i + 1)
                        else:
                            dve.wait_ge(s["down_done"], units)
                        v.tensor_tensor(r[:, 2 * h:2 * h + 2, :], tok2(B[h]), r[:, 2 * h:2 * h + 2, :],
                                        ALU.add).then_inc(s["x2_ready"], 1)

                def fm_units(i, lo_, hi_, base, e_block=None):
                    for v_ in range(lo_, hi_):
                        if base == HU and v_ == LAG - 1:
                            QT_lo(i, 0)
                        unit(i, base + v_, 1)
                        if e_block is not None and v_ > LAG:
                            e_step(e_block, v_ - LAG - 1)

                def x2_stats(b, q):
                    dve.wait_ge(at_parity(q, "x2_even_loaded", "x2_odd_loaded"), 16 * half_count(b, q))
                    v.tensor_copy(touch[:, 0:4], ident[:, 0:4])
                    for t in range(TILES):
                        v.bn_stats(stats2[:, t, :], x2_of(b)[:, t, :]).then_inc(m["x2_stats"], 1)

                def x2_normalise(b):
                    dve.wait_ge(m["x2_rstd"], 10 * (b + 1))
                    if not is_first(b):
                        dve.wait_ge(m["XT_ps"], 2 * b)
                    for t in range(TILES):
                        v.tensor_scalar(xn[:, t, :], x2_of(b)[:, t, :], lnw2[:, 0, t:t + 1], lnw2[:, 1, t:t + 1],
                                        ALU.subtract, ALU.mult).then_inc(m["x2_normed"], 1)

                def XT_lo(b, q, k):
                    dve.wait_ge(m["XT_hi"], 2 * b + k + 1)
                    lo(XT[q][1][:, k, :], routing_bank(b, k)[:, :], XT[q][0][:, k, :]).then_inc(m["XT_lo"], 1)

                def r_step(b, k):
                    dve.wait_ge(m["route_steps"], ROUTE * b + k)

                R = [rt[:, j, :, :] for j in range(11)]

                def softplus_start(b):
                    lg = routing_bank(b, 0)[:, 0:TILES * 2 * EXPERTS].rearrange("p (t e) -> p t e", t=TILES)
                    r = m["route_steps"]
                    dve.wait_ge(m["logits_ps"], b + 1)
                    v.tensor_tensor(R[0], lg[:, :, EXPERTS:2 * EXPERTS],
                                    ebB[:, :].unsqueeze(1).to_broadcast([P, TILES, EXPERTS]), ALU.add).then_inc(r, 1)
                    r_step(b, 1)
                    v.tensor_tensor(R[1], lg[:, :, 0:EXPERTS], R[0], ALU.add).then_inc(r, 1)
                    r_step(b, 2)
                    v.tensor_scalar(R[0], R[1], -1.0, None, ALU.mult).then_inc(r, 1)
                    r_step(b, 3)
                    v.tensor_tensor(R[2], R[1], R[0], ALU.max).then_inc(r, 1)
                    dve.wait_ge(m["exp_done"], b + 1)
                    v.tensor_scalar(R[4], R[3], 1.0, None, ALU.add).then_inc(r, 1)

                def softplus_end(b):
                    r = m["route_steps"]
                    r_step(b, 5)
                    v.tensor_scalar(R[0], R[4], -1.0, None, ALU.add).then_inc(r, 1)
                    r_step(b, 6)
                    v.tensor_scalar(R[7], R[0], 1e-30, None, ALU.max).then_inc(r, 1)
                    r_step(b, 7)
                    v.reciprocal(R[9], R[7]).then_inc(r, 1)
                    v.scalar_tensor_tensor(out=R[0], in0=R[0], scalar=0.0, in1=R[3], op0=ALU.is_equal,
                                           op1=ALU.mult).then_inc(r, 1)
                    r_step(b, 9)
                    v.tensor_tensor(R[9], R[9], R[3], ALU.mult).then_inc(r, 1)
                    v.scalar_tensor_tensor(out=R[0], in0=R[1], scalar=0.0, in1=R[0], op0=ALU.max,
                                           op1=ALU.add).then_inc(r, 1)
                    r_step(b, 11)
                    dve.wait_ge(m["ln_done"], b + 1)
                    v.tensor_tensor(R[6], R[5], R[9], ALU.mult).then_inc(r, 1)
                    r_step(b, 12)
                    v.tensor_tensor(R[6], R[6], R[0], ALU.add).then_inc(r, 1)

                def select(b):
                    r = m["route_steps"]
                    v.tensor_copy(touch[:, 0:4], R[1][:, :, 0])
                    for t in range(TILES):
                        mx = v.max(top8[:, t, :], R[1][:, t, :])
                    mx.then_inc(r, 1)
                    r_step(b, 14)
                    v.tensor_copy(touch[:, 4:8], top8[:, :, 0])
                    for t in range(TILES):
                        mx = v.max_index(topi[:, t, :], top8[:, t, :], R[1][:, t, :])
                    mx.then_inc(r, 1)
                    r_step(b, 15)
                    v.tensor_copy(topf[:, :, 0:2], topi[:, :, 0:2]).then_inc(r, 1)
                    r_step(b, 16)
                    io = iota[:, :].unsqueeze(1).to_broadcast([P, TILES, EXPERTS])
                    v.tensor_tensor(R[10], io, topf[:, :, 0:1].to_broadcast([P, TILES, EXPERTS]), ALU.is_equal)
                    v.tensor_tensor(R[2], io, topf[:, :, 1:2].to_broadcast([P, TILES, EXPERTS]),
                                    ALU.is_equal).then_inc(r, 1)
                    r_step(b, 17)
                    v.tensor_tensor(R[10], R[10], R[2], ALU.add).then_inc(r, 1)

                def combine(b):
                    dve.wait_ge(m["activation_done"], b + 1)
                    r_step(b, ROUTE)
                    v.tensor_tensor(R[7], R[10], R[8], ALU.mult).then_inc(m["combine_steps"], 1)
                    dve.wait_ge(m["combine_steps"], 2 * b + 1)
                    if not is_first(b):
                        dve.wait_ge(m["cfT_ps"], b)
                    v.tensor_copy(cfh[:, :, :], R[7]).then_inc(m["combine_steps"], 1)
                    dve.wait_ge(m["combine_steps"], 2 * b + 2)
                    for r in (0, BIAS_LO):
                        v.tensor_copy(cfx[:, :, r:r + EXPERTS], cfh[:, :, :].bitcast(F32))
                        last = lo(cfx[:, :, r + EXPERTS:r + 2 * EXPERTS], R[7], cfh[:, :, :])
                    last.then_inc(m["cf_placed"], 1)

                def output(b, q):
                    if not is_first(b):
                        dve.wait_ge(at_parity(q, "y_even_stored", "y_odd_stored"), 16 * half_count(b, q))
                    for h in range(2):
                        dve.wait_ge(m["sum_ps"], 2 * b + h + 1)
                        v.tensor_tensor(y[q][:, 2 * h:2 * h + 2, :], tok2(Y[h]), x2_of(b)[:, 2 * h:2 * h + 2, :],
                                        ALU.add).then_inc(m["y_formed"], 1)

                v.memset(touch1[:, :], 0.0).then_inc(s["x2_ready"], 2)
                a_step(0, 0)
                aggregate(s["a_stats"], TILES)
                a_step(0, 1)
                a_step(0, 2)
                aggregate(s["a_stats"], 2 * TILES)
                dve.wait_ge(s["const_pool"], 3)
                state_lo(0, 0)
                a_step(0, 3)
                scale_shift(n32, s["norm_weights_loaded"], 16 * 2, s["a_norm"], 2 * TILES, s["a_out"], 0)
                lo_weights(("h2", 1), 0)
                nT_lo(0)
                lo_weights(("h2", 2), 1)
                dve.wait_ge(s["cols_out"], 1)
                for u in range(LAG):
                    unit(0, u, off(0))
                lo_weights(("h1", 1), 2)
                lo_weights(("h1", 2), 3)
                h_part(0, False)
                attention(0, False)
                for u in range(LAG):
                    unit(1, u, off(1))
                    for step in ((0,), (1, 2), (3,))[u]:
                        e_step(0, step)
                with dve.Fori(1, NBLK - 1) as i:
                    h_part(i, False)
                    fm_units(i, 0, LAG, HU)
                    attention(i, False)
                    fm_units(i, LAG, NH, HU, i)
                    next_units(i + 1)
                    x2_out(i - 1, unit_base(i + 1))
                last = NBLK - 1
                h_part(last, True)
                fm_units(last, 0, LAG, HU)
                attention(last, True)
                for v_ in range(LAG, NH):
                    unit(last, HU + v_, 1)
                    for step in ((0,), (1,), (2, 3), (4,), (5,))[v_ - LAG]:
                        e_step(last, step)
                        if step == 0:
                            aggregate(s["e_stats"], 8 * last + TILES)
                        if step == 4:
                            aggregate(s["e_stats"], 8 * last + 2 * TILES)
                    if v_ == LAG + 3:
                        x2_stats(0, 0)
                scale_shift(work, s["norm_weights_loaded"], 16 * 2, s["e_norm"], 2 * TILES * NBLK, s["e_out"], 2 * last)
                lo_T(n2T, M, "n2T_hi", "n2T_lo", 2 * last)
                dve.wait_ge(m["weights_hi"], 1)
                lo(rw[:, :, EXPERTS:2 * EXPERTS], routing_cols, rw[:, :, 0:EXPERTS]).then_inc(m["weights_lo"], 1)
                x2_normalise(0)
                x2_out(last - 1, unit_base(NBLK))
                dve.wait_ge(m["weights_hi"], 4)
                lo(eW1[1][:, :, :, :].rearrange("p k e h -> p (k e h)"), e1_32[:, :, :, :].rearrange("p k e h -> p (k e h)"),
                   eW1[0][:, :, :, :].rearrange("p k e h -> p (k e h)")).then_inc(m["weights_lo"], 1)
                fm_units(NBLK, 0, 2, 0)
                for k in range(KD):
                    XT_lo(0, 0, k)
                fm_units(NBLK, 2, 3, 0)
                softplus_start(0)
                x2_stats(1, 1)
                fm_units(NBLK, 3, 4, 0)
                softplus_end(0)
                select(0)
                fm_units(NBLK, 4, 5, 0)
                lo(eW2[1][:, :, :], e2_32[:, :, :], eW2[0][:, :, :]).then_inc(m["weights_lo"], 1)
                low = slice(BIAS_LO, 2 * BIAS_LO)
                lo(biasR[low, :], bias32[low, :], biasR[low, :]).then_inc(m["weights_lo"], 1)
                fm_units(NBLK, 5, 6, 0)
                x2_normalise(1)
                fm_units(NBLK, 6, 7, 0)
                dve.wait_ge(m["consts_set"], 16)
                combine(0)
                fm_units(NBLK, 7, NH, 0)
                XT_lo(1, 1, 0)

                def turn(b, q, ahead):
                    late = int(is_first(b))
                    if is_first(b):
                        x2_out(NBLK - 1, unit_base(NBLK) + NH)
                    for u in range(UNITS):
                        U = UNITS * b + u
                        slot, two = u % 3, (q + u) % 2
                        if u < EXPERTS:
                            dve.wait_ge(m["silu_done"], U + 1)
                            dve.wait_ge(m["spread_ps"], EXPERTS * b + u + 1)
                            v.tensor_tensor(h32[:, two, :], CB[u % 2][:, :], s32[:, two, :],
                                            ALU.mult).then_inc(m["scaled"], 1)
                        if not is_first(b) and u == LAG - 1:
                            output(b - 1, 1 - q)
                        if ahead >= 1 and u == 6:
                            combine(b + 1)
                        dve.wait_ge(m["hidden_hi"], U + 1)
                        lo(H[1][:, slot, :], (h32 if u < EXPERTS else s32)[:, two, :],
                           H[0][:, slot, :]).then_inc(m["hidden_lo"], 1)
                        if ahead >= 1:
                            if u in (0, 1) and not (is_first(b) and u == 1):
                                XT_lo(b + 1, 1 - q, u + late)
                            if u - late == 2:
                                softplus_start(b + 1)
                            if u - late == 3:
                                softplus_end(b + 1)
                            if u - late == 4:
                                select(b + 1)
                        if ahead >= 2:
                            if u == 5:
                                x2_stats(b + 2, q)
                            if u == 7:
                                x2_normalise(b + 2)

                pairs(dve, turn)
                output(NBLK - 1, 1)

            @block.tensor
            def _(pe):
                t_ = nc.tensor

                def up(i, u, j, ht, src):
                    U = unit_base(i) + u
                    first = isinstance(i, int) and i == 0
                    if not (first and u < 2):
                        pe.wait_ge(s["gelu_done"], U - 1)
                    b = upB[u % 2]
                    w = W2[MLP[j], 1]
                    for k in range(KD):
                        last = mm3(b[:, :], w, src, (slice(None), k, slice(ht * P, ht * P + P)),
                                   (slice(None), k, slice(None)), start=(k == 0), stop=(k == KD - 1))
                    last.then_inc(s["up_ready"], 1)

                def down_rows(i, u, ht, slot_off):
                    pe.wait_ge(s["split_ready"], unit_base(i) + u + 1)
                    slot = (slot_off + u) % 3
                    for t in range(TILES):
                        last = mm3(tok2(B[t // 2])[:, t % 2, :], G, W2["fm", 2],
                                   (slice(None), slot, slice(t * P, t * P + P)), (slice(None), ht, slice(None)),
                                   start=(ht == 0 and t % 2 == 0), stop=(ht == NH - 1))
                        if ht == NH - 1 and t % 2 == 1 and t < TILES - 1:
                            last.then_inc(s["f_ready"], 1)
                    return last

                def transposes(src_tile, banks, ps):
                    for k in range(KD):
                        for t in range(TILES):
                            last = t_.transpose(banks[k][:, t * P:(t + 1) * P], src_tile[:, t, k * P:(k + 1) * P],
                                                ident[:, :])
                        last.then_inc(s[ps], 1)

                def T_nT(i):
                    pe.wait_ge(s["a_out"], 2 * i + 2)
                    if not (isinstance(i, int) and i == 0):
                        pe.wait_ge(s["s_masked"], 4 * i)
                    transposes(n32, A, "nT_ps")

                def T_n2T(i):
                    pe.wait_ge(s["e_out"], 2 * i + 2)
                    transposes(work, M, "n2T_ps")

                def down_h(i, u, o):
                    j = u // NH
                    ht = u % NH
                    acc, ready = ((A, "k_ready"), (B, "q_ready"))[j]
                    if ht == 0 and not (isinstance(i, int) and i == 0):
                        if j == 0:
                            pe.wait_ge(s["t_gelu"], 2 * i)
                        else:
                            pe.wait_ge(s["x2_ready"], 2 * i)
                    pe.wait_ge(s["split_ready"], unit_base(i) + u + 1)
                    slot = (o + u) % 3
                    w = W2[MLP[j], 2]
                    for f in range(KD):
                        ws = (slice(None), ht, slice(f * P, f * P + P))
                        vs = (slice(None), slot, slice(None))
                        last = mm3(acc[f][:, :], w, G, ws, vs, start=(ht == 0), stop=(ht == NH - 1))
                        if ht == NH - 1 and f == 0:
                            last.then_inc(s[ready], 1)
                    last.then_inc(s["down_done"], 1)

                def down(i, u):
                    if u < HU:
                        down_h(i, u, off(i))
                        return
                    if u == HU:
                        pe.wait_ge(s["q_lo"], 2 * i + 2)
                    down_rows(i, u, u - HU, 1).then_inc(s["down_done"], 1)

                def next_units(i, has_fm):
                    pe.wait_ge(s["nT_lo"], 2 * (i + 1))
                    for u in range(LAG):
                        up(i, u, 0, u, nT)
                        if has_fm:
                            down(i - 1, FU - LAG + u)

                def h_part(i):
                    first = isinstance(i, int) and i == 0
                    for u in range(LAG, HU):
                        if first and u in (3, 8, 11):
                            pe.wait_ge(s["w_lo"], {3: 2, 8: 3, 11: 4}[u])
                        up(i, u, u // NH, u % NH, nT)
                        down(i, u - LAG)
                        if u == 9 and not first:
                            T_n2T(i - 1)
                        if u == 13:
                            pe.wait_ge(s["k_f32"], 2 * i + 2)
                            if not first:
                                pe.wait_ge(s["n2T_lo"], 2 * i)
                            for h in range(2):
                                for t in (2 * h, 2 * h + 1):
                                    for k in range(KD):
                                        lt = t_.transpose(tok2(M[h])[:, t % 2, k * P:(k + 1) * P],
                                                          KT32[:, k, t * P:(t + 1) * P], ident[:, :])
                                lt.then_inc(s["ktok_ps"], 1)

                def attention(i, last):
                    pe.wait_ge(s["ktok_lo"], 2 * i + 2)
                    pe.wait_ge(s["ntok_lo"], i + 1)
                    for c in range(CHUNKS):
                        for fh in range(KD):
                            for t in (2 * c, 2 * c + 1):
                                lt = mm3(M[c][:, fh * D:(fh + 1) * D], Ktok, ntok,
                                         (slice(None), t, slice(fh * P, (fh + 1) * P)), (slice(None), t, slice(None)),
                                         start=(fh == 0 and t == 2 * c), stop=(t == 2 * c + 1))
                        lt.then_inc(s["delta_ready"], 1)
                    pe.wait_ge(s["k_lo"], 2 * i + 2)
                    for k in range(KD):
                        pe.wait_ge(s["q_lo"], 2 * i + k + 1)
                        for c in range(CHUNKS):
                            for n, (key, zn, c0) in enumerate(((2 * c, 2, 0), (2 * c + 1, 1, 2 * P))):
                                lt = mm3(A[c][:, c0:c0 + zn * P], KT, QT,
                                         (slice(None), k, slice(key * P, key * P + P)),
                                         (slice(None), k, slice(key * P, (key + zn) * P)),
                                         start=(n == 0 and k == 0), stop=(k == KD - 1))
                            if k == KD - 1:
                                lt.then_inc(s["s_ps"], 1)
                    for c in range(CHUNKS):
                        pe.wait_ge(s["state_lo"], 2 * i + c + 1)
                        pe.wait_ge(s["state_add"], 2 * i + c + 1)
                        for zz in range(2):
                            for k in range(KD):
                                lt = mm3(tok2(M[c])[:, zz, :], QT, St[c],
                                         (slice(None), k, slice((2 * c + zz) * P, (2 * c + zz + 1) * P)),
                                         (slice(None), slice(k * D, (k + 1) * D)), start=(zz == 0 and k == 0))
                        lt.then_inc(s["qs_done"], 1)
                    for c in range(CHUNKS):
                        pe.wait_ge(s["s_lo"], 2 * i + c + 1)
                        for zz, at_, key in ((0, 0, 0), (1, P, 0), (1, 2 * P, 1)):
                            lt = mm3(tok2(M[c])[:, zz, :], SP_, ntok, (slice(None), c, slice(at_, at_ + P)),
                                     (slice(None), 2 * c + key, slice(None)), stop=(zz == key))
                        lt.then_inc(s["t_ready"], 1)
                    if not last:
                        T_nT(i + 1)

                def fm_units(i, lo_, hi_):
                    if lo_ == 0:
                        pe.wait_ge(s["n2T_lo"], 2 * i)
                    for v_ in range(lo_, hi_):
                        up(i, HU + v_, 2, v_, n2T)
                        down(i, HU + v_ - LAG)

                def T_X(b, k):
                    if k == 0:
                        pe.wait_ge(m["x2_normed"], TILES * (b + 1))
                        if is_first(b):
                            pe.wait_ge(s["s_masked"], 4 * NBLK)
                        elif not (isinstance(b, int) and b == 1):
                            pe.wait_ge(m["cfT_out"], b)
                    elif not is_first(b):
                        pe.wait_ge(m["XT_lo"], 2 * b + 1)
                    for t in range(TILES):
                        last = nc.tensor.transpose(routing_bank(b, k)[:, t * P:(t + 1) * P], xn[:, t, k * P:(k + 1) * P],
                                                   ident[:, :])
                    last.then_inc(m["XT_ps"], 1)

                def logits(b, q):
                    pe.wait_ge(m["XT_lo"], 2 * (b + 1))
                    E2 = 2 * EXPERTS
                    for t in range(TILES):
                        for k in range(KD):
                            for part in (1, 0):
                                last = mm(routing_bank(b, 0)[:, t * E2:(t + 1) * E2], XT[q][part][:, k, t * P:(t + 1) * P],
                                          rw[:, k, :], start=(t == 0 and k == 0 and part == 1),
                                          stop=(k == KD - 1 and part == 0))
                    last.then_inc(m["logits_ps"], 1)

                def T_cf(b):
                    pe.wait_ge(m["cf_placed"], b + 1)
                    for t in range(TILES):
                        last = nc.tensor.transpose(routing_bank(b, 1)[:, t * P:(t + 1) * P], cfx[:, t, :], ident[:, :])
                    last.then_inc(m["cfT_ps"], 1)

                def expert_up(b, q, u):
                    U = UNITS * b + u
                    if not (is_first(b) and u < 3):
                        pe.wait_ge(m["hidden_hi"], U - 2)
                    elif u < 2:
                        pe.wait_ge(s["gelu_done"], unit_base(NBLK) + NH - 1 + u)
                    for k in range(KD):
                        last = mm3(up3[u % 3][:, :], eW1, XT[q], (slice(None), k, u, slice(None)),
                                   (slice(None), k, slice(None)), start=(k == 0), stop=(k == KD - 1))
                    last.then_inc(m["up_ps"], 1)

                def spread(b, q, u):
                    if u == 0:
                        pe.wait_ge(m["cfT_out"], b + 1)
                    if not (is_first(b) and u < 2):
                        pe.wait_ge(m["scaled"], EXPERTS * b + u - 1)
                    elif u == 1:
                        pe.wait_ge(s["x2_ready"], 2 * NBLK + 1)
                    mm(CB[u % 2][:, :], sel[:, u, :], cfT[q][:, :], start=True, stop=True).then_inc(m["spread_ps"], 1)

                def expert_down(b, u):
                    pe.wait_ge(m["hidden_lo"], UNITS * b + u + 1)
                    for t in range(TILES):
                        if u == 0 and t % 2 == 0 and not is_first(b):
                            pe.wait_ge(m["y_formed"], 2 * b - 1 + t // 2)
                        elif u == 0 and t == 0:
                            pe.wait_ge(m["weights_lo"], 4)
                            pe.wait_ge(s["x2_ready"], 2 * NBLK + 2)
                        last = mm3(tok2(Y[t // 2])[:, t % 2, :], H, eW2, (slice(None), u % 3, slice(t * P, t * P + P)),
                                   (slice(None), u, slice(None)), start=(u == 0 and t % 2 == 0))
                    last.then_inc(m["down_done"], 1)

                def biases(b, q):
                    rows = slice(0, 2 * BIAS_LO)
                    for t in range(TILES):
                        last = mm(tok2(Y[t // 2])[:, t % 2, :], cfT[q][rows, t * P:(t + 1) * P], biasR[rows, :],
                                  stop=True)
                        if t % 2 == 1:
                            last.then_inc(m["sum_ps"], 1)

                pe.wait_ge(s["const_pool"], 3)
                pe.wait_ge(s["rows_loaded"], 16 * 9)
                t_.transpose(B[0][:, 0:NROWS], brows[0:NROWS, :], ident[0:NROWS, 0:NROWS]).then_inc(s["cols_ps"], 1)
                T_nT(0)
                pe.wait_ge(s["w_lo"], 1)
                next_units(0, False)
                h_part(0)
                for u in range(HU - LAG, HU):
                    down(0, u)
                attention(0, False)
                pe.wait_ge(s["w_lo"], 6)
                next_units(1, False)
                with pe.Fori(1, NBLK - 1) as i:
                    h_part(i)
                    fm_units(i, 0, LAG)
                    attention(i, False)
                    fm_units(i, LAG, NH)
                    next_units(i + 1, True)
                last = NBLK - 1
                h_part(last)
                fm_units(last, 0, LAG)
                attention(last, True)
                fm_units(last, LAG, NH)
                for u in range(FU - LAG, FU):
                    down(last, u)
                T_n2T(last)
                pe.wait_ge(s["n2T_lo"], 2 * NBLK)
                for v_ in range(NH + LAG):
                    if v_ < NH:
                        up(NBLK, v_, 2, v_, n2T)
                    else:
                        if v_ == NH:
                            pe.wait_ge(m["weights_lo"], 2)
                        expert_up(0, 0, v_ - NH)
                    if v_ == LAG:
                        pe.wait_ge(m["weights_lo"], 1)
                        logits(0, 0)
                    if v_ >= LAG:
                        if v_ == LAG:
                            pe.wait_ge(s["x2_ready"], 2 * NBLK)
                        down_rows(NBLK, v_ - LAG, v_ - LAG, 1).then_inc(s["down_done"], 1)
                    if v_ == 1:
                        T_X(0, 0)
                        T_X(0, 1)
                    if v_ == NH + 1:
                        T_cf(0)
                        T_X(1, 0)
                spread(0, 0, 0)

                def turn(b, q, ahead):
                    first = is_first(b)
                    late = int(first)
                    for u in range(UNITS):
                        lead_in = first and u < LAG
                        if not lead_in:
                            expert_up(b, q, u)
                        if u == 0 and not first:
                            expert_down(b - 1, LAST)
                            spread(b, q, 0)
                        elif u > 0:
                            if u < EXPERTS:
                                spread(b, q, u)
                            if u >= LAG:
                                expert_down(b, u - LAG)
                            elif not first:
                                expert_down(b - 1, LAST + u)
                                if u == LAG - 1:
                                    biases(b - 1, 1 - q)
                        if ahead >= 1:
                            if u in ((1,) if first else (0, 1)):
                                T_X(b + 1, u)
                            if u - late == 2:
                                logits(b + 1, 1 - q)
                            if u == UNITS - 1:
                                T_cf(b + 1)

                pairs(pe, turn)
                for u in range(LAST, UNITS):
                    expert_down(NBLK - 1, u)
                biases(NBLK - 1, 1)


_INS = ["L0_attn_x", "L0_attn_ln_g", "L0_attn_ln_b", "L0_attn_h1_w1", "L0_attn_h1_b1", "L0_attn_h1_w2",
        "L0_attn_h1_b2", "L0_attn_h2_w1", "L0_attn_h2_b1", "L0_attn_h2_w2", "L0_attn_h2_b2", "L0_attn_fm_w1",
        "L0_attn_fm_b1", "L0_attn_fm_w2", "L0_attn_fm_b2", "L0_ffn_routing_W", "L0_ffn_expert_bias",
        "L0_ffn_sW1", "L0_ffn_sb1", "L0_ffn_sW2", "L0_ffn_sb2", "L0_ffn_rW1", "L0_ffn_rb1", "L0_ffn_rW2",
        "L0_ffn_rb2"]
_OUTS = [((4, 2048, 256), "float32")]


def kernel(**inputs):
    import numpy as _np
    import concourse.bacc as _bacc
    from concourse import mybir as _mybir
    from concourse.bass_utils import run_bass_kernel_spmd as _run

    nc = _bacc.Bacc("TRN2", target_bir_lowering=False, num_devices=1)
    arrays, args = {}, []
    for name in _INS:
        a = _np.ascontiguousarray(inputs[name])
        arrays[f"in_{name}_dram"] = a
        args.append(nc.dram_tensor(f"in_{name}_dram", a.shape, _mybir.dt.from_np(a.dtype), kind="ExternalInput").ap())
    for i, (shape, dtype) in enumerate(_OUTS):
        dt = _mybir.dt.from_np(_np.dtype(dtype))
        args.append(nc.dram_tensor(f"out_{i}_dram", shape, dt, kind="ExternalOutput").ap())
    bass_preln_layer(nc, *args)
    r = _run(nc, [arrays], core_ids=[0])
    return r.results[0]["out_0_dram"]
```
